# Optimizing a Trainium2 kernel written in Bass

```python
import numpy as np
import jax
import jax.numpy as jnp

def _softmax(x, axis=-1):
    return jax.nn.softmax(x, axis=axis)

def _gelu(x):
    return jax.nn.gelu(x, approximate=True)

def _silu(x):
    return jax.nn.silu(x)

def _sigmoid(x):
    return jax.nn.sigmoid(x)

def _layernorm(x, axis=-1, eps=1e-05):
    m = jnp.mean(x, axis=axis, keepdims=True)
    v = jnp.var(x, axis=axis, keepdims=True)
    return (x - m) / jnp.sqrt(v + eps)

def _scatter_add(tgt, idx, src, axis=0):
    return tgt.at[idx].add(src)

def _segment_sum(src, seg, n):
    return jax.ops.segment_sum(src, seg, n)
kernel_name = 'mk_xattn_ffn_d4_seqx_r8_4f9507'

def setup_inputs(seed: int=0):
    np.random.seed(seed)
    _w = jnp.asarray

    def _rec_inputs():
        import jax
        import jax.numpy as jnp
        _rk = jax.random.key(seed)
        x = -0.0002928 + 1 * jax.random.normal(jax.random.fold_in(_rk, 1), (8, 256, 128), jnp.float32)
        _lenS = 256 - jax.random.randint(jax.random.fold_in(_rk, 7), (8,), 0, max(1, 256 // 4) + 1, jnp.int32)
        _lenS2 = 256 - jax.random.randint(jax.random.fold_in(_rk, 8), (8,), 0, max(1, 256 // 4) + 1, jnp.int32)
        _ctx_1024P = jax.random.normal(jax.random.fold_in(_rk, 11), (8, 16, 128), jnp.float32)
        _ctx_1024c = jax.random.dirichlet(jax.random.fold_in(_rk, 511), 0.3 * jnp.ones((16,), jnp.float32), (8, 256))
        _ctx_1024t = jnp.einsum('bsk,bkd->bsd', _ctx_1024c, _ctx_1024P)
        _ctx_1024t = _ctx_1024t * jax.lax.rsqrt(jnp.mean(jnp.square(_ctx_1024t)) + 1e-12) * 0.953939
        ctx_1024 = -1.39393e-06 + 0.999914 * (_ctx_1024t + 0.3 * jax.random.normal(jax.random.fold_in(_rk, 611), (8, 256, 128), jnp.float32))
        _validS = jnp.arange(256)[None, :] < _lenS[:, None]
        _validS2 = jnp.arange(256)[None, :] < _lenS2[:, None]
        _causal = jnp.tril(jnp.ones((256, 256), dtype=bool))
        mask_BxSxS2_if1 = jnp.where(jnp.ones((8, 256, 256), dtype=bool), 1, 0).astype(jnp.int32)
        mask_BxS2_if1 = jnp.where(jnp.ones((8, 256), dtype=bool), 1, 0).astype(jnp.int32)
        mask_BxS2_ik0 = jnp.where(jnp.broadcast_to(_validS2[:, :], (8, 256)), 0, 1).astype(jnp.int32)
        return (x, ctx_1024, mask_BxSxS2_if1, mask_BxS2_if1, mask_BxS2_ik0)
    x, ctx_1024, mask_BxSxS2_if1, mask_BxS2_if1, mask_BxS2_ik0 = _rec_inputs()

    def _L0_xattn_setup():
        import jax, jax.numpy as jnp
        import numpy as np
        H = 16
        key = jax.random.key(seed)
        ks = jax.random.split(key, 8)
        B, S, C = (2, 256, 128)
        sd = 1.0 / np.sqrt(C)
        return {'x': jax.random.normal(ks[0], (B, S, C), dtype=jnp.float32), 'context': jax.random.normal(ks[1], (B, S, C), dtype=jnp.float32), 'Wq': jax.random.normal(ks[2], (C, C), dtype=jnp.float32) * sd, 'Wk': jax.random.normal(ks[3], (C, C), dtype=jnp.float32) * sd, 'Wv': jax.random.normal(ks[4], (C, C), dtype=jnp.float32) * sd, 'Wo': jax.random.normal(ks[5], (C, C), dtype=jnp.float32) * sd, 'bo': jax.random.normal(ks[6], (C,), dtype=jnp.float32) * 0.01}
    _L0_xattn_all = _L0_xattn_setup()
    _L0_xattn_in = {k: v for k, v in _L0_xattn_all.items() if k in ('Wq', 'Wk', 'Wv', 'Wo', 'bo')}
    del _L0_xattn_all

    def _L0_ffn_setup():
        import jax, jax.numpy as jnp
        import numpy as np
        DIM = 128
        INTER = 128
        E = 32
        K = 4
        G = 8
        LG = 4
        ROUTE_SCALE = 1.0
        CAP_FACTOR = 1.25
        B, S = (4, 256)

        def _gate(xf, wg):
            logits = xf @ wg.T
            scores = jax.nn.softmax(logits, axis=-1)
            sg = scores.reshape(-1, G, E // G)
            group_scores = sg.max(axis=-1)
            _, gtop = jax.lax.top_k(group_scores, LG)
            keep_g = jnp.sum(jax.nn.one_hot(gtop, G, dtype=jnp.float32), axis=1) > 0
            masked = jnp.where(keep_g[:, :, None], sg, -jnp.inf).reshape(-1, E)
            _, idx = jax.lax.top_k(masked, K)
            w = jnp.take_along_axis(scores, idx, axis=1)
            w = w / (w.sum(-1, keepdims=True) + 1e-09) * ROUTE_SCALE
            return (w.astype(xf.dtype), idx)

        def _forward(x, wg, w1, w2, w3, sw1, sw2, sw3):
            shape = x.shape
            xf = x.reshape(-1, DIM)
            N = xf.shape[0]
            cap = max(1, int(CAP_FACTOR * N * K / E))
            w, idx = _gate(xf, wg)
            fe = idx.reshape(-1)
            oh = jax.nn.one_hot(fe, E, dtype=jnp.int32)
            pos = (jnp.cumsum(oh, axis=0) * oh).sum(-1) - 1
            keep = pos < cap
            dest = jnp.where(keep, fe * cap + pos, E * cap)
            tok = jnp.arange(N * K, dtype=jnp.int32) // K
            buf_tok = jnp.full((E * cap + 1,), N, jnp.int32).at[dest].set(tok)[:-1]
            buf_w = jnp.zeros((E * cap + 1,), x.dtype).at[dest].set(w.reshape(-1))[:-1]
            xp = jnp.concatenate([xf, jnp.zeros((1, DIM), x.dtype)], axis=0)
            xe = xp[buf_tok].reshape(E, cap, DIM)
            h = jax.nn.silu(jnp.einsum('ecd,edh->ech', xe, w1)) * jnp.einsum('ecd,edh->ech', xe, w3)
            out = jnp.einsum('ech,ehd->ecd', h, w2) * buf_w.reshape(E, cap, 1)
            y = jnp.zeros((N + 1, DIM), x.dtype).at[buf_tok].add(out.reshape(E * cap, DIM))[:N]
            z = jax.nn.silu(xf @ sw1) * (xf @ sw3) @ sw2
            return (y + z).reshape(shape)
        key = jax.random.key(seed)
        ks = jax.random.split(key, 9)
        sd = DIM ** (-0.5)
        si = INTER ** (-0.5)
        x = jax.random.normal(ks[0], (B, S, DIM), jnp.float32)
        wg = jax.random.normal(ks[1], (E, DIM), jnp.float32) * sd
        w1 = jax.random.normal(ks[2], (E, DIM, INTER), jnp.float32) * sd
        w3 = jax.random.normal(ks[3], (E, DIM, INTER), jnp.float32) * sd
        w2 = jax.random.normal(ks[4], (E, INTER, DIM), jnp.float32) * si
        sw1 = jax.random.normal(ks[5], (DIM, INTER), jnp.float32) * sd
        sw3 = jax.random.normal(ks[6], (DIM, INTER), jnp.float32) * sd
        sw2 = jax.random.normal(ks[7], (INTER, DIM), jnp.float32) * si
        return dict(x=x, wg=wg, w1=w1, w2=w2, w3=w3, sw1=sw1, sw2=sw2, sw3=sw3)
    _L0_ffn_all = _L0_ffn_setup()
    _L0_ffn_in = {k: v for k, v in _L0_ffn_all.items() if k in ('wg', 'w1', 'w2', 'w3', 'sw1', 'sw2', 'sw3')}
    del _L0_ffn_all

    def _L1_xattn_setup():
        import jax, jax.numpy as jnp
        import numpy as np
        import math
        D_MODEL = 128
        N_HEAD = 16
        D_K = D_MODEL // N_HEAD
        key = jax.random.key(seed)
        ks = jax.random.split(key, 12)
        B, S = (2, 256)
        scale = 1.0 / math.sqrt(D_MODEL)
        inp = {'q': jax.random.normal(ks[0], (B, S, D_MODEL), dtype=jnp.float32), 'k': jax.random.normal(ks[1], (B, S, D_MODEL), dtype=jnp.float32), 'v': jax.random.normal(ks[2], (B, S, D_MODEL), dtype=jnp.float32), 'mask': jnp.ones((B, S, S), dtype=jnp.int32), 'Wq': jax.random.normal(ks[3], (D_MODEL, D_MODEL), dtype=jnp.float32) * scale, 'bq': jnp.zeros((D_MODEL,), dtype=jnp.float32), 'Wk': jax.random.normal(ks[4], (D_MODEL, D_MODEL), dtype=jnp.float32) * scale, 'bk': jnp.zeros((D_MODEL,), dtype=jnp.float32), 'Wv': jax.random.normal(ks[5], (D_MODEL, D_MODEL), dtype=jnp.float32) * scale, 'bv': jnp.zeros((D_MODEL,), dtype=jnp.float32), 'Wo': jax.random.normal(ks[6], (D_MODEL, D_MODEL), dtype=jnp.float32) * scale, 'bo': jnp.zeros((D_MODEL,), dtype=jnp.float32)}
        return inp
    _L1_xattn_all = _L1_xattn_setup()
    _L1_xattn_in = {k: v for k, v in _L1_xattn_all.items() if k in ('Wq', 'bq', 'Wk', 'bk', 'Wv', 'bv', 'Wo', 'bo')}
    del _L1_xattn_all

    def _L1_ffn_setup():
        import jax, jax.numpy as jnp
        import numpy as np
        EPS = 1e-06
        N_EXPERTS = 8

        def _rms_norm(x, scale, eps=EPS):
            mean_sq = jnp.mean(x.astype(jnp.float32) ** 2, axis=-1, keepdims=True)
            s = scale.astype(jnp.float32) * jax.lax.rsqrt(mean_sq + eps)
            return x * s.astype(x.dtype)

        def _dist2(x, y):
            nx = jnp.sum(x ** 2, axis=-1)[..., :, None]
            ny = jnp.sum(y ** 2, axis=-1)[..., None, :]
            return nx + ny - 2.0 * (x @ y.T)
        key = jax.random.key(seed)
        ks = jax.random.split(key, 5)
        dim, hidden, E = (128, 256, N_EXPERTS)
        x = jax.random.normal(ks[0], (4, 256, dim), dtype=jnp.float32)
        scale = jnp.ones((dim,), dtype=jnp.float32)
        centroids = jax.random.normal(ks[1], (E, dim), dtype=jnp.float32)
        up_w = jax.random.normal(ks[2], (E, dim, hidden * 2), dtype=jnp.float32) * dim ** (-0.5)
        down_w = jax.random.normal(ks[3], (E, hidden, dim), dtype=jnp.float32) * hidden ** (-0.5)
        return {'x': x, 'scale': scale, 'centroids': centroids, 'up_w': up_w, 'down_w': down_w}
    _L1_ffn_all = _L1_ffn_setup()
    _L1_ffn_in = {k: v for k, v in _L1_ffn_all.items() if k in ('scale', 'centroids', 'up_w', 'down_w')}
    del _L1_ffn_all

    def _L2_xattn_setup():
        import jax, jax.numpy as jnp
        import numpy as np
        D_MODEL = 128
        N_HEADS = 16
        HEAD_DIM = D_MODEL // N_HEADS
        ROPE_BASE = 10000.0

        def apply_rope(x):
            b, s, h, d = x.shape
            h_half = d // 2
            theta = 1.0 / ROPE_BASE ** (jnp.arange(0, d, 2, dtype=jnp.float32) / d)
            idx_theta = jnp.arange(s, dtype=jnp.float32)[:, None] * theta[None, :]
            cos = jnp.cos(idx_theta)[None, :, None, :]
            sin = jnp.sin(idx_theta)[None, :, None, :]
            xs = x.reshape(b, s, h, h_half, 2)
            x0, x1 = (xs[..., 0], xs[..., 1])
            out = jnp.stack((x0 * cos - x1 * sin, x1 * cos + x0 * sin), axis=-1)
            return out.reshape(b, s, h, d)
        key = jax.random.key(seed)
        ks = jax.random.split(key, 8)
        B, S, D = (2, 256, D_MODEL)
        scale = 0.02
        return {'Q': jax.random.normal(ks[0], (B, S, D), dtype=jnp.float32), 'K': jax.random.normal(ks[1], (B, S, D), dtype=jnp.float32), 'V': jax.random.normal(ks[2], (B, S, D), dtype=jnp.float32), 'attention_mask': jnp.ones((B, S), dtype=jnp.int32), 'Wq': jax.random.normal(ks[3], (D, D), dtype=jnp.float32) * scale, 'Wk': jax.random.normal(ks[4], (D, D), dtype=jnp.float32) * scale, 'Wv': jax.random.normal(ks[5], (D, D), dtype=jnp.float32) * scale, 'Wo': jax.random.normal(ks[6], (D, D), dtype=jnp.float32) * scale, 'bo': jax.random.normal(ks[7], (D,), dtype=jnp.float32) * scale}
    _L2_xattn_all = _L2_xattn_setup()
    _L2_xattn_in = {k: v for k, v in _L2_xattn_all.items() if k in ('Wq', 'Wk', 'Wv', 'Wo', 'bo')}
    del _L2_xattn_all

    def _L2_ffn_setup():
        import jax, jax.numpy as jnp
        import numpy as np
        LN_EPS = 0.001
        EPS = 1e-05
        QB = 128.0

        def ste_round(x):
            return x + jax.lax.stop_gradient(jnp.round(x) - x)
        key = jax.random.key(seed)
        k1, k2 = jax.random.split(key)
        x = jax.random.normal(k1, (4, 1024, 128), dtype=jnp.float32)
        weight = jax.random.normal(k2, (128, 128), dtype=jnp.float32) * 0.02
        ln_gamma = jnp.ones((128,), dtype=jnp.float32)
        ln_beta = jnp.zeros((128,), dtype=jnp.float32)
        return {'x': x, 'weight': weight, 'ln_gamma': ln_gamma, 'ln_beta': ln_beta}
    _L2_ffn_all = _L2_ffn_setup()
    _L2_ffn_in = {k: v for k, v in _L2_ffn_all.items() if k in ('weight', 'ln_gamma', 'ln_beta')}
    del _L2_ffn_all

    def _L3_xattn_setup():
        import jax, jax.numpy as jnp
        import numpy as np
        B, S, SE, D, H = (2, 256, 256, 128, 16)
        DH = D // H
        key = jax.random.key(seed)
        ks = jax.random.split(key, 6)
        scale = 0.02
        return {'hidden_states': jax.random.normal(ks[0], (B, S, D), dtype=jnp.float32), 'encoder_hidden_states': jax.random.normal(ks[1], (B, SE, D), dtype=jnp.float32), 'encoder_attention_mask': jax.random.randint(ks[2], (B, SE), 0, 2, dtype=jnp.int32), 'Wq': jax.random.normal(ks[3], (D, D), dtype=jnp.float32) * scale, 'Wkv': jax.random.normal(ks[4], (2 * D, D), dtype=jnp.float32) * scale, 'Wo': jax.random.normal(ks[5], (D, D), dtype=jnp.float32) * scale}
    _L3_xattn_all = _L3_xattn_setup()
    _L3_xattn_in = {k: v for k, v in _L3_xattn_all.items() if k in ('Wq', 'Wkv', 'Wo')}
    del _L3_xattn_all

    def _L3_ffn_setup():
        import jax, jax.numpy as jnp
        import numpy as np
        B, L, D = (4, 64, 128)
        E, TOP_K = (16, 4)
        F = 4 * D
        key = jax.random.key(seed)
        ks = jax.random.split(key, 6)
        scale = 0.02
        return {'x': jax.random.normal(ks[0], (B, L, D), jnp.float32), 'keys': jax.random.normal(ks[1], (E, D), jnp.float32), 'w1': jax.random.normal(ks[2], (E, F, D), jnp.float32) * scale, 'b1': jnp.zeros((E, F), jnp.float32), 'w2': jax.random.normal(ks[3], (E, D, F), jnp.float32) * scale, 'b2': jnp.zeros((E, D), jnp.float32), 'rw': jax.random.normal(ks[4], (E, D), jnp.float32) * scale, 'rb': jnp.zeros((E,), jnp.float32)}
    _L3_ffn_all = _L3_ffn_setup()
    _L3_ffn_in = {k: v for k, v in _L3_ffn_all.items() if k in ('keys', 'w1', 'b1', 'w2', 'b2', 'rw', 'rb')}
    del _L3_ffn_all
    return {'x': x, 'ctx_1024': ctx_1024, 'mask_BxSxS2_if1': mask_BxSxS2_if1, 'mask_BxS2_if1': mask_BxS2_if1, 'mask_BxS2_ik0': mask_BxS2_ik0, 'L0_xattn_Wq': _L0_xattn_in['Wq'], 'L0_xattn_Wk': _L0_xattn_in['Wk'], 'L0_xattn_Wv': _L0_xattn_in['Wv'], 'L0_xattn_Wo': _L0_xattn_in['Wo'], 'L0_xattn_bo': _L0_xattn_in['bo'], 'L0_ffn_wg': _L0_ffn_in['wg'], 'L0_ffn_w1': _L0_ffn_in['w1'], 'L0_ffn_w2': _L0_ffn_in['w2'], 'L0_ffn_w3': _L0_ffn_in['w3'], 'L0_ffn_sw1': _L0_ffn_in['sw1'], 'L0_ffn_sw2': _L0_ffn_in['sw2'], 'L0_ffn_sw3': _L0_ffn_in['sw3'], 'L1_xattn_Wq': _L1_xattn_in['Wq'], 'L1_xattn_bq': _L1_xattn_in['bq'], 'L1_xattn_Wk': _L1_xattn_in['Wk'], 'L1_xattn_bk': _L1_xattn_in['bk'], 'L1_xattn_Wv': _L1_xattn_in['Wv'], 'L1_xattn_bv': _L1_xattn_in['bv'], 'L1_xattn_Wo': _L1_xattn_in['Wo'], 'L1_xattn_bo': _L1_xattn_in['bo'], 'L1_ffn_scale': _L1_ffn_in['scale'], 'L1_ffn_centroids': _L1_ffn_in['centroids'], 'L1_ffn_up_w': _L1_ffn_in['up_w'], 'L1_ffn_down_w': _L1_ffn_in['down_w'], 'L2_xattn_Wq': _L2_xattn_in['Wq'], 'L2_xattn_Wk': _L2_xattn_in['Wk'], 'L2_xattn_Wv': _L2_xattn_in['Wv'], 'L2_xattn_Wo': _L2_xattn_in['Wo'], 'L2_xattn_bo': _L2_xattn_in['bo'], 'L2_ffn_weight': _L2_ffn_in['weight'], 'L2_ffn_ln_gamma': _L2_ffn_in['ln_gamma'], 'L2_ffn_ln_beta': _L2_ffn_in['ln_beta'], 'L3_xattn_Wq': _L3_xattn_in['Wq'], 'L3_xattn_Wkv': _L3_xattn_in['Wkv'], 'L3_xattn_Wo': _L3_xattn_in['Wo'], 'L3_ffn_keys': _L3_ffn_in['keys'], 'L3_ffn_w1': _L3_ffn_in['w1'], 'L3_ffn_b1': _L3_ffn_in['b1'], 'L3_ffn_w2': _L3_ffn_in['w2'], 'L3_ffn_b2': _L3_ffn_in['b2'], 'L3_ffn_rw': _L3_ffn_in['rw'], 'L3_ffn_rb': _L3_ffn_in['rb']}

def reference(x, ctx_1024, mask_BxSxS2_if1, mask_BxS2_if1, mask_BxS2_ik0, L0_xattn_Wq, L0_xattn_Wk, L0_xattn_Wv, L0_xattn_Wo, L0_xattn_bo, L0_ffn_wg, L0_ffn_w1, L0_ffn_w2, L0_ffn_w3, L0_ffn_sw1, L0_ffn_sw2, L0_ffn_sw3, L1_xattn_Wq, L1_xattn_bq, L1_xattn_Wk, L1_xattn_bk, L1_xattn_Wv, L1_xattn_bv, L1_xattn_Wo, L1_xattn_bo, L1_ffn_scale, L1_ffn_centroids, L1_ffn_up_w, L1_ffn_down_w, L2_xattn_Wq, L2_xattn_Wk, L2_xattn_Wv, L2_xattn_Wo, L2_xattn_bo, L2_ffn_weight, L2_ffn_ln_gamma, L2_ffn_ln_beta, L3_xattn_Wq, L3_xattn_Wkv, L3_xattn_Wo, L3_ffn_keys, L3_ffn_w1, L3_ffn_b1, L3_ffn_w2, L3_ffn_b2, L3_ffn_rw, L3_ffn_rb):
    import jax
    import jax.numpy as jnp

    def _L0_xattn_ref(x, context, Wq, Wk, Wv, Wo, bo):
        import jax, jax.numpy as jnp
        import numpy as np
        H = 16
        b, s, c = x.shape
        hd = c // H
        scale = hd ** (-0.5)
        q = (x @ Wq.T).reshape(b, s, H, hd).transpose(0, 2, 1, 3)
        k = (context @ Wk.T).reshape(b, s, H, hd).transpose(0, 2, 1, 3)
        v = (context @ Wv.T).reshape(b, s, H, hd).transpose(0, 2, 1, 3)
        att = jax.nn.softmax(jnp.einsum('bhqd,bhkd->bhqk', q, k) * scale, axis=-1)
        o = jnp.einsum('bhqk,bhkd->bhqd', att, v)
        o = o.transpose(0, 2, 1, 3).reshape(b, s, c)
        return o @ Wo.T + bo

    def _L0_ffn_ref(x, wg, w1, w2, w3, sw1, sw2, sw3):
        import jax, jax.numpy as jnp
        import numpy as np
        DIM = 128
        INTER = 128
        E = 32
        K = 4
        G = 8
        LG = 4
        ROUTE_SCALE = 1.0
        CAP_FACTOR = 1.25
        B, S = (4, 256)

        def _gate(xf, wg):
            logits = xf @ wg.T
            scores = jax.nn.softmax(logits, axis=-1)
            sg = scores.reshape(-1, G, E // G)
            group_scores = sg.max(axis=-1)
            _, gtop = jax.lax.top_k(group_scores, LG)
            keep_g = jnp.sum(jax.nn.one_hot(gtop, G, dtype=jnp.float32), axis=1) > 0
            masked = jnp.where(keep_g[:, :, None], sg, -jnp.inf).reshape(-1, E)
            _, idx = jax.lax.top_k(masked, K)
            w = jnp.take_along_axis(scores, idx, axis=1)
            w = w / (w.sum(-1, keepdims=True) + 1e-09) * ROUTE_SCALE
            return (w.astype(xf.dtype), idx)

        def _forward(x, wg, w1, w2, w3, sw1, sw2, sw3):
            shape = x.shape
            xf = x.reshape(-1, DIM)
            N = xf.shape[0]
            cap = max(1, int(CAP_FACTOR * N * K / E))
            w, idx = _gate(xf, wg)
            fe = idx.reshape(-1)
            oh = jax.nn.one_hot(fe, E, dtype=jnp.int32)
            pos = (jnp.cumsum(oh, axis=0) * oh).sum(-1) - 1
            keep = pos < cap
            dest = jnp.where(keep, fe * cap + pos, E * cap)
            tok = jnp.arange(N * K, dtype=jnp.int32) // K
            buf_tok = jnp.full((E * cap + 1,), N, jnp.int32).at[dest].set(tok)[:-1]
            buf_w = jnp.zeros((E * cap + 1,), x.dtype).at[dest].set(w.reshape(-1))[:-1]
            xp = jnp.concatenate([xf, jnp.zeros((1, DIM), x.dtype)], axis=0)
            xe = xp[buf_tok].reshape(E, cap, DIM)
            h = jax.nn.silu(jnp.einsum('ecd,edh->ech', xe, w1)) * jnp.einsum('ecd,edh->ech', xe, w3)
            out = jnp.einsum('ech,ehd->ecd', h, w2) * buf_w.reshape(E, cap, 1)
            y = jnp.zeros((N + 1, DIM), x.dtype).at[buf_tok].add(out.reshape(E * cap, DIM))[:N]
            z = jax.nn.silu(xf @ sw1) * (xf @ sw3) @ sw2
            return (y + z).reshape(shape)
        return _forward(x, wg, w1, w2, w3, sw1, sw2, sw3)

    def _L1_xattn_ref(q, k, v, mask, Wq, bq, Wk, bk, Wv, bv, Wo, bo):
        import jax, jax.numpy as jnp
        import numpy as np
        import math
        D_MODEL = 128
        N_HEAD = 16
        D_K = D_MODEL // N_HEAD
        B, S, _ = q.shape

        def proj(x, W, b):
            y = x @ W.T + b
            return y.reshape(B, -1, N_HEAD, D_K).transpose(0, 2, 1, 3)
        qh = proj(q, Wq, bq)
        kh = proj(k, Wk, bk)
        vh = proj(v, Wv, bv)
        scores = jnp.einsum('bhqd,bhkd->bhqk', qh, kh) / math.sqrt(D_K)
        scores = jnp.where(mask[:, None, :, :] == 0, -1000000000.0, scores)
        attn = jax.nn.softmax(scores, axis=-1)
        out = jnp.einsum('bhqk,bhkd->bhqd', attn, vh)
        concat = out.transpose(0, 2, 1, 3).reshape(B, -1, D_MODEL)
        return concat @ Wo.T + bo

    def _L1_ffn_ref(x, scale, centroids, up_w, down_w):
        import jax, jax.numpy as jnp
        import numpy as np
        EPS = 1e-06
        N_EXPERTS = 8

        def _rms_norm(x, scale, eps=EPS):
            mean_sq = jnp.mean(x.astype(jnp.float32) ** 2, axis=-1, keepdims=True)
            s = scale.astype(jnp.float32) * jax.lax.rsqrt(mean_sq + eps)
            return x * s.astype(x.dtype)

        def _dist2(x, y):
            nx = jnp.sum(x ** 2, axis=-1)[..., :, None]
            ny = jnp.sum(y ** 2, axis=-1)[..., None, :]
            return nx + ny - 2.0 * (x @ y.T)
        skip = x
        xn = _rms_norm(x, scale)
        ids = jnp.argmin(_dist2(xn, centroids), axis=-1)
        out = jnp.zeros_like(x)
        for e in range(N_EXPERTS):
            h = jnp.einsum('bsd,dh->bsh', xn, up_w[e])
            a, g = jnp.split(h, 2, axis=-1)
            y = jnp.einsum('bsh,hd->bsd', a * jax.nn.silu(g), down_w[e])
            out = jnp.where((ids == e)[..., None], y, out)
        return out + skip

    def _L2_xattn_ref(Q, K, V, attention_mask, Wq, Wk, Wv, Wo, bo):
        import jax, jax.numpy as jnp
        import numpy as np
        D_MODEL = 128
        N_HEADS = 16
        HEAD_DIM = D_MODEL // N_HEADS
        ROPE_BASE = 10000.0

        def apply_rope(x):
            b, s, h, d = x.shape
            h_half = d // 2
            theta = 1.0 / ROPE_BASE ** (jnp.arange(0, d, 2, dtype=jnp.float32) / d)
            idx_theta = jnp.arange(s, dtype=jnp.float32)[:, None] * theta[None, :]
            cos = jnp.cos(idx_theta)[None, :, None, :]
            sin = jnp.sin(idx_theta)[None, :, None, :]
            xs = x.reshape(b, s, h, h_half, 2)
            x0, x1 = (xs[..., 0], xs[..., 1])
            out = jnp.stack((x0 * cos - x1 * sin, x1 * cos + x0 * sin), axis=-1)
            return out.reshape(b, s, h, d)
        b, s, d = Q.shape
        q = (Q @ Wq.T).reshape(b, s, N_HEADS, HEAD_DIM)
        k = (K @ Wk.T).reshape(b, s, N_HEADS, HEAD_DIM)
        v = (V @ Wv.T).reshape(b, s, N_HEADS, HEAD_DIM)
        q = apply_rope(q)
        k = apply_rope(k)
        scores = jnp.einsum('bnhd,bmhd->bhnm', q, k) / jnp.sqrt(jnp.float32(HEAD_DIM))
        pad = (attention_mask != 0)[:, None, None, :]
        scores = jnp.where(pad, scores, -jnp.inf)
        causal = jnp.tril(jnp.ones((s, s), dtype=bool))[None, None]
        scores = jnp.where(causal, scores, -jnp.inf)
        attn = jax.nn.softmax(scores, axis=-1)
        out = jnp.einsum('bhnm,bmhd->bnhd', attn, v).reshape(b, s, d)
        return out @ Wo.T + bo

    def _L2_ffn_ref(x, weight, ln_gamma, ln_beta):
        import jax, jax.numpy as jnp
        import numpy as np
        LN_EPS = 0.001
        EPS = 1e-05
        QB = 128.0

        def ste_round(x):
            return x + jax.lax.stop_gradient(jnp.round(x) - x)
        mu = jnp.mean(x, axis=-1, keepdims=True)
        var = jnp.var(x, axis=-1, keepdims=True)
        xn = (x - mu) * jax.lax.rsqrt(var + LN_EPS) * ln_gamma + ln_beta
        beta = jnp.mean(jnp.abs(weight))
        w_q = jnp.clip(ste_round(weight / (beta + EPS)), -1.0, 1.0)
        gamma = jnp.max(jnp.abs(xn))
        xq = jnp.clip(xn * QB / gamma, -QB + EPS, QB - EPS)
        y = jnp.einsum('bsd,du->bsu', xq, w_q)
        return y * (gamma * beta / QB)

    def _L3_xattn_ref(hidden_states, encoder_hidden_states, encoder_attention_mask, Wq, Wkv, Wo):
        import jax, jax.numpy as jnp
        import numpy as np
        B, S, SE, D, H = (2, 256, 256, 128, 16)
        DH = D // H
        b, s, _ = hidden_states.shape
        se = encoder_hidden_states.shape[1]
        att_scale = DH ** (-0.5)
        q = (hidden_states @ Wq.T).reshape(b, s, H, DH).transpose(0, 2, 1, 3)
        kv = (encoder_hidden_states @ Wkv.T).reshape(b, se, 2, H, DH).transpose(2, 0, 3, 1, 4)
        k, v = (kv[0], kv[1])
        scores = jnp.einsum('bhsd,bhed->bhse', q, k) * att_scale
        mask = encoder_attention_mask[:, None, None, :]
        scores = jnp.where(mask == 0, -jnp.inf, scores)
        attn = jax.nn.softmax(scores, axis=-1)
        out = jnp.einsum('bhse,bhed->bhsd', attn, v)
        out = out.transpose(0, 2, 1, 3).reshape(b, s, H * DH)
        return out @ Wo.T

    def _L3_ffn_ref(x, keys, w1, b1, w2, b2, rw, rb):
        import jax, jax.numpy as jnp
        import numpy as np
        B, L, D = (4, 64, 128)
        E, TOP_K = (16, 4)
        F = 4 * D
        diff = x[:, :, None, :] - keys
        dist2 = jnp.sum(diff * diff, axis=-1)
        logits = -dist2 + jnp.einsum('bld,ed->ble', x, rw) + rb
        topv, topi = jax.lax.top_k(logits, TOP_K)
        w = jax.nn.softmax(topv, axis=-1)
        hidden = jax.nn.gelu(jnp.einsum('bld,efd->blef', x, w1) + b1, approximate=False)
        exp_out = jnp.einsum('blef,edf->bled', hidden, w2) + b2
        sel = jnp.take_along_axis(exp_out, topi[..., None], axis=2)
        fused = jnp.sum(w[..., None] * sel, axis=2)
        return fused
    x = x + _L0_xattn_ref(_layernorm(x, axis=-1), ctx_1024, L0_xattn_Wq, L0_xattn_Wk, L0_xattn_Wv, L0_xattn_Wo, L0_xattn_bo)
    x = x + _L0_ffn_ref(_layernorm(x, axis=-1), L0_ffn_wg, L0_ffn_w1, L0_ffn_w2, L0_ffn_w3, L0_ffn_sw1, L0_ffn_sw2, L0_ffn_sw3)
    x = x + _L1_xattn_ref(_layernorm(x, axis=-1), ctx_1024, ctx_1024, mask_BxSxS2_if1, L1_xattn_Wq, L1_xattn_bq, L1_xattn_Wk, L1_xattn_bk, L1_xattn_Wv, L1_xattn_bv, L1_xattn_Wo, L1_xattn_bo)
    x = x + _L1_ffn_ref(_layernorm(x, axis=-1), L1_ffn_scale, L1_ffn_centroids, L1_ffn_up_w, L1_ffn_down_w)
    x = x + _L2_xattn_ref(_layernorm(x, axis=-1), ctx_1024, ctx_1024, mask_BxS2_if1, L2_xattn_Wq, L2_xattn_Wk, L2_xattn_Wv, L2_xattn_Wo, L2_xattn_bo)
    x = x + _L2_ffn_ref(_layernorm(x, axis=-1), L2_ffn_weight, L2_ffn_ln_gamma, L2_ffn_ln_beta)
    x = x + _L3_xattn_ref(_layernorm(x, axis=-1), ctx_1024, mask_BxS2_ik0, L3_xattn_Wq, L3_xattn_Wkv, L3_xattn_Wo)
    x = x + _L3_ffn_ref(_layernorm(x, axis=-1), L3_ffn_keys, L3_ffn_w1, L3_ffn_b1, L3_ffn_w2, L3_ffn_b2, L3_ffn_rw, L3_ffn_rb)
    return x

_drawn_inputs = setup_inputs


def setup_inputs(seed=0):
    import zlib

    import numpy as np

    out = dict(_drawn_inputs(seed))
    spreads = {'L1_xattn_bq': (0.0, 0.1),
     'L1_xattn_bk': (0.0, 2.0),
     'L1_xattn_bv': (0.0, 0.1),
     'L1_xattn_bo': (0.0, 0.1),
     'L1_ffn_scale': (1.0, 0.2),
     'L2_ffn_ln_gamma': (1.0, 0.6),
     'L2_ffn_ln_beta': (0.0, 0.8),
     'L3_ffn_b1': (0.0, 0.8),
     'L3_ffn_b2': (0.0, 0.279),
     'L3_ffn_rb': (0.0, 2.0)}
    factors = {'L2_xattn_Wq': 8.0,
     'L2_xattn_Wk': 8.0,
     'L2_xattn_Wv': 5.413,
     'L2_xattn_Wo': 5.589,
     'L2_xattn_bo': 6.863,
     'L3_xattn_Wq': 8.0,
     'L3_xattn_Wkv': 5.013,
     'L3_xattn_Wo': 4.951,
     'L3_ffn_w1': 2.858,
     'L3_ffn_rw': 8.0}
    for name, (base, spread) in spreads.items():
        noise = np.random.default_rng([zlib.crc32(name.encode()), seed]).standard_normal(out[name].shape)
        drawn = base * np.exp(spread * noise) if base else spread * noise
        out[name] = jnp.asarray(drawn.astype(out[name].dtype))
    for name, factor in factors.items():
        out[name] = (out[name] * factor).astype(out[name].dtype)
    return out
```

```python
from contextlib import ExitStack

import numpy as np

import concourse.bass as bass
from concourse import mybir

F32 = mybir.dt.float32
BF16 = mybir.dt.bfloat16
I32 = mybir.dt.int32
ALU = mybir.AluOpType
ACT = mybir.ActivationFunctionType
AXX = mybir.AxisListType.X
RMAX = bass.bass_isa.ReduceOp.max

B, S, D, H = 8, 256, 128, 16
HD = D // H
N = B * S
P = 128
TILES = N // P
CHUNK = 512
CHUNKS = N // CHUNK
PAIRS = H // 2
PARTS = 3
BLOCKS = 6
STACK = BLOCKS * HD
VW = 32
LN_EPS = 1e-5
NEG = -1e30
MASKED = -1e9
LAG = 4

Q_BLOCKS = [(0, 3, 0, 0), (3, 2, 1, 0), (5, 1, 2, 0)]
K_BLOCKS = [(0, 3, 0, 1), (3, 2, 0, 1), (5, 1, 0, 0)]


def at_least(eng, sem, n):
    if not isinstance(n, int) or n > 0:
        eng.wait_ge(sem, n)


def apart(eng, n, passed):
    if not isinstance(n, int):
        eng.sem_inc(passed, 1)


class Chain:

    def __init__(self, eng, sem, base=0, passed=None):
        self.eng, self.sem, self.base, self.n, self.passed = eng, sem, base, 0, passed

    def __call__(self, ins):
        ins.then_inc(self.sem, 1)
        self.n += 1
        self.eng.wait_ge(self.sem, self.base + self.n)
        apart(self.eng, self.base, self.passed)

    def rebase(self, base):
        self.base, self.n = base, 0


class Semaphores:

    def __init__(self, nc, ctx, tag):
        self.nc, self.ctx, self.tag, self.numbers = nc, ctx, tag, []

    def __call__(self, name):
        s = self.ctx.enter_context(self.nc.semaphore(f"{self.tag}_{name}"))
        self.numbers.append(s.num)
        return s

    def open_block(self):
        self.ctx.callback(self.clear)
        return self.ctx.enter_context(self.nc.Block())

    def clear(self):
        numbers, start = sorted(self.numbers), 0
        for n in range(1, len(numbers) + 1):
            if n == len(numbers) or numbers[n] != numbers[n - 1] + 1:
                self.nc.gpsimd.sem_clear(range(numbers[start], numbers[n - 1] + 1))
                start = n
        self.nc.all_engine_barrier()


class Chip:

    def __init__(self, nc, ctx, dram):
        self.nc, self.dram = nc, dram

        def sb(name, shape, dt=F32):
            return ctx.enter_context(nc.sbuf_tensor(name, shape, dt))

        self.x = sb("x", [P, TILES, D])
        self.xn = sb("xn", [P, TILES, D])
        self.xnT = sb("xnT", [P, N])
        self.ident = sb("ident", [P, P])
        self.identb = sb("identb", [P, P], BF16)
        self.ones = sb("ones", [P, P])
        self.zrow = sb("zrow", [1, CHUNK], BF16)
        self.rev = sb("rev", [P, 32])
        self.pick = sb("pick", [P, PAIRS, P], BF16)
        self.qs = sb("qs", [P, 2, PAIRS, S], BF16)
        self.ks = sb("ks", [P, 2, H, S], BF16)
        self.mT = sb("mT", [P, 2, S], BF16)
        self.vaug = sb("vaug", [P, 2, 2, H, VW])
        self.psum = [ctx.enter_context(nc.psum_tensor(f"bank{i}", [P, CHUNK], F32)) for i in range(8)]


def start_up(chip):
    nc, c = chip.nc, chip
    with ExitStack() as ctx:
        sem = Semaphores(nc, ctx, "start")
        loaded, filled, cleared = sem("x_loaded"), sem("filled"), sem("cleared")
        block = sem.open_block()

        @block.sync
        def _(sp):
            sp.dma_start(c.x[:, :, :], c.dram["x"].rearrange("(t p) d -> p t d", p=P)).then_inc(loaded, 16)
            sp.wait_ge(loaded, 16)

        @block.vector
        def _(dve):
            for t in (c.qs, c.ks):
                dve.memset(t[:, :, :, :], 0.0).then_inc(cleared, 1)
            dve.memset(c.mT[:, :, :], 0.0).then_inc(cleared, 1)
            dve.memset(c.vaug[:, :, :, :, :], 0.0).then_inc(cleared, 1)
            dve.wait_ge(cleared, 4)
            for r in (32, 96):
                dve.memset(c.qs[r:r + 32, :, :, :], 1.0)
            dve.memset(c.vaug[:, :, :, :, HD:HD + 1], 1.0).then_inc(cleared, 1)
            dve.wait_ge(cleared, 5)

        @block.gpsimd
        def _(pool):
            done = Chain(pool, filled)
            done(pool.memset(c.ones[:, :], 1.0))
            done(pool.memset(c.zrow[:, :], 0.0))
            done(pool.iota(c.rev[:, :], [[-1, 32]], base=32, channel_multiplier=0,
                           allow_small_or_imprecise_dtypes=True))
            for m in (c.ident, c.identb):
                done(pool.memset(m[:, :], 0.0))
                done(pool.affine_select(out=m[:, :], in_=m[:, :], compare_op=ALU.not_equal, fill=1.0,
                                        base=0, pattern=[[-1, P]], channel_multiplier=1))
            done(pool.memset(c.pick[:, :, :], 0.0))
            for part in range(PARTS):
                done(pool.affine_select(out=c.pick[:, :, :], in_=c.pick[:, :, :], compare_op=ALU.not_equal,
                                        fill=1.0, base=-8 * part, pattern=[[-1, PAIRS], [0, P]],
                                        channel_multiplier=1))


class Norm:

    def __init__(self, chip, ctx, tag, sem):
        nc, self.c = chip.nc, chip
        self.centred, self.squared, self.summed = sem("norm_centred"), sem("norm_squared"), sem("norm_summed")
        self.rooted, self.normed = sem("norm_rooted"), sem("norm_normed")
        self.turned, self.copied = sem("norm_turned"), sem("norm_copied")
        self.sq = ctx.enter_context(nc.sbuf_tensor(f"{tag}_sq", [P, TILES, D], F32))
        self.st = ctx.enter_context(nc.sbuf_tensor(f"{tag}_st", [P, 4, TILES], F32))
        self.eps = ctx.enter_context(nc.sbuf_tensor(f"{tag}_eps", [P, 2], F32))
        self.rounds = 0

    def each(self, n):
        return self.st[:, n, :].unsqueeze(2).to_broadcast([P, TILES, D])

    def vector(self, dve, chain, src, dst, eps, centre=True):
        self.rounds += 1
        r = self.rounds
        x, y, st = src[:, :, :], dst[:, :, :], self.st
        chain(dve.memset(self.eps[:, 0:1], eps))
        if centre:
            chain(dve.tensor_reduce(st[:, 0, :], x, AXX, ALU.add))
            chain(dve.tensor_scalar(st[:, 1, :], st[:, 0, :], 1.0 / D, None, ALU.mult))
            dve.tensor_tensor(y, x, self.each(1), ALU.subtract).then_inc(self.centred, 1)
        else:
            dve.memset(self.eps[:, 1:2], 0.0).then_inc(self.centred, 1)
        dve.wait_ge(self.squared, r)
        dve.tensor_reduce(st[:, 2, :], self.sq[:, :, :], AXX, ALU.add).then_inc(self.summed, 1)
        dve.wait_ge(self.rooted, r)
        chain(dve.reciprocal(st[:, 3, :], st[:, 2, :]))
        dve.tensor_tensor(y, y if centre else x, self.each(3), ALU.mult).then_inc(self.normed, 1)
        dve.wait_ge(self.normed, r)

    def scalar(self, act, src, r):
        act.wait_ge(self.centred, r)
        act.activation(self.sq[:, :, :], src[:, :, :], ACT.Square).then_inc(self.squared, 1)
        act.wait_ge(self.summed, r)
        act.activation(self.st[:, 2, :], self.st[:, 2, :], ACT.Sqrt, scale=1.0 / D,
                       bias=self.eps[:, 0:1]).then_inc(self.rooted, 1)

    def tensor(self, pe, src, banks):
        for g in range(CHUNKS):
            for t in range(4):
                i = pe.transpose(self.c.psum[banks[g]][:, t * P:(t + 1) * P], src[:, 4 * g + t, :],
                                 self.c.ident[:, :])
            i.then_inc(self.turned, 1)

    def copy_scalar(self, act, banks, n=2):
        for g in range(n):
            act.wait_ge(self.turned, g + 1)
            act.activation(self.c.xnT[:, g * CHUNK:(g + 1) * CHUNK], self.c.psum[banks[g]][:, :],
                           ACT.Copy).then_inc(self.copied, 1)

    def copy_vector(self, dve, banks, n=2):
        for g in range(n, CHUNKS):
            dve.wait_ge(self.turned, g + 1)
            dve.tensor_copy(self.c.xnT[:, g * CHUNK:(g + 1) * CHUNK],
                            self.c.psum[banks[g]][:, :]).then_inc(self.copied, 1)


def attention(chip, tag, biased=False, rope=False, full_mask=None, causal=False, key_mask=None,
              out_bias=True):
    nc, c, dram = chip.nc, chip, chip.dram
    SCALE = float(HD) ** -0.5
    masked = causal or full_mask is not None
    with ExitStack() as ctx:
        def sb(name, shape, dt=F32):
            return ctx.enter_context(nc.sbuf_tensor(f"{tag}_{name}", shape, dt))

        sem = Semaphores(nc, ctx, tag)
        norm = Norm(chip, ctx, tag + "n", sem)
        wq, wk, wv, wo = (sb(n, [P, P]) for n in ("wq", "wk", "wv", "wo"))
        wsq, wsk = (sb(n, [P, P]) for n in ("wsq", "wsk")) if rope else (None, None)
        cos, sin = (sb(n, [P, S]) for n in ("cos", "sin")) if rope else (None, None)
        bqk = sb("bqk", [P, 2]) if biased else None
        bv = sb("bv", [P, D]) if biased else None
        bo = sb("bo", [1, D]) if out_bias else None
        ctxb = sb("ctxb", [P, 2, S])
        qk = sb("qk", [P, 2, S])
        qks = sb("qks", [P, 2, S]) if rope else None
        rest = sb("rest", [P, 2, S])
        parts = sb("parts", [P, PARTS, 2, S], BF16)
        nmax = sb("nmax", [P, 2, 2, PAIRS])
        nrest = sb("nrest", [P, 2, PAIRS])
        nparts = sb("nparts", [P, 2, 2, 4 * PAIRS], BF16)
        probs = sb("probs", [P, 4, 2, S])
        pv = sb("pv", [P, 2, CHUNK])
        recip = sb("recip", [P, 2, 2, 4])
        o = sb("o", [P, 2, D])
        oT = sb("oT", [P, S])
        maskq = sb("maskq", [P, 2, 2, S], BF16) if masked else None
        maskk = sb("maskk", [P, 2, 2, S], BF16) if masked else None
        rawq = sb("rawq", [P, 2, S], I32) if full_mask else None
        rawk = sb("rawk", [P, 2, S], I32) if full_mask else None
        km = sb("km", [B, S], I32) if key_mask else None
        kmb = sb("kmb", [B, S], BF16) if key_mask else None

        def scratch(name, shape, dt):
            return nc.dram_tensor(f"{tag}_{name}", shape, dt, kind="Internal").ap()

        q_dram, k_dram = (scratch(n, (2, P, BLOCKS, S), BF16) for n in ("q_dram", "k_dram"))
        m_dram = scratch("m_dram", (B, S), BF16) if key_mask else None

        weights_in = sem("weights_in")
        ctx_in = [sem("ctx_in0"), sem("ctx_in1")]
        stack_in = [sem("stack_in0"), sem("stack_in1")]
        split_out = sem("split_out")
        maskq_in, maskk_in, maskq_made, maskk_made = (sem(n) for n in ("mq_in", "mk_in", "mq_made", "mk_made"))
        keymask_in, keymask_made, keymask_out = (sem(n) for n in ("km_in", "km_made", "km_out"))
        qk_ready, qk_read, sw_ready, sw_read = (sem(n) for n in ("qk_ready", "qk_read", "sw_ready", "sw_read"))
        v_ready, v_read = sem("v_ready"), sem("v_read")
        split_done = sem("split_done")
        max_ready, max_read = sem("max_ready"), sem("max_read")
        nsplit_done = sem("nsplit_done")
        mT_ready, mT_read = sem("mT_ready"), sem("mT_read")
        score_ready, exp_done = sem("score_ready"), sem("exp_done")
        pv_ready, pv_read = sem("pv_ready"), sem("pv_read")
        heads_turned, recip_done, heads_read = sem("heads_turned"), sem("recip_done"), sem("heads_read")
        o_turned, oT_read = sem("o_turned"), sem("oT_read")
        out_ready, out_read = sem("out_ready"), sem("out_read")
        dve_own, pool_own = sem("dve_own"), sem("pool_own")
        sp_passed, pool_passed = sem("sp_passed"), sem("pool_passed")

        MAXB, SCB, PVB, AUX, TAIL = (0, 1), (2, 3), (4, 5), 6, 7
        auxb = c.psum[AUX][:, :].bitcast(BF16)
        weight_names = [("wq", wq), ("wk", wk), ("wv", wv), ("wo", wo)]
        n_stack = 4 + (2 if key_mask else 0)

        n_weights = len(weight_names) + 4 * rope + 3 * biased + out_bias

        def mask_slot(u):
            return 0 if causal else u

        block = sem.open_block()

        @block.sync
        def _(sp):
            for name, tile in weight_names:
                sp.dma_start(tile[:, :], dram[f"{tag}_{name}"]).then_inc(weights_in, 16)
            if rope:
                for name, tile in (("wsq", wsq), ("wsk", wsk), ("cos", cos), ("sin", sin)):
                    sp.dma_start(tile[:, :], dram[f"{tag}_{name}"]).then_inc(weights_in, 16)
            if biased:
                for n, name in enumerate(("bq", "bk")):
                    sp.dma_start(bqk[:, n:n + 1], dram[f"{tag}_{name}"].rearrange("(p a) -> p a", a=1)).then_inc(weights_in, 16)
                sp.dma_start(bv[:, :], dram[f"{tag}_bv"].rearrange("(a n) -> a n", a=1).to_broadcast([P, D])).then_inc(weights_in, 16)
            if out_bias:
                sp.dma_start(bo[:, :], dram[f"{tag}_bo"].rearrange("(a n) -> a n", a=1)).then_inc(weights_in, 16)
            if key_mask:
                sp.dma_start(km[:, :], dram[key_mask]).then_inc(keymask_in, 16)
                sp.wait_ge(keymask_made, 1)
                sp.dma_start(m_dram, kmb[:, :]).then_inc(keymask_out, 16)
                sp.wait_ge(keymask_out, 16)

            def load_ctx(j, u):
                sp.dma_start(ctxb[:, u, :], dram["ctxT"][:, bass.ds((2 * j + u) * S, S)]).then_inc(ctx_in[u], 16)

            def load_maskq(b):
                at_least(sp, maskq_made, b)
                apart(sp, b, sp_passed)
                sp.dma_start(rawq[:, :, :], dram[full_mask][bass.ds(b, 1), :, :]
                             .rearrange("a (t p) k -> p (a t) k", p=P)).then_inc(maskq_in, 16)

            def load_maskk(b):
                at_least(sp, maskk_made, b)
                apart(sp, b, sp_passed)
                sp.dma_start(rawk[:, :, :], dram[full_mask + "_T"][bass.ds(b, 1), :, :]
                             .rearrange("a (t p) q -> p (a t) q", p=P)).then_inc(maskk_in, 16)

            def write_parts(j, u):
                b = 2 * j + u
                if not (isinstance(j, int) and j == 0):
                    sp.wait_ge(stack_in[u], 16 * n_stack * j)
                    apart(sp, j, sp_passed)
                sp.wait_ge(split_done, b + 1)
                for n, (where, blocks) in enumerate(((q_dram, Q_BLOCKS), (k_dram, K_BLOCKS))):
                    for first, count, part, step in blocks:
                        if step:
                            src = parts[:, part:part + count, n, :]
                        else:
                            src = parts[:, part:part + 1, n, :].to_broadcast([P, count, S])
                        sp.dma_start(where[u, :, first:first + count, :], src).then_inc(split_out, 16)
                sp.wait_ge(split_out, 96 * (b + 1))
                apart(sp, b, sp_passed)

            def load_stacks(j, u):
                b = 2 * j + u
                at_least(sp, score_ready, H * (b - 1))
                apart(sp, b, sp_passed)
                for par in range(2):
                    rows = slice(64 * par, 64 * par + STACK)
                    for where, dst in ((q_dram, c.qs[rows, u, :, :]), (k_dram, c.ks[rows, u, par::2, :])):
                        src = where[u].rearrange("(g h d) c t -> h (d c) g t", g=PAIRS, h=2)[par]
                        sp.dma_start(dst, src).then_inc(stack_in[u], 16)
                    if key_mask:
                        row = slice(64 * par + STACK, 64 * par + STACK + 1)
                        src = m_dram[bass.ds(b, 1), :].unsqueeze(1).to_broadcast([1, PAIRS, S])
                        sp.dma_start(c.ks[row, u, par::2, :], src).then_inc(stack_in[u], 16)

            def step(j, u, last=False):
                b = 2 * j + u
                if full_mask and not last:
                    load_maskq(b + 2)
                if full_mask and not (last and u == 1):
                    load_maskk(b + 1)
                if not last:
                    sp.wait_ge(v_ready, b + 1)
                    apart(sp, b, sp_passed)
                    load_ctx(j + 1, u)
                    write_parts(j + 1, u)
                    load_stacks(j + 1, u)

            load_ctx(0, 0)
            load_ctx(0, 1)
            if full_mask:
                load_maskq(0)
                load_maskk(0)
                load_maskq(1)
            for u in range(2):
                write_parts(0, u)
                load_stacks(0, u)
            step(0, 0)
            step(0, 1)
            with sp.Fori(1, B // 2 - 1) as j:
                step(j, 0)
                step(j, 1)
            step(B // 2 - 1, 0, True)
            step(B // 2 - 1, 1, True)

        @block.tensor
        def _(pe):
            pe.wait_ge(norm.normed, 1)
            norm.tensor(pe, c.xn, (0, 1, 2, 3))
            pe.wait_ge(norm.copied, CHUNKS)
            pe.wait_ge(weights_in, 16 * n_weights)

            def project_qk(j, u, a, b_, ready):
                b = 2 * j + u
                pe.wait_ge(ctx_in[u], 16 * (j + 1))
                pe.matmul(c.psum[AUX][:, 0:S], a[:, :], c.xnT[:, bass.ds(b * S, S)], start=True, stop=True)
                pe.matmul(c.psum[AUX][:, S:2 * S], b_[:, :], ctxb[:, u, :], start=True, stop=True).then_inc(ready, 1)

            def project_v(j, u):
                pe.wait_ge(ctx_in[u], 16 * (j + 1))
                for t in range(2):
                    i = pe.matmul(c.psum[AUX][:, t * D:(t + 1) * D], ctxb[:, u, t * P:(t + 1) * P], wv[:, :],
                                  start=True, stop=True)
                i.then_inc(v_ready, 1)

            def max_scores(b, u, h):
                bank = c.psum[MAXB[h % 2]]
                at_least(pe, max_read, H * b + h - 1)
                if masked:
                    if full_mask:
                        pe.wait_ge(maskq_made, b + 1)
                for t in range(2):
                    if masked:
                        pe.matmul(bank[:, t * S:(t + 1) * S], c.identb[:, :], maskq[:, mask_slot(u), t, :],
                                  start=True, stop=False)
                    i = pe.matmul(bank[:, t * S:(t + 1) * S], c.qs[:, u, h // 2, t * P:(t + 1) * P],
                                  c.ks[:, u, h, :], start=not masked, stop=True)
                i.then_inc(max_ready, 1)

            def turn_max(b, half):
                pe.wait_ge(nsplit_done, 2 * b + half + 1)
                for t in range(2):
                    i = pe.transpose(auxb[0:32, t * P:(t + 1) * P], nparts[:, half, t, :], c.identb[:, :])
                i.then_inc(mT_ready, 1)

            def scores(b, u, h):
                bank = c.psum[SCB[h % 2]]
                at_least(pe, exp_done, H * b + h - 1)
                if h % PAIRS == 0:
                    pe.wait_ge(mT_read, 2 * b + h // PAIRS + 1)
                if masked:
                    if full_mask:
                        pe.wait_ge(maskk_made, b + 1)
                    pe.matmul(bank[:, :], c.identb[:, :], maskk[:, mask_slot(u), :, :], start=True, stop=False)
                for t in range(2):
                    pe.matmul(bank[:, t * S:(t + 1) * S], c.ks[:, u, h, t * P:(t + 1) * P],
                              c.qs[:, u, h // 2, :], start=(not masked and t == 0), stop=False)
                pe.matmul(bank[:, :], c.pick[:, h % PAIRS, :],
                          c.mT[:, h // PAIRS, :].unsqueeze(1).to_broadcast([P, 2, S]), start=False,
                          stop=True).then_inc(score_ready, 1)

            def weigh(b, u, h):
                if h % 8 == 0:
                    at_least(pe, pv_read, 2 * b + h // 8 - 1)
                if h == 0:
                    pe.wait_ge(v_read, b + 1)
                pe.wait_ge(exp_done, H * b + h + 1)
                j = h % 4
                out = c.psum[PVB[h // 8]][32 * j:32 * j + 32, (h // 4 % 2) * S:(h // 4 % 2 + 1) * S]
                for t in range(2):
                    i = pe.matmul(out, c.vaug[:, u, t, h, :], probs[:, h % 4, t, :], start=(t == 0), stop=(t == 1))
                i.then_inc(pv_ready, 1)

            def turn_heads(b, half):
                pe.wait_ge(pv_read, 2 * b + half + 1)
                if half:
                    pe.wait_ge(heads_read, 2 * b + 1)
                else:
                    at_least(pe, out_read, b)
                for q in range(4):
                    i = pe.transpose(c.psum[TAIL][:, q * P:(q + 1) * P], pv[:, half, q * P:(q + 1) * P], c.ident[:, :])
                i.then_inc(heads_turned, 1)

            def turn_o(b):
                pe.wait_ge(heads_read, 2 * b + 2)
                for t in range(2):
                    i = pe.transpose(c.psum[TAIL][:, t * P:(t + 1) * P], o[:, t, :], c.ident[:, :])
                i.then_inc(o_turned, 1)

            def project_out(b):
                pe.wait_ge(oT_read, b + 1)
                for t in range(2):
                    dst = c.psum[TAIL][:, t * P:(t + 1) * P]
                    i = pe.matmul(dst, oT[:, t * P:(t + 1) * P], wo[:, :], start=True, stop=not out_bias)
                    if out_bias:
                        i = pe.matmul(dst, c.ones[0:1, :], bo[:, :], start=False, stop=True)
                i.then_inc(out_ready, 1)

            def step(j, u, last=False):
                b = 2 * j + u
                first = isinstance(b, int) and b == 0
                ends = last and u == 1
                for h in range(H):
                    scores(b, u, h)
                    if h < LAG:
                        max_scores(b, u, H - LAG + h)
                    elif not ends:
                        if h == LAG:
                            pe.wait_ge(stack_in[1 - u], 16 * n_stack * (j + 1 + u))
                        max_scores(b + 1, 1 - u, h - LAG)
                    if h > 0:
                        weigh(b, u, h - 1)
                    elif not first:
                        weigh(b - 1, 1 - u, H - 1)
                    if h == 2 and not first:
                        turn_heads(b - 1, 1)
                    if h == 4 and not first:
                        turn_o(b - 1)
                    if h == 6:
                        pe.wait_ge(mT_read, 2 * b + 1)
                        turn_max(b, 1)
                    if h == 7 and not first:
                        project_out(b - 1)
                    if h == 8 and not last:
                        pe.wait_ge(mT_read, 2 * b + 2)
                        project_qk(j + 1, u, wq, wk, qk_ready)
                    if h == 10:
                        if not ends:
                            pe.wait_ge(mT_read, 2 * b + 2)
                            if not last:
                                pe.wait_ge(qk_read, b + 3)
                            project_v(j + u, 1 - u)
                        turn_heads(b, 0)
                    if h == 12 and rope and not last:
                        pe.wait_ge(v_read, b + 2)
                        project_qk(j + 1, u, wsq, wsk, sw_ready)
                    if h == 14 and not ends:
                        pe.wait_ge(v_read, b + 2)
                        if rope and not last:
                            pe.wait_ge(sw_read, b + 3)
                        turn_max(b + 1, 0)

            for u in range(2):
                at_least(pe, qk_read, u)
                if rope:
                    at_least(pe, sw_read, u)
                project_qk(0, u, wq, wk, qk_ready)
                if rope:
                    pe.wait_ge(qk_read, u + 1)
                    project_qk(0, u, wsq, wsk, sw_ready)
            pe.wait_ge(qk_read, 2)
            if rope:
                pe.wait_ge(sw_read, 2)
            project_v(0, 0)
            pe.wait_ge(stack_in[0], 16 * n_stack)
            for h in range(H - LAG):
                max_scores(0, 0, h)
            pe.wait_ge(v_read, 1)
            turn_max(0, 0)
            step(0, 0)
            step(0, 1)
            with pe.Fori(1, B // 2 - 1) as j:
                step(j, 0)
                step(j, 1)
            step(B // 2 - 1, 0, True)
            step(B // 2 - 1, 1, True)
            weigh(B - 1, 1, H - 1)
            turn_heads(B - 1, 1)
            turn_o(B - 1)
            project_out(B - 1)

        @block.scalar
        def _(act):
            norm.scalar(act, c.xn, 1)
            norm.copy_scalar(act, (0, 1, 2, 3))

            def take_qk(b, dst, ready, read, bias):
                act.wait_ge(ready, b + 1)
                at_least(act, split_done, b)
                if bias:
                    act.wait_ge(weights_in, 16 * n_weights)
                    act.activation(dst[:, 0, :], c.psum[AUX][:, 0:S], ACT.Identity, bias=bqk[:, 0:1])
                    act.activation(dst[:, 1, :], c.psum[AUX][:, S:2 * S], ACT.Identity,
                                   bias=bqk[:, 1:2]).then_inc(read, 1)
                else:
                    act.activation(dst[:, :, :], c.psum[AUX][:, :], ACT.Copy).then_inc(read, 1)

            def take_max(b, half):
                act.wait_ge(mT_ready, 2 * b + half + 1)
                at_least(act, score_ready, H * (b - 1) + 8 * (half + 1))
                act.activation(c.mT[0:32, half, :], auxb[0:32, 0:S], ACT.Copy).then_inc(mT_read, 1)

            def take_pv(b, half):
                act.wait_ge(pv_ready, H * b + 8 * (half + 1))
                at_least(act, heads_turned, 2 * (b - 1) + half + 1)
                act.activation(pv[:, half, :], c.psum[PVB[half]][:, :], ACT.Copy).then_inc(pv_read, 1)

            def step(j, u, last=False):
                b = 2 * j + u
                first = isinstance(b, int) and b == 0
                ends = last and u == 1
                for h in range(H):
                    act.wait_ge(score_ready, H * b + h + 1)
                    at_least(act, pv_ready, H * b + h - 3)
                    act.activation(probs[:, h % 4, :, :], c.psum[SCB[h % 2]][:, :], ACT.Exp,
                                   scale=SCALE).then_inc(exp_done, 1)
                    if h == 1 and not first:
                        take_pv(b - 1, 1)
                    if h == 5 and not first:
                        act.wait_ge(o_turned, b)
                        act.activation(oT[:, :], c.psum[TAIL][:, 0:S], ACT.Copy).then_inc(oT_read, 1)
                    if h == 6:
                        take_max(b, 1)
                    if h == 8 and not last:
                        take_qk(b + 2, qk, qk_ready, qk_read, biased)
                    if h == 9:
                        take_pv(b, 0)
                    if h == 12 and rope and not last:
                        take_qk(b + 2, qks, sw_ready, sw_read, False)
                    if h == 14 and not ends:
                        take_max(b + 1, 0)

            for u in range(2):
                take_qk(u, qk, qk_ready, qk_read, biased)
                if rope:
                    take_qk(u, qks, sw_ready, sw_read, False)
            take_max(0, 0)
            step(0, 0)
            step(0, 1)
            with act.Fori(1, B // 2 - 1) as j:
                step(j, 0)
                step(j, 1)
            step(B // 2 - 1, 0, True)
            step(B // 2 - 1, 1, True)
            take_pv(B - 1, 1)
            act.wait_ge(o_turned, B)
            act.activation(oT[:, :], c.psum[TAIL][:, 0:S], ACT.Copy).then_inc(oT_read, 1)

        @block.vector
        def _(dve):
            chain = Chain(dve, dve_own)
            if key_mask:
                dve.wait_ge(keymask_in, 16)
                dve.tensor_scalar(kmb[:, :], km[:, :], 0.0, NEG, ALU.is_equal, ALU.mult).then_inc(keymask_made, 1)
            norm.vector(dve, chain, c.x, c.xn, LN_EPS)
            norm.copy_vector(dve, (0, 1, 2, 3))
            if biased:
                dve.wait_ge(weights_in, 16 * n_weights)

            def take_v(b, u):
                dve.wait_ge(v_ready, b + 1)
                at_least(dve, pv_ready, H * (b - 1))
                for t in range(2):
                    dst = c.vaug[:, u, t, :, 0:HD]
                    src = c.psum[AUX][:, t * D:(t + 1) * D].rearrange("p (h d) -> p h d", h=H)
                    if biased:
                        i = dve.tensor_tensor(dst, src, bv[:, :].rearrange("p (h d) -> p h d", h=H), ALU.add)
                    else:
                        i = dve.tensor_copy(dst, src)
                i.then_inc(v_read, 1)

            def head_max(b, h):
                dve.wait_ge(max_ready, H * b + h + 1)
                if h % 8 == 0:
                    at_least(dve, nsplit_done, 2 * b + h // 8 - 1)
                dve.tensor_reduce(nmax[:, h // 8, :, h % 8], c.psum[MAXB[h % 2]][:, :].rearrange(
                    "p (t k) -> p t k", t=2), AXX, ALU.max, negate=True).then_inc(max_read, 1)

            def take_heads(b, half):
                dve.wait_ge(heads_turned, 2 * b + half + 1)
                t4 = c.psum[TAIL][:, :].rearrange("p (g t h w) -> p g t h w", g=2, t=2, h=4)
                for t in range(2):
                    i = dve.reciprocal(recip[:, t, :, :], t4[:, :, t, :, HD])
                i.then_inc(recip_done, 1)
                dve.wait_ge(recip_done, 2 * b + half + 1)
                at_least(dve, o_turned, b)
                for t in range(2):
                    i = dve.tensor_tensor(
                        o[:, t, 64 * half:64 * half + 64].rearrange("p (g h d) -> p g h d", g=2, h=4),
                        t4[:, :, t, :, 0:HD], recip[:, t, :, :].unsqueeze(3).to_broadcast([P, 2, 4, HD]), ALU.mult)
                i.then_inc(heads_read, 1)

            def add_out(b):
                dve.wait_ge(out_ready, b + 1)
                xs = c.x[:, bass.ds(2 * b, 2), :]
                dve.tensor_tensor(xs, xs, c.psum[TAIL][:, 0:S].rearrange("p (t d) -> p t d", t=2),
                                  ALU.add).then_inc(out_read, 1)

            def make_maskq(b, u):
                dve.wait_ge(maskq_in, 16 * (b + 1))
                at_least(dve, max_ready, H * (b - 1))
                dve.tensor_scalar(maskq[:, u, :, :], rawq[:, :, :], 0.0, MASKED, ALU.is_equal,
                                  ALU.mult).then_inc(maskq_made, 1)

            def make_maskk(b, u):
                dve.wait_ge(maskk_in, 16 * (b + 1))
                at_least(dve, score_ready, H * (b - 1))
                dve.tensor_scalar(maskk[:, u, :, :], rawk[:, :, :], 0.0, MASKED, ALU.is_equal,
                                  ALU.mult).then_inc(maskk_made, 1)

            def step(j, u, last=False):
                b = 2 * j + u
                first = isinstance(b, int) and b == 0
                ends = last and u == 1
                for h in range(H):
                    if h < LAG:
                        head_max(b, H - LAG + h)
                    elif not ends:
                        head_max(b + 1, h - LAG)
                    if h == 2 and not first:
                        take_heads(b - 1, 1)
                    if h == 6 and full_mask and not last:
                        make_maskq(b + 2, u)
                    if h == 8 and not first:
                        add_out(b - 1)
                    if h == 10 and not ends:
                        take_v(b + 1, 1 - u)
                    if h == 11:
                        take_heads(b, 0)
                    if h == 12 and full_mask and not ends:
                        make_maskk(b + 1, 1 - u)

            if full_mask:
                make_maskq(0, 0)
                make_maskk(0, 0)
                make_maskq(1, 1)
            take_v(0, 0)
            for h in range(H - LAG):
                head_max(0, h)
            step(0, 0)
            step(0, 1)
            with dve.Fori(1, B // 2 - 1) as j:
                step(j, 0)
                step(j, 1)
            step(B // 2 - 1, 0, True)
            step(B // 2 - 1, 1, True)
            take_heads(B - 1, 1)
            add_out(B - 1)

        @block.gpsimd
        def _(pool):
            chain = Chain(pool, pool_own, passed=pool_passed)
            chain(pool.memset(nparts[:, :, :, :], 0.0))
            if causal:
                for table, sign in ((maskq, 1), (maskk, -1)):
                    chain(pool.memset(table[:, 0, :, :], 0.0))
                    for t in range(2):
                        chain(pool.affine_select(out=table[:, 0, t, :], in_=table[:, 0, t, :],
                                                 compare_op=ALU.is_ge, fill=NEG, base=sign * P * t,
                                                 pattern=[[-sign, S]], channel_multiplier=sign))
            if rope:
                pool.wait_ge(weights_in, 16 * n_weights)
            setup = chain.n
            per_step = 8 + (7 if rope else 4)

            def split(src, spare, dsts, last_sem):
                for n, dst in enumerate(dsts):
                    i = pool.tensor_scalar(dst, src, 1.0, 1.0, ALU.mult, ALU.mult)
                    if n == PARTS - 1:
                        i.then_inc(last_sem, 1)
                    else:
                        chain(i)
                        chain(pool.tensor_tensor(spare, src, dst, ALU.subtract))
                        src = spare

            def split_max(b, half):
                pool.wait_ge(max_read, H * b + 8 * (half + 1))
                at_least(pool, mT_ready, 2 * b + half - 1)
                apart(pool, b, pool_passed)
                split(nmax[:, half, :, :], nrest[:, :, :],
                      [nparts[:, half, :, 8 * n:8 * n + 8] for n in range(PARTS)], nsplit_done)

            def split_qk(b):
                pool.wait_ge(qk_read, b + 1)
                at_least(pool, split_out, 96 * b)
                apart(pool, b, pool_passed)
                if rope:
                    pool.wait_ge(sw_read, b + 1)
                    both = [P, 2, S]
                    chain(pool.tensor_tensor(qk[:, :, :], qk[:, :, :], cos[:, :].unsqueeze(1).to_broadcast(both), ALU.mult))
                    chain(pool.tensor_tensor(qks[:, :, :], qks[:, :, :], sin[:, :].unsqueeze(1).to_broadcast(both), ALU.mult))
                    chain(pool.tensor_tensor(qk[:, :, :], qk[:, :, :], qks[:, :, :], ALU.add))
                split(qk[:, :, :], rest[:, :, :], [parts[:, n, :, :] for n in range(PARTS)], split_done)

            def step(j, u, last=False):
                b = 2 * j + u
                split_max(b, 1)
                if not last:
                    split_qk(b + 2)
                if not (last and u == 1):
                    split_max(b + 1, 0)

            split_qk(0)
            split_qk(1)
            split_max(0, 0)
            before = chain.n
            step(0, 0)
            step(0, 1)
            assert chain.n == before + 2 * per_step, (chain.n, before, per_step)
            with pool.Fori(1, B // 2 - 1) as j:
                chain.rebase(before + 2 * per_step * j)
                step(j, 0)
                step(j, 1)
            chain.rebase(before + 2 * per_step * (B // 2 - 1))
            step(B // 2 - 1, 0, True)
            step(B // 2 - 1, 1, True)


def top_experts(dve, chain, cur, n, k, sel, tmp, flag, best, lower):
    every = [P, TILES, n]

    def all_of(a):
        return a.unsqueeze(2).to_broadcast(every)

    for i in range(k):
        top = best[:, i, :]
        chain(dve.tensor_reduce(top, cur, AXX, ALU.max))
        chain(dve.tensor_tensor(tmp, cur, all_of(top), ALU.is_equal))
        chain(dve.tensor_tensor(tmp, tmp, lower, ALU.mult))
        chain(dve.tensor_reduce(flag, tmp, AXX, ALU.max))
        chain(dve.tensor_tensor(tmp, tmp, all_of(flag), ALU.is_equal))
        if i == 0:
            chain(dve.tensor_copy(sel, tmp))
        else:
            chain(dve.tensor_tensor(sel, sel, tmp, ALU.add))
        if i < k - 1:
            chain(dve.scalar_tensor_tensor(cur, tmp, NEG, cur, ALU.mult, ALU.add))


def experts(chip, tag, kind):
    nc, c, dram = chip.nc, chip, chip.dram
    shared = kind == "capacity"
    E = {"capacity": 32, "nearest": 8, "top": 16}[kind]
    HB = {"capacity": 1, "nearest": 2, "top": 4}[kind]
    UP = {"capacity": 2, "nearest": 4, "top": 4}[kind]
    gated = kind != "top"
    UNITS = HB * CHUNKS
    K = {"capacity": 4, "nearest": 1, "top": 4}[kind]
    GROUPS = 8
    CAP = int(1.25 * N * 4 / 32)
    ACTF = ACT.Silu if gated else ACT.Gelu
    SLOTS = 4
    with ExitStack() as ctx:
        def sb(name, shape, dt=F32):
            return ctx.enter_context(nc.sbuf_tensor(f"{tag}_{name}", shape, dt))

        sem = Semaphores(nc, ctx, tag)
        norm = Norm(chip, ctx, tag + "n", sem)
        router = sb("router", [P, E])
        up = sb("up", [P, 2, UP, P])
        down = sb("down", [P, 2, HB, P])
        gate = sb("gate", [P, 2, N])
        act_out = sb("act_out", [P, SLOTS, CHUNK])
        weighed = sb("weighed", [P, SLOTS, CHUNK]) if gated else None
        hidden = sb("hidden", [P, SLOTS, CHUNK])
        sharedw = sb("sharedw", [P, 3, P]) if shared else None
        logits, work, tmp, sel, W = (sb(n, [P, TILES, E]) for n in ("logits", "work", "tmp", "sel", "W"))
        best = sb("best", [P, 4, TILES])
        flag = sb("flag", [P, TILES])
        gT = sb("gT", [E, N])
        outT = sb("outT", [P, N])
        g_dram = nc.dram_tensor(f"{tag}_gates", (E, N), F32, kind="Internal").ap()
        xr = c.xn
        if shared:
            grp, gwork, gtmp, gsel = (sb(n, [P, TILES, GROUPS]) for n in ("grp", "gwork", "gtmp", "gsel"))
            selb = sb("selb", [P, TILES, E], BF16)
            upper = sb("upper", [P, P], BF16)
            onesb = sb("onesb", [P, P], BF16)
        if kind == "nearest":
            xr = sb("xr", [P, TILES, D])
            scale = sb("scale", [P, D])
            csq, cm2 = sb("csq", [P, E]), sb("cm2", [P, E])
            nx = sb("nx", [P, TILES])
        if kind == "top":
            csq, cm2 = sb("csq", [P, E]), sb("cm2", [P, E])
            rw = sb("rw", [P, E])
            rb = sb("rb", [1, E])
            b1 = sb("b1", [P, 2, HB])
            b2 = sb("b2", [E, D])
            nx = sb("nx", [P, TILES])

        small_in = sem("small_in")
        w_in = [sem("w_in0"), sem("w_in1")]
        g_in = [sem("g_in0"), sem("g_in1")]
        scaled = sem("scaled")
        router_made, logits_ready, shifted, exped = (sem(n) for n in ("router_made", "logits_ready", "shifted", "exped"))
        sel_ready, counted, gates_ready, gates_turned, gates_copied, gates_out = (
            sem(n) for n in ("sel_ready", "counted", "gates_ready", "gates_turned", "gates_copied", "gates_out"))
        up_ready, act_done, weighed_done, hidden_done, down_done = (
            sem(n) for n in ("up_ready", "act_done", "weighed_done", "hidden_done", "down_done"))
        acc_ready, acc_copied, out_turned = sem("acc_ready"), sem("acc_copied"), sem("out_turned")
        sp_passed = sem("sp_passed")
        dve_own, pool_own, act_own, pe_own = sem("dve_own"), sem("pool_own"), sem("act_own"), sem("pe_own")

        OFF = CHUNKS if shared else 0
        ACC = (0, 1, 2, 3)
        A_BANKS = (4, 5) if gated else (4, 5, 6, 7)
        NA = len(A_BANKS)
        LOGITS = 4
        n_small = {"capacity": 4, "nearest": 2, "top": 4}[kind]
        n_w = {"capacity": 3, "nearest": 2, "top": 3}[kind]
        block = sem.open_block()

        @block.sync
        def _(sp):
            sp.dma_start(router[:, :], dram[f"{tag}_router"]).then_inc(small_in, 16)
            if shared:
                for n, name in enumerate(("sw1", "sw3", "sw2")):
                    sp.dma_start(sharedw[:, n, :], dram[f"{tag}_{name}"]).then_inc(small_in, 16)
            if kind == "nearest":
                sp.dma_start(scale[:, :], dram[f"{tag}_scale"].rearrange("(a n) -> a n", a=1)
                             .to_broadcast([P, D])).then_inc(small_in, 16)
            if kind == "top":
                sp.dma_start(rw[:, :], dram[f"{tag}_rw"]).then_inc(small_in, 16)
                sp.dma_start(rb[:, :], dram[f"{tag}_rb"].rearrange("(a n) -> a n", a=1)).then_inc(small_in, 16)
                sp.dma_start(b2[:, :], dram[f"{tag}_b2"]).then_inc(small_in, 16)

            def load(j, u):
                e = 2 * j + u
                at_least(sp, down_done, OFF + UNITS * (e - 1))
                apart(sp, e, sp_passed)
                one = bass.ds(e, 1)
                if kind == "capacity":
                    for n, name in enumerate(("w1", "w3")):
                        sp.dma_start(up[:, u, n, :], dram[f"{tag}_{name}"][one, :, :].rearrange("e d h -> d (e h)"))\
                          .then_inc(w_in[u], 16)
                    sp.dma_start(down[:, u, 0, :], dram[f"{tag}_w2"][one, :, :].rearrange("e h d -> h (e d)"))\
                      .then_inc(w_in[u], 16)
                else:
                    sp.dma_start(up[:, u, :, :], dram[f"{tag}_up"][one, :, :].rearrange("e d (b h) -> d (e b) h", b=UP))\
                      .then_inc(w_in[u], 16)
                    sp.dma_start(down[:, u, :, :], dram[f"{tag}_down"][one, :, :].rearrange("e (b h) d -> h (e b) d", b=HB))\
                      .then_inc(w_in[u], 16)
                if kind == "top":
                    sp.dma_start(b1[:, u, :], dram[f"{tag}_b1"][one, :, :].rearrange("e p b -> p (e b)"))\
                      .then_inc(w_in[u], 16)

            def load_gate(j, u):
                e = 2 * j + u
                at_least(sp, weighed_done if gated else hidden_done, OFF + UNITS * (e - 1))
                apart(sp, e, sp_passed)
                sp.dma_start(gate[:, u, :], g_dram[bass.ds(e, 1), :].to_broadcast([P, N])).then_inc(g_in[u], 16)

            load(0, 0)
            load(0, 1)
            sp.wait_ge(gates_copied, CHUNKS)
            sp.dma_start(g_dram, gT[:, :]).then_inc(gates_out, 16)
            sp.wait_ge(gates_out, 16)
            load_gate(0, 0)
            load_gate(0, 1)
            with sp.Fori(1, E // 2) as j:
                for u in range(2):
                    load(j, u)
                    load_gate(j, u)

        @block.tensor
        def _(pe):
            pe.wait_ge(*((scaled, 1) if kind == "nearest" else (norm.normed, 1)))
            norm.tensor(pe, xr, (0, 1, 2, 3))
            pe.wait_ge(norm.copied, CHUNKS)
            pe.wait_ge(small_in, 16 * n_small)
            if kind != "capacity":
                pe.wait_ge(router_made, 2)
            for t in range(TILES):
                dst = c.psum[LOGITS][:, t * E:(t + 1) * E]
                lhs = c.xnT[:, t * P:(t + 1) * P]
                if kind == "capacity":
                    i = pe.matmul(dst, lhs, router[:, :], start=True, stop=True)
                else:
                    pe.matmul(dst, lhs, cm2[:, :], start=True, stop=False)
                    if kind == "top":
                        pe.matmul(dst, lhs, rw[:, :], start=False, stop=False)
                        pe.matmul(dst, c.ones[0:1, :], rb[:, :], start=False, stop=False)
                    i = pe.matmul(dst, c.ones[:, :], csq[:, :], start=False, stop=True)
            i.then_inc(logits_ready, 1)
            if shared:
                pe.wait_ge(sel_ready, 1)
                pe.wait_ge(pool_own, 3)
                bank = c.psum[LOGITS + 1]
                pe.matmul(bank[:, :], upper[:, :], selb[:, :, :], start=True, stop=False)
                for t in range(TILES - 1):
                    rest = TILES - 1 - t
                    pe.matmul(bank[:, (t + 1) * E:], onesb[:, :],
                              selb[:, t:t + 1, :].to_broadcast([P, rest, E]), start=False, stop=False)
                i = pe.matmul(bank[:, :], c.zrow[:, 0:P], c.zrow[:, :], start=False, stop=True)
                i.then_inc(counted, 1)
            pe.wait_ge(gates_ready, 1)
            for g in range(CHUNKS):
                for t in range(4):
                    i = pe.transpose(c.psum[g][0:E, t * P:(t + 1) * P], W[:, 4 * g + t, :], c.ident[:, :])
                i.then_inc(gates_turned, 1)
            pe.wait_ge(gates_copied, CHUNKS)
            for g in range(CHUNKS):
                if kind == "top":
                    pe.matmul(c.psum[ACC[g]][:, :], b2[:, :], gT[:, g * CHUNK:(g + 1) * CHUNK], start=True, stop=False)
                else:
                    pe.matmul(c.psum[ACC[g]][:, :], c.zrow[:, 0:P], c.zrow[:, :], start=True, stop=False)

            def project_up(n, k, ups):
                cs = slice(k % CHUNKS * CHUNK, (k % CHUNKS + 1) * CHUNK)
                at_least(pe, act_done, n - NA + 1)
                i = pe.matmul(c.psum[A_BANKS[k % NA]][:, :], ups[0], c.xnT[:, cs], start=True, stop=True)
                if gated:
                    at_least(pe, hidden_done, n - 1)
                    i = pe.matmul(c.psum[6 + k % 2][:, :], ups[1], c.xnT[:, cs], start=True, stop=True)
                i.then_inc(up_ready, 1)

            def project_down(n, k, w):
                pe.wait_ge(hidden_done, n + 1)
                pe.matmul(c.psum[ACC[k % CHUNKS]][:, :], w, hidden[:, k % SLOTS, :], start=False,
                          stop=False).then_inc(down_done, 1)

            def ups(u, k):
                i = k // CHUNKS
                if kind == "capacity":
                    return up[:, u, 0, :], up[:, u, 1, :]
                if kind == "nearest":
                    return up[:, u, 2 + i, :], up[:, u, i, :]
                return (up[:, u, i, :],)

            def expert(j, u, first=False):
                n0 = OFF + UNITS * (2 * j + u)
                for k in range(UNITS):
                    if k == 0:
                        pe.wait_ge(w_in[u], 16 * n_w * (j + 1))
                    project_up(n0 + k, k, ups(u, k))
                    if k > 0:
                        project_down(n0 + k - 1, k - 1, down[:, u, (k - 1) // CHUNKS, :])
                    elif not first:
                        project_down(n0 - 1, UNITS - 1, down[:, 1 - u, HB - 1, :])

            if shared:
                for k in range(CHUNKS):
                    project_up(k, k, (sharedw[:, 0, :], sharedw[:, 1, :]))
                    if k:
                        project_down(k - 1, k - 1, sharedw[:, 2, :])
                project_down(CHUNKS - 1, CHUNKS - 1, sharedw[:, 2, :])
            expert(0, 0, True)
            expert(0, 1)
            with pe.Fori(1, E // 2) as j:
                expert(j, 0)
                expert(j, 1)
            project_down(OFF + UNITS * E - 1, UNITS - 1, down[:, 1, HB - 1, :])
            for g in range(CHUNKS):
                pe.matmul(c.psum[ACC[g]][:, :], c.zrow[:, 0:P], c.zrow[:, :], start=False,
                          stop=True).then_inc(acc_ready, 1)
            for g in range(CHUNKS):
                pe.wait_ge(acc_copied, g + 1)
                for t in range(4):
                    i = pe.transpose(c.psum[4 + g][:, t * P:(t + 1) * P],
                                     outT[:, (4 * g + t) * P:(4 * g + t + 1) * P], c.ident[:, :])
                i.then_inc(out_turned, 1)

        @block.scalar
        def _(act):
            chain = Chain(act, act_own)
            norm.scalar(act, c.xn, 1)
            if kind == "nearest":
                norm.scalar(act, c.xn, 2)
            if kind != "capacity":
                act.wait_ge(small_in, 16 * n_small)
                sign = 1.0 if kind == "nearest" else -1.0
                act.mul(cm2[:, :], router[:, :], -2.0 * sign).then_inc(router_made, 1)
                chain(act.activation(csq[:, :], router[:, :], ACT.Square))
                act.mul(csq[:, :], csq[:, :], sign).then_inc(router_made, 1)
            norm.copy_scalar(act, (0, 1, 2, 3))
            if kind != "nearest":
                act.wait_ge(shifted, 1)
                act.activation(work[:, :, :], work[:, :, :], ACT.Exp).then_inc(exped, 1)
            for g in range(CHUNKS):
                act.wait_ge(gates_turned, g + 1)
                act.activation(gT[:, g * CHUNK:(g + 1) * CHUNK], c.psum[g][0:E, :], ACT.Copy).then_inc(gates_copied, 1)

            def unit(n, k, bias=0.0):
                act.wait_ge(up_ready, n + 1)
                at_least(act, weighed_done if gated else hidden_done, n - SLOTS + 1)
                act.activation(act_out[:, k % SLOTS, :], c.psum[A_BANKS[k % NA]][:, :], ACTF,
                               bias=bias).then_inc(act_done, 1)

            for k in range(OFF):
                unit(k, k)

            def expert(j, u):
                n0 = OFF + UNITS * (2 * j + u)
                if kind == "top":
                    act.wait_ge(w_in[u], 16 * n_w * (j + 1))
                for k in range(UNITS):
                    bias = 0.0
                    if kind == "top":
                        bias = b1[:, u, k // CHUNKS:k // CHUNKS + 1]
                    unit(n0 + k, k, bias)

            expert(0, 0)
            expert(0, 1)
            with act.Fori(1, E // 2) as j:
                expert(j, 0)
                expert(j, 1)
            for g in range(0, CHUNKS):
                act.wait_ge(acc_ready, g + 1)
                act.activation(outT[:, g * CHUNK:(g + 1) * CHUNK], c.psum[ACC[g]][:, :], ACT.Copy).then_inc(acc_copied, 1)

        @block.vector
        def _(dve):
            chain = Chain(dve, dve_own)
            norm.vector(dve, chain, c.x, c.xn, LN_EPS)
            if kind == "nearest":
                norm.vector(dve, chain, c.xn, xr, 1e-6, centre=False)
                dve.wait_ge(small_in, 16 * n_small)
                dve.tensor_tensor(xr[:, :, :], xr[:, :, :], scale[:, :].unsqueeze(1).to_broadcast([P, TILES, D]),
                                  ALU.mult).then_inc(scaled, 1)
                dve.wait_ge(scaled, 1)
            norm.copy_vector(dve, (0, 1, 2, 3))
            every = [P, TILES, E]

            def all_of(a):
                return a.unsqueeze(2).to_broadcast(every)

            lower = c.rev[:, 0:E].unsqueeze(1).to_broadcast(every)
            lg = c.psum[LOGITS][:, 0:TILES * E].rearrange("p (t e) -> p t e", t=TILES)
            if kind != "capacity":
                chain(dve.tensor_tensor(norm.sq[:, :, :], xr[:, :, :], xr[:, :, :], ALU.mult))
                chain(dve.tensor_reduce(nx[:, :], norm.sq[:, :, :], AXX, ALU.add))
            dve.wait_ge(logits_ready, 1)
            if kind == "capacity":
                chain(dve.tensor_reduce(flag[:, :], lg, AXX, ALU.max))
                dve.tensor_tensor(work[:, :, :], lg, all_of(flag[:, :]), ALU.subtract).then_inc(shifted, 1)
                dve.wait_ge(exped, 1)
                chain(dve.tensor_reduce(flag[:, :], work[:, :, :], AXX, ALU.add))
                chain(dve.reciprocal(flag[:, :], flag[:, :]))
                chain(dve.tensor_tensor(logits[:, :, :], work[:, :, :], all_of(flag[:, :]), ALU.mult))
                chain(dve.tensor_reduce(gwork[:, :, :], logits[:, :, :].rearrange("p t (g i) -> p (t g) i", g=GROUPS),
                                        AXX, ALU.max))
                top_experts(dve, chain, gwork[:, :, :], GROUPS, 4, gsel[:, :, :], gtmp[:, :, :], flag[:, :], best,
                            c.rev[:, 0:GROUPS].unsqueeze(1).to_broadcast([P, TILES, GROUPS]))
                by_group = [P, TILES * GROUPS, E // GROUPS]
                keep = gsel[:, :, :].rearrange("p t g -> p (t g)").unsqueeze(2).to_broadcast(by_group)
                less = gtmp[:, :, :].rearrange("p t g -> p (t g)").unsqueeze(2).to_broadcast(by_group)
                cur = work[:, :, :].rearrange("p t (g i) -> p (t g) i", g=GROUPS)
                chain(dve.tensor_scalar(gtmp[:, :, :], gsel[:, :, :], -1.0, None, ALU.add))
                chain(dve.tensor_tensor(cur, logits[:, :, :].rearrange("p t (g i) -> p (t g) i", g=GROUPS), keep, ALU.mult))
                chain(dve.tensor_tensor(cur, cur, less, ALU.add))
                top_experts(dve, chain, work[:, :, :], E, K, sel[:, :, :], tmp[:, :, :], flag[:, :], best, lower)
                dve.tensor_copy(selb[:, :, :], sel[:, :, :]).then_inc(sel_ready, 1)
                chain(dve.tensor_tensor(W[:, :, :], logits[:, :, :], sel[:, :, :], ALU.mult))
                chain(dve.tensor_reduce(flag[:, :], W[:, :, :], AXX, ALU.add))
                chain(dve.tensor_scalar(flag[:, :], flag[:, :], 1e-9, None, ALU.add))
                chain(dve.reciprocal(flag[:, :], flag[:, :]))
                chain(dve.tensor_tensor(W[:, :, :], W[:, :, :], all_of(flag[:, :]), ALU.mult))
                dve.wait_ge(counted, 1)
                chain(dve.tensor_scalar(tmp[:, :, :], c.psum[LOGITS + 1][:, :].rearrange("p (t e) -> p t e", t=TILES),
                                        float(CAP), None, ALU.is_lt))
                dve.tensor_tensor(W[:, :, :], W[:, :, :], tmp[:, :, :], ALU.mult).then_inc(gates_ready, 1)
            elif kind == "nearest":
                chain(dve.tensor_tensor(work[:, :, :], lg, all_of(nx[:, :]), ALU.add))
                chain(dve.tensor_scalar(work[:, :, :], work[:, :, :], -1.0, None, ALU.mult))
                top_experts(dve, chain, work[:, :, :], E, K, W[:, :, :], tmp[:, :, :], flag[:, :], best, lower)
                dve.tensor_copy(W[:, :, :], W[:, :, :]).then_inc(gates_ready, 1)
            else:
                chain(dve.tensor_tensor(logits[:, :, :], lg, all_of(nx[:, :]), ALU.subtract))
                chain(dve.tensor_copy(work[:, :, :], logits[:, :, :]))
                top_experts(dve, chain, work[:, :, :], E, K, sel[:, :, :], tmp[:, :, :], flag[:, :], best, lower)
                dve.tensor_tensor(work[:, :, :], logits[:, :, :], all_of(best[:, 0, :]), ALU.subtract)\
                   .then_inc(shifted, 1)
                dve.wait_ge(exped, 1)
                chain(dve.tensor_tensor(W[:, :, :], work[:, :, :], sel[:, :, :], ALU.mult))
                chain(dve.tensor_reduce(flag[:, :], W[:, :, :], AXX, ALU.add))
                chain(dve.reciprocal(flag[:, :], flag[:, :]))
                dve.tensor_tensor(W[:, :, :], W[:, :, :], all_of(flag[:, :]), ALU.mult).then_inc(gates_ready, 1)
            if kind == "nearest":
                chain(dve.tensor_tensor(c.x[:, :, :], c.x[:, :, :], c.xn[:, :, :], ALU.add))

            def unit(n, k, u):
                dve.wait_ge(weighed_done if gated else act_done, n + 1)
                at_least(dve, down_done, n - SLOTS + 1)
                cs = slice(k % CHUNKS * CHUNK, (k % CHUNKS + 1) * CHUNK)
                if gated:
                    i = dve.tensor_tensor(hidden[:, k % SLOTS, :], weighed[:, k % SLOTS, :], c.psum[6 + k % 2][:, :], ALU.mult)
                else:
                    i = dve.tensor_tensor(hidden[:, k % SLOTS, :], act_out[:, k % SLOTS, :], gate[:, u, cs], ALU.mult)
                i.then_inc(hidden_done, 1)

            for k in range(OFF):
                unit(k, k, 0)

            def expert(j, u):
                if not gated:
                    dve.wait_ge(g_in[u], 16 * (j + 1))
                for k in range(UNITS):
                    unit(OFF + UNITS * (2 * j + u) + k, k, u)

            expert(0, 0)
            expert(0, 1)
            with dve.Fori(1, E // 2) as j:
                expert(j, 0)
                expert(j, 1)
            for g in range(CHUNKS):
                dve.wait_ge(out_turned, g + 1)
                xs = c.x[:, 4 * g:4 * g + 4, :]
                dve.tensor_tensor(xs, xs, c.psum[4 + g][:, :].rearrange("p (t d) -> p t d", t=4), ALU.add)

        @block.gpsimd
        def _(pool):
            chain = Chain(pool, pool_own)
            if shared:
                chain(pool.memset(onesb[:, :], 1.0))
                chain(pool.memset(upper[:, :], 1.0))
                chain(pool.affine_select(out=upper[:, :], in_=upper[:, :], compare_op=ALU.is_gt, fill=0.0, base=0,
                                         pattern=[[1, P]], channel_multiplier=-1))
            if gated:
                def unit(n, k, gates):
                    pool.wait_ge(act_done, n + 1)
                    at_least(pool, hidden_done, n - SLOTS + 1)
                    if gates is None:
                        i = pool.tensor_scalar(weighed[:, k % SLOTS, :], act_out[:, k % SLOTS, :], 1.0, 1.0,
                                               ALU.mult, ALU.mult)
                    else:
                        i = pool.tensor_tensor(weighed[:, k % SLOTS, :], act_out[:, k % SLOTS, :], gates, ALU.mult)
                    i.then_inc(weighed_done, 1)

                for k in range(OFF):
                    unit(k, k, None)

                def expert(j, u):
                    pool.wait_ge(g_in[u], 16 * (j + 1))
                    for k in range(UNITS):
                        cs = slice(k % CHUNKS * CHUNK, (k % CHUNKS + 1) * CHUNK)
                        unit(OFF + UNITS * (2 * j + u) + k, k, gate[:, u, cs])

                expert(0, 0)
                expert(0, 1)
                with pool.Fori(1, E // 2) as j:
                    expert(j, 0)
                    expert(j, 1)


def ternary(chip, tag):
    nc, c, dram = chip.nc, chip, chip.dram
    EPS, QB, LN2_EPS = 1e-5, 128.0, 1e-3
    ROUND = 1.5 * 2.0 ** 23
    with ExitStack() as ctx:
        def sb(name, shape, dt=F32):
            return ctx.enter_context(nc.sbuf_tensor(f"{tag}_{name}", shape, dt))

        sem = Semaphores(nc, ctx, tag)
        norm = Norm(chip, ctx, tag + "n", sem)
        w, wq, wabs = sb("w", [P, D]), sb("wq", [P, D]), sb("wabs", [P, 1])
        gamma, beta = sb("gamma", [P, D]), sb("beta", [P, D])
        st = sb("st", [P, 8])
        loaded, made, summed, peak, peak_all, clipped, out_ready = (
            sem(n) for n in ("loaded", "made", "summed", "peak", "peak_all", "clipped", "out_ready"))
        dve_own = sem("dve_own")
        block = sem.open_block()

        @block.sync
        def _(sp):
            sp.dma_start(w[:, :], dram[f"{tag}_w"]).then_inc(loaded, 16)
            for name, tile in (("gamma", gamma), ("beta", beta)):
                sp.dma_start(tile[:, :], dram[f"{tag}_{name}"].rearrange("(a n) -> a n", a=1)
                             .to_broadcast([P, D])).then_inc(loaded, 16)

        @block.gpsimd
        def _(pool):
            pool.wait_ge(peak, 1)
            pool.partition_all_reduce(st[:, 4:5], st[:, 3:4], P, RMAX).then_inc(peak_all, 1)

        @block.scalar
        def _(act):
            norm.scalar(act, c.xn, 1)
            norm.scalar(act, c.xn, 2)
            norm.copy_scalar(act, (0, 1, 2, 3))

        @block.tensor
        def _(pe):
            pe.wait_ge(made, 1)
            pe.matmul(c.psum[4][:, 0:1], c.ones[:, :], wabs[:, :], start=True, stop=True).then_inc(summed, 1)
            pe.wait_ge(clipped, 1)
            norm.tensor(pe, c.xn, (0, 1, 2, 3))
            pe.wait_ge(norm.copied, CHUNKS)
            for g in range(CHUNKS):
                for t in range(4):
                    n = 4 * g + t
                    i = pe.matmul(c.psum[4 + g][:, t * P:(t + 1) * P], c.xnT[:, n * P:(n + 1) * P], wq[:, :],
                                  start=True, stop=True)
                i.then_inc(out_ready, 1)

        @block.vector
        def _(dve):
            chain = Chain(dve, dve_own)
            dve.wait_ge(loaded, 48)
            dve.tensor_reduce(wabs[:, :], w[:, :], AXX, ALU.add, apply_absolute_value=True).then_inc(made, 1)
            norm.vector(dve, chain, c.x, c.xn, LN_EPS)
            norm.vector(dve, chain, c.xn, c.xn, LN2_EPS)
            every = [P, TILES, D]
            xn = c.xn[:, :, :]
            chain(dve.tensor_tensor(xn, xn, gamma[:, :].unsqueeze(1).to_broadcast(every), ALU.mult))
            chain(dve.tensor_tensor(xn, xn, beta[:, :].unsqueeze(1).to_broadcast(every), ALU.add))
            dve.tensor_reduce(st[:, 3:4], c.xn[:, :, :].rearrange("p t d -> p (t d)"), AXX, ALU.max,
                              apply_absolute_value=True).then_inc(peak, 1)
            dve.wait_ge(summed, 1)
            chain(dve.tensor_scalar(st[:, 0:1], c.psum[4][:, 0:1], 1.0 / (D * D), None, ALU.mult))
            chain(dve.tensor_scalar(st[:, 1:2], st[:, 0:1], EPS, None, ALU.add))
            chain(dve.reciprocal(st[:, 1:2], st[:, 1:2]))
            chain(dve.tensor_scalar(wq[:, :], w[:, :], st[:, 1:2], None, ALU.mult))
            chain(dve.tensor_scalar(wq[:, :], wq[:, :], 2.0, -2.0, ALU.min, ALU.max))
            chain(dve.tensor_scalar(wq[:, :], wq[:, :], ROUND, None, ALU.add))
            chain(dve.tensor_scalar(wq[:, :], wq[:, :], -ROUND, None, ALU.add))
            chain(dve.tensor_scalar(wq[:, :], wq[:, :], 1.0, -1.0, ALU.min, ALU.max))
            dve.wait_ge(peak_all, 1)
            chain(dve.reciprocal(st[:, 5:6], st[:, 4:5]))
            chain(dve.tensor_tensor(st[:, 6:7], st[:, 4:5], st[:, 0:1], ALU.mult))
            chain(dve.tensor_scalar(st[:, 6:7], st[:, 6:7], 1.0 / QB, None, ALU.mult))
            chain(dve.tensor_scalar(xn, xn, QB, st[:, 5:6], ALU.mult, ALU.mult))
            dve.tensor_scalar(xn, xn, QB - EPS, EPS - QB, ALU.min, ALU.max).then_inc(clipped, 1)
            norm.copy_vector(dve, (0, 1, 2, 3))
            for g in range(CHUNKS):
                dve.wait_ge(out_ready, g + 1)
                xs = c.x[:, 4 * g:4 * g + 4, :]
                dve.scalar_tensor_tensor(xs, c.psum[4 + g][:, :].rearrange("p (t d) -> p t d", t=4), st[:, 6:7],
                                         xs, ALU.mult, ALU.add)


def store_x(chip, out):
    nc, c = chip.nc, chip
    with ExitStack() as ctx:
        sem = Semaphores(nc, ctx, "end")
        stored = sem("stored")
        block = sem.open_block()

        @block.sync
        def _(sp):
            sp.dma_start(out.rearrange("(t p) d -> p t d", p=P), c.x[:, :, :]).then_inc(stored, 16)
            sp.wait_ge(stored, 16)


def build(nc, dram, out, upto=8, first=0):
    with ExitStack() as ctx:
        chip = Chip(nc, ctx, dram)
        start_up(chip)
        sublayers = [
            lambda: attention(chip, "a0"),
            lambda: experts(chip, "f0", "capacity"),
            lambda: attention(chip, "a1", biased=True, full_mask="mask"),
            lambda: experts(chip, "f1", "nearest"),
            lambda: attention(chip, "a2", rope=True, causal=True, key_mask="keep2"),
            lambda: ternary(chip, "f2"),
            lambda: attention(chip, "a3", key_mask="keep3", out_bias=False),
            lambda: experts(chip, "f3", "top"),
        ]
        for sublayer in sublayers[first:upto]:
            sublayer()
        store_x(chip, out)


def rotary():
    theta = (1.0 / np.float32(10000.0) ** (np.arange(0, HD, 2, dtype=np.float32) / np.float32(HD))).astype(np.float32)
    angle = np.arange(S, dtype=np.float32)[None, :] * np.repeat(theta, 2)[:, None]
    sign = np.where(np.arange(HD) % 2 == 0, -1.0, 1.0).astype(np.float32)[:, None]
    cos, sin = np.cos(angle), np.sin(angle) * sign
    return np.tile(cos, (H, 1)).astype(np.float32), np.tile(sin, (H, 1)).astype(np.float32)


def arrange(v):
    swap = np.arange(D) ^ 1
    cos, sin = rotary()
    a = {"x": v["x"].reshape(N, D), "ctxT": v["ctx_1024"].reshape(N, D).T,
         "mask": v["mask_BxSxS2_if1"], "mask_T": v["mask_BxSxS2_if1"].transpose(0, 2, 1),
         "keep2": v["mask_BxS2_if1"], "keep3": v["mask_BxS2_ik0"]}
    for n in range(3):
        for w in "qkvo":
            a[f"a{n}_w{w}"] = v[f"L{n}_xattn_W{w}"].T
        a[f"a{n}_bo"] = v[f"L{n}_xattn_bo"]
    for w in "qkv":
        a[f"a1_b{w}"] = v[f"L1_xattn_b{w}"]
    a["a2_wsq"], a["a2_wsk"] = v["L2_xattn_Wq"][swap].T, v["L2_xattn_Wk"][swap].T
    a["a2_cos"], a["a2_sin"] = cos, sin
    a["a3_wq"], a["a3_wo"] = v["L3_xattn_Wq"].T, v["L3_xattn_Wo"].T
    a["a3_wk"], a["a3_wv"] = v["L3_xattn_Wkv"][:D].T, v["L3_xattn_Wkv"][D:].T
    a["f0_router"] = v["L0_ffn_wg"].T
    for w in ("w1", "w2", "w3", "sw1", "sw2", "sw3"):
        a[f"f0_{w}"] = v[f"L0_ffn_{w}"]
    a["f1_router"], a["f1_scale"] = v["L1_ffn_centroids"].T, v["L1_ffn_scale"]
    a["f1_up"], a["f1_down"] = v["L1_ffn_up_w"], v["L1_ffn_down_w"]
    a["f2_w"], a["f2_gamma"], a["f2_beta"] = v["L2_ffn_weight"], v["L2_ffn_ln_gamma"], v["L2_ffn_ln_beta"]
    a["f3_router"], a["f3_rw"], a["f3_rb"] = v["L3_ffn_keys"].T, v["L3_ffn_rw"].T, v["L3_ffn_rb"]
    a["f3_up"], a["f3_down"] = v["L3_ffn_w1"].transpose(0, 2, 1), v["L3_ffn_w2"].transpose(0, 2, 1)
    a["f3_b1"] = v["L3_ffn_b1"].reshape(16, 4, P).transpose(0, 2, 1)
    a["f3_b2"] = v["L3_ffn_b2"]
    return {k: np.ascontiguousarray(x) for k, x in a.items()}


UPTO = 8


def kernel(**inputs):
    import numpy as _np
    import concourse.bacc as _bacc
    from concourse import mybir as _mybir
    from concourse.bass_utils import run_bass_kernel_spmd as _run

    nc = _bacc.Bacc("TRN2", target_bir_lowering=False, num_devices=1)
    arrays, dram = {}, {}
    for name, a in arrange({k: _np.asarray(x) for k, x in inputs.items()}).items():
        arrays[f"in_{name}"] = a
        dram[name] = nc.dram_tensor(f"in_{name}", a.shape, _mybir.dt.from_np(a.dtype), kind="ExternalInput").ap()
    out = nc.dram_tensor("out_x", (N, D), _mybir.dt.float32, kind="ExternalOutput").ap()
    build(nc, dram, out, UPTO)
    r = _run(nc, [arrays], core_ids=[0])
    return r.results[0]["out_x"].reshape(B, S, D)
```

```python
from contextlib import ExitStack

import numpy as np

import concourse.bass as bass
from concourse import mybir

F32 = mybir.dt.float32
BF16 = mybir.dt.bfloat16
F32R = mybir.dt.float32r
I32 = mybir.dt.int32
ALU = mybir.AluOpType
ACT = mybir.ActivationFunctionType
AXX = mybir.AxisListType.X
RMAX = bass.bass_isa.ReduceOp.max

B, S, D, H = 8, 256, 128, 16
HD = D // H
N = B * S
P = 128
TILES = N // P
CHUNK = 512
CHUNKS = N // CHUNK
PAIRS = H // 2
PARTS = 3
BLOCKS = 6
STACK = BLOCKS * HD
EXTRA = 2 * STACK
MROWS = P - EXTRA
VW = 32
LN_EPS = 1e-5
NEG = -1e30
MASKED = -1e9
LAG = 4

Q_BLOCKS = [(0, 3, 0, 0), (3, 2, 1, 0), (5, 1, 2, 0)]
K_BLOCKS = [(0, 3, 0, 1), (3, 2, 0, 1), (5, 1, 0, 0)]


def at_least(eng, sem, n):
    if not isinstance(n, int) or n > 0:
        eng.wait_ge(sem, n)


def apart(eng, n, passed):
    if not isinstance(n, int):
        eng.sem_inc(passed, 1)


class Chain:

    def __init__(self, eng, sem, base=0, passed=None):
        self.eng, self.sem, self.base, self.n, self.passed = eng, sem, base, 0, passed

    def __call__(self, ins):
        ins.then_inc(self.sem, 1)
        self.n += 1
        self.eng.wait_ge(self.sem, self.base + self.n)
        apart(self.eng, self.base, self.passed)

    def rebase(self, base):
        self.base, self.n = base, 0


class Semaphores:

    def __init__(self, nc, ctx, tag):
        self.nc, self.ctx, self.tag, self.numbers = nc, ctx, tag, []

    def __call__(self, name):
        s = self.ctx.enter_context(self.nc.semaphore(f"{self.tag}_{name}"))
        self.numbers.append(s.num)
        return s

    def open_block(self):
        self.ctx.callback(self.clear)
        return self.ctx.enter_context(self.nc.Block())

    def clear(self):
        numbers, start = sorted(self.numbers), 0
        for n in range(1, len(numbers) + 1):
            if n == len(numbers) or numbers[n] != numbers[n - 1] + 1:
                self.nc.gpsimd.sem_clear(range(numbers[start], numbers[n - 1] + 1))
                start = n
        self.nc.all_engine_barrier()


class Chip:

    def __init__(self, nc, ctx, dram):
        self.nc, self.dram = nc, dram

        def sb(name, shape, dt=F32):
            return ctx.enter_context(nc.sbuf_tensor(name, shape, dt))

        self.x = sb("x", [P, TILES, D])
        self.xn = sb("xn", [P, TILES, D])
        self.xnT = sb("xnT", [P, N])
        self.ctxT = sb("ctxT", [P, N])
        self.ident = sb("ident", [P, P])
        self.identb = sb("identb", [P, P], BF16)
        self.ones = sb("ones", [P, P])
        self.zrow = sb("zrow", [1, CHUNK], BF16)
        self.rev = sb("rev", [P, 32])
        self.own_rows = sb("own_rows", [P, PAIRS], BF16)
        self.qs = sb("qs", [P, 2, PAIRS, S], BF16)
        self.ks = sb("ks", [P, 2, H, S], BF16)
        self.vaug = sb("vaug", [P, 2, 2, H, VW])
        self.psum = [ctx.enter_context(nc.psum_tensor(f"bank{i}", [P, CHUNK], F32)) for i in range(8)]


def start_up(chip):
    nc, c = chip.nc, chip
    with ExitStack() as ctx:
        sem = Semaphores(nc, ctx, "start")
        loaded, filled, cleared = sem("x_loaded"), sem("filled"), sem("cleared")
        ROWS_MADE = 1 + PARTS
        block = sem.open_block()

        @block.sync
        def _(sp):
            sp.dma_start(c.x[:, :, :], c.dram["x"].rearrange("(t p) d -> p t d", p=P)).then_inc(loaded, 16)
            sp.dma_start(c.ctxT[:, :], c.dram["ctxT"]).then_inc(loaded, 16)
            sp.wait_ge(loaded, 32)

        @block.vector
        def _(dve):
            dve.memset(c.vaug[:, :, :, :, :], 0.0).then_inc(cleared, 1)
            dve.memset(c.ks[0:EXTRA, :, :, :].bitcast(F32), 0.0)
            dve.memset(c.qs[EXTRA:P, :, :, :], 1.0)
            dve.wait_ge(cleared, 1)
            dve.memset(c.vaug[:, :, :, :, HD:HD + 1], 1.0)

        @block.scalar
        def _(act):
            act.wait_ge(filled, ROWS_MADE)
            for u in range(2):
                for half in range(2):
                    act.activation(c.ks[EXTRA:P, u, 8 * half:8 * half + 8, :],
                                   c.own_rows[EXTRA:P, :].unsqueeze(2).to_broadcast([MROWS, PAIRS, S]), ACT.Copy)

        @block.gpsimd
        def _(pool):
            done = Chain(pool, filled)
            done(pool.memset(c.own_rows[:, :], 0.0))
            for part in range(PARTS):
                done(pool.affine_select(out=c.own_rows[:, :], in_=c.own_rows[:, :], compare_op=ALU.not_equal,
                                        fill=1.0, base=-(EXTRA + 1 + 8 * part), pattern=[[-1, PAIRS]],
                                        channel_multiplier=1))
            assert done.n == ROWS_MADE
            done(pool.memset(c.ones[:, :], 1.0))
            done(pool.memset(c.zrow[:, :], 0.0))
            done(pool.iota(c.rev[:, :], [[-1, 32]], base=32, channel_multiplier=0,
                           allow_small_or_imprecise_dtypes=True))
            for m in (c.ident, c.identb):
                done(pool.memset(m[:, :], 0.0))
                done(pool.affine_select(out=m[:, :], in_=m[:, :], compare_op=ALU.not_equal, fill=1.0,
                                        base=0, pattern=[[-1, P]], channel_multiplier=1))


class Norm:

    def __init__(self, chip, ctx, tag, sem):
        nc, self.c = chip.nc, chip
        self.centred, self.squared, self.summed = sem("norm_centred"), sem("norm_squared"), sem("norm_summed")
        self.rooted, self.normed = sem("norm_rooted"), sem("norm_normed")
        self.turned, self.copied = sem("norm_turned"), sem("norm_copied")
        self.sq = ctx.enter_context(nc.sbuf_tensor(f"{tag}_sq", [P, TILES, D], F32))
        self.st = ctx.enter_context(nc.sbuf_tensor(f"{tag}_st", [P, 4, TILES], F32))
        self.eps = ctx.enter_context(nc.sbuf_tensor(f"{tag}_eps", [P, 2], F32))
        self.rounds = 0

    def each(self, n):
        return self.st[:, n, :].unsqueeze(2).to_broadcast([P, TILES, D])

    def vector(self, dve, chain, src, dst, eps, centre=True):
        self.rounds += 1
        r = self.rounds
        x, y, st = src[:, :, :], dst[:, :, :], self.st
        chain(dve.memset(self.eps[:, 0:1], eps))
        if centre:
            chain(dve.tensor_reduce(st[:, 0, :], x, AXX, ALU.add))
            chain(dve.tensor_scalar(st[:, 1, :], st[:, 0, :], 1.0 / D, None, ALU.mult))
            dve.tensor_tensor(y, x, self.each(1), ALU.subtract).then_inc(self.centred, 1)
        else:
            dve.memset(self.eps[:, 1:2], 0.0).then_inc(self.centred, 1)
        dve.wait_ge(self.squared, r)
        dve.tensor_reduce(st[:, 2, :], self.sq[:, :, :], AXX, ALU.add).then_inc(self.summed, 1)
        dve.wait_ge(self.rooted, r)
        chain(dve.reciprocal(st[:, 3, :], st[:, 2, :]))
        dve.tensor_tensor(y, y if centre else x, self.each(3), ALU.mult).then_inc(self.normed, 1)
        dve.wait_ge(self.normed, r)

    def scalar(self, act, src, r):
        act.wait_ge(self.centred, r)
        act.activation(self.sq[:, :, :], src[:, :, :], ACT.Square).then_inc(self.squared, 1)
        act.wait_ge(self.summed, r)
        act.activation(self.st[:, 2, :], self.st[:, 2, :], ACT.Sqrt, scale=1.0 / D,
                       bias=self.eps[:, 0:1]).then_inc(self.rooted, 1)

    def tensor(self, pe, src, banks):
        for g in range(CHUNKS):
            for t in range(4):
                i = pe.transpose(self.c.psum[banks[g]][:, t * P:(t + 1) * P], src[:, 4 * g + t, :],
                                 self.c.ident[:, :])
            i.then_inc(self.turned, 1)

    def copy_scalar(self, act, banks, n=2):
        for g in range(n):
            act.wait_ge(self.turned, g + 1)
            act.activation(self.c.xnT[:, g * CHUNK:(g + 1) * CHUNK], self.c.psum[banks[g]][:, :],
                           ACT.Copy).then_inc(self.copied, 1)

    def copy_vector(self, dve, banks, n=2):
        for g in range(n, CHUNKS):
            dve.wait_ge(self.turned, g + 1)
            dve.tensor_copy(self.c.xnT[:, g * CHUNK:(g + 1) * CHUNK],
                            self.c.psum[banks[g]][:, :]).then_inc(self.copied, 1)


def attention(chip, tag, biased=False, rope=False, full_mask=None, causal=False, key_mask=None,
              out_bias=True):
    nc, c, dram = chip.nc, chip, chip.dram
    SCALE = float(HD) ** -0.5
    masked = causal or full_mask is not None
    with ExitStack() as ctx:
        def sb(name, shape, dt=F32):
            return ctx.enter_context(nc.sbuf_tensor(f"{tag}_{name}", shape, dt))

        sem = Semaphores(nc, ctx, tag)
        norm = Norm(chip, ctx, tag + "n", sem)
        wq, wk, wv, wo = (sb(n, [P, P]) for n in ("wq", "wk", "wv", "wo"))
        wsq, wsk = (sb(n, [P, P]) for n in ("wsq", "wsk")) if rope else (None, None)
        cos, sin = (sb(n, [P, S]) for n in ("cos", "sin")) if rope else (None, None)
        bqk = sb("bqk", [P, 2]) if biased else None
        bv = sb("bv", [P, D]) if biased else None
        bo = sb("bo", [1, D]) if out_bias else None
        values = sb("values", [P, TILES, D])
        qk = sb("qk", [P, 2, S])
        qks = sb("qks", [P, 2, S]) if rope else None
        rest = sb("rest", [P, 2, S])
        parts = sb("parts", [P, PARTS, 2, S], BF16)
        nmax = sb("nmax", [P, 2, 2, PAIRS])
        nrest = sb("nrest", [P, 2, PAIRS])
        nparts = sb("nparts", [P, 2, 2, MROWS], BF16)
        probs = sb("probs", [P, 4, 2 * S])
        pv = sb("pv", [P, 2, CHUNK])
        recip = sb("recip", [P, 2, 2, 4])
        o = sb("o", [P, 2, D])
        oT = sb("oT", [P, S])
        mask_shape = [P, P] if causal else [P, 2, 2, S]
        maskq = sb("maskq", mask_shape, BF16) if masked else None
        maskk = sb("maskk", mask_shape, BF16) if masked else None
        rawq = sb("rawq", [P, 2, S], I32) if full_mask else None
        rawk = sb("rawk", [P, 2, S], I32) if full_mask else None
        km = sb("km", [B, S], I32) if key_mask else None
        kmb = sb("kmb", [B, S], BF16) if key_mask else None

        def scratch(name, shape, dt):
            return nc.dram_tensor(f"{tag}_{name}", shape, dt, kind="Internal").ap()

        q_dram, k_dram = (scratch(n, (2, P, BLOCKS, S), BF16) for n in ("q_dram", "k_dram"))
        m_dram = scratch("m_dram", (B, S), BF16) if key_mask else None

        weights_in = sem("weights_in")
        stack_in = [[sem(f"stack_in{u}{half}") for half in range(2)] for u in range(2)]
        unused_made = sem("unused_made")
        split_out = sem("split_out")
        maskq_in, maskk_in, maskq_made, maskk_made = (sem(n) for n in ("mq_in", "mk_in", "mq_made", "mk_made"))
        keymask_in, keymask_made, keymask_out = (sem(n) for n in ("km_in", "km_made", "km_out"))
        qk_ready, qk_read, sw_ready, sw_read = (sem(n) for n in ("qk_ready", "qk_read", "sw_ready", "sw_read"))
        v_ready, v_copied, v_taken = sem("v_ready"), sem("v_copied"), sem("v_taken")
        split_done = sem("split_done")
        max_ready, max_read = sem("max_ready"), sem("max_read")
        nsplit_done = sem("nsplit_done")
        mT_ready, mT_read = sem("mT_ready"), sem("mT_read")
        score_ready, exp_done = sem("score_ready"), sem("exp_done")
        pv_ready, pv_read = sem("pv_ready"), sem("pv_read")
        heads_turned, recip_done, heads_read = sem("heads_turned"), sem("recip_done"), sem("heads_read")
        o_turned, oT_read = sem("o_turned"), sem("oT_read")
        out_ready, out_read = sem("out_ready"), sem("out_read")
        dve_own, pool_own = sem("dve_own"), sem("pool_own")
        sp_passed, pool_passed = sem("sp_passed"), sem("pool_passed")

        CAUSAL_BLOCKS = ((0, 0), (0, 1), (1, 1))
        n_exp = (len(CAUSAL_BLOCKS) if causal else 4) * P
        MAXB, SCB, PVB, AUX, TAIL = (0, 1), (2, 3), (4, 5), 6, 7
        auxb = c.psum[AUX][:, :].bitcast(BF16)
        weight_names = [("wq", wq), ("wk", wk), ("wv", wv), ("wo", wo)]
        n_stack = 3 + (1 if key_mask else 0)
        rows = EXTRA + (1 if key_mask else 0)

        n_weights = len(weight_names) + 4 * rope + 3 * biased + out_bias

        block = sem.open_block()

        @block.sync
        def _(sp):
            for name, tile in weight_names:
                sp.dma_start(tile[:, :], dram[f"{tag}_{name}"]).then_inc(weights_in, 16)
            if rope:
                for name, tile in (("wsq", wsq), ("wsk", wsk), ("cos", cos), ("sin", sin)):
                    sp.dma_start(tile[:, :], dram[f"{tag}_{name}"]).then_inc(weights_in, 16)
            if biased:
                for n, name in enumerate(("bq", "bk")):
                    sp.dma_start(bqk[:, n:n + 1], dram[f"{tag}_{name}"].rearrange("(p a) -> p a", a=1)).then_inc(weights_in, 16)
                sp.dma_start(bv[:, :], dram[f"{tag}_bv"].rearrange("(a n) -> a n", a=1).to_broadcast([P, D])).then_inc(weights_in, 16)
            if out_bias:
                sp.dma_start(bo[:, :], dram[f"{tag}_bo"].rearrange("(a n) -> a n", a=1)).then_inc(weights_in, 16)
            if key_mask:
                sp.dma_start(km[:, :], dram[key_mask]).then_inc(keymask_in, 16)
                sp.wait_ge(keymask_made, 1)
                sp.dma_start(m_dram, kmb[:, :]).then_inc(keymask_out, 16)
                sp.wait_ge(keymask_out, 16)

            def load_maskq(b):
                at_least(sp, maskq_made, b)
                apart(sp, b, sp_passed)
                sp.dma_start(rawq[:, :, :], dram[full_mask][bass.ds(b, 1), :, :]
                             .rearrange("a (t p) k -> p (a t) k", p=P)).then_inc(maskq_in, 16)

            def load_maskk(b):
                at_least(sp, maskk_made, b)
                apart(sp, b, sp_passed)
                sp.dma_start(rawk[:, :, :], dram[full_mask + "_T"][bass.ds(b, 1), :, :]
                             .rearrange("a (t p) q -> p (a t) q", p=P)).then_inc(maskk_in, 16)

            def write_parts(j, u):
                b = 2 * j + u
                if not (isinstance(j, int) and j == 0):
                    for half in range(2):
                        sp.wait_ge(stack_in[u][half], 16 * n_stack * j)
                        apart(sp, j, sp_passed)
                sp.wait_ge(split_done, b + 1)
                for n, (where, blocks) in enumerate(((q_dram, Q_BLOCKS), (k_dram, K_BLOCKS))):
                    for first, count, part, step in blocks:
                        if step:
                            src = parts[:, part:part + count, n, :]
                        else:
                            src = parts[:, part:part + 1, n, :].to_broadcast([P, count, S])
                        sp.dma_start(where[u, :, first:first + count, :], src).then_inc(split_out, 16)
                sp.wait_ge(split_out, 96 * (b + 1))
                apart(sp, b, sp_passed)

            def load_stacks(j, u):
                b = 2 * j + u
                for half in range(2):
                    at_least(sp, score_ready, H * (b - 2) + 8 * (half + 1))
                    apart(sp, b, sp_passed)
                    pairs = slice(4 * half, 4 * half + 4)
                    src = q_dram[u].rearrange("(g h d) c t -> (h d c) g t", g=PAIRS, h=2)
                    sp.dma_start(c.qs[0:EXTRA, u, pairs, :], src[:, pairs, :]).then_inc(stack_in[u][half], 16)
                    for par in range(2):
                        src = k_dram[u].rearrange("(g h d) c t -> h (d c) g t", g=PAIRS, h=2)[par]
                        sp.dma_start(c.ks[STACK * par:STACK * (par + 1), u, 8 * half + par:8 * half + 8:2, :],
                                     src[:, pairs, :]).then_inc(stack_in[u][half], 16)
                    if key_mask:
                        sp.dma_start(c.ks[EXTRA:EXTRA + 1, u, 8 * half:8 * half + 8, :],
                                     m_dram[bass.ds(b, 1), :].unsqueeze(1).to_broadcast([1, PAIRS, S]))\
                          .then_inc(stack_in[u][half], 16)

            def step(j, u, last=False):
                b = 2 * j + u
                if full_mask and not last:
                    load_maskq(b + 2)
                if full_mask and not (last and u == 1):
                    load_maskk(b + 1)
                if not last:
                    write_parts(j + 1, u)
                    load_stacks(j + 1, u)

            if full_mask:
                load_maskq(0)
                load_maskk(0)
                load_maskq(1)
            for u in range(2):
                write_parts(0, u)
                load_stacks(0, u)
            step(0, 0)
            step(0, 1)
            with sp.Fori(1, B // 2 - 1) as j:
                step(j, 0)
                step(j, 1)
            step(B // 2 - 1, 0, True)
            step(B // 2 - 1, 1, True)

        @block.tensor
        def _(pe):
            pe.wait_ge(weights_in, 16 * n_weights)
            for g in range(CHUNKS):
                for t in range(4):
                    token = (4 * g + t) * P
                    i = pe.matmul(c.psum[4 + g][:, t * D:(t + 1) * D], c.ctxT[:, token:token + P], wv[:, :],
                                  start=True, stop=True)
                i.then_inc(v_ready, 1)
            pe.wait_ge(norm.normed, 1)
            norm.tensor(pe, c.xn, (0, 1, 2, 3))
            pe.wait_ge(norm.copied, CHUNKS)
            pe.wait_ge(v_copied, CHUNKS)

            def project_qk(j, u, a, b_, ready):
                tokens = bass.ds((2 * j + u) * S, S)
                pe.matmul(c.psum[AUX][:, 0:S], a[:, :], c.xnT[:, tokens], start=True, stop=True)
                pe.matmul(c.psum[AUX][:, S:2 * S], b_[:, :], c.ctxT[:, tokens], start=True, stop=True).then_inc(ready, 1)

            def max_scores(b, u, h):
                bank = c.psum[MAXB[h % 2]]
                q, k = c.qs[0:rows, u, h // 2, :], c.ks[0:rows, u, h, :]
                at_least(pe, max_read, H * b + h - 1)
                if causal:
                    if h < 2:
                        pe.wait_ge(unused_made, 1)
                    for qt, kt in ((1, 0), (0, 0), (1, 1)):
                        dst = bank[:, qt * S + kt * P:qt * S + (kt + 1) * P]
                        if qt == kt:
                            pe.matmul(dst, c.identb[:, :], maskq[:, :], start=True, stop=False)
                        i = pe.matmul(dst, q[:, qt * P:(qt + 1) * P], k[:, kt * P:(kt + 1) * P], start=qt != kt,
                                      stop=True)
                else:
                    if full_mask:
                        pe.wait_ge(maskq_made, b + 1)
                    for t in range(2):
                        dst = bank[:, t * S:(t + 1) * S]
                        if full_mask:
                            pe.matmul(dst, c.identb[:, :], maskq[:, u, t, :], start=True, stop=False)
                        i = pe.matmul(dst, q[:, t * P:(t + 1) * P], k, start=not full_mask, stop=True)
                i.then_inc(max_ready, 1)

            def turn_max(b, half):
                pe.wait_ge(nsplit_done, 2 * b + half + 1)
                for t in range(2):
                    i = pe.transpose(auxb[0:MROWS, t * P:(t + 1) * P], nparts[:, half, t, :], c.identb[:, :])
                i.then_inc(mT_ready, 1)

            def scores(b, u, h):
                bank = c.psum[SCB[h % 2]]
                at_least(pe, exp_done, H * b + h - 1)
                if h % PAIRS == 0:
                    pe.wait_ge(mT_read, 2 * b + h // PAIRS + 1)
                q, k = c.qs[:, u, h // 2, :], c.ks[:, u, h, :]
                if causal:
                    for n, (kt, qt) in enumerate(CAUSAL_BLOCKS):
                        dst = bank[:, n * P:(n + 1) * P]
                        if qt == kt:
                            pe.matmul(dst, c.identb[:, :], maskk[:, :], start=True, stop=False)
                        i = pe.matmul(dst, k[:, kt * P:(kt + 1) * P], q[:, qt * P:(qt + 1) * P], start=qt != kt,
                                      stop=True)
                else:
                    if full_mask:
                        pe.wait_ge(maskk_made, b + 1)
                    for t in range(2):
                        dst = bank[:, t * S:(t + 1) * S]
                        if full_mask:
                            pe.matmul(dst, c.identb[:, :], maskk[:, u, t, :], start=True, stop=False)
                        i = pe.matmul(dst, k[:, t * P:(t + 1) * P], q, start=not full_mask, stop=True)
                i.then_inc(score_ready, 1)

            def weigh(b, u, h):
                if h % 8 == 0:
                    at_least(pe, pv_read, 2 * b + h // 8 - 1)
                if h == 0:
                    pe.wait_ge(v_taken, b + 1)
                pe.wait_ge(exp_done, H * b + h + 1)
                j = h % 4
                out = c.psum[PVB[h // 8]][32 * j:32 * j + 32, (h // 4 % 2) * S:(h // 4 % 2 + 1) * S]
                if causal:
                    for n, (kt, qt) in enumerate(CAUSAL_BLOCKS):
                        i = pe.matmul(out[:, qt * P:(qt + 1) * P], c.vaug[:, u, kt, h, :],
                                      probs[:, h % 4, n * P:(n + 1) * P], start=(kt == 0), stop=(kt == qt))
                else:
                    for t in range(2):
                        i = pe.matmul(out, c.vaug[:, u, t, h, :], probs[:, h % 4, t * S:(t + 1) * S], start=(t == 0),
                                      stop=(t == 1))
                i.then_inc(pv_ready, 1)

            def turn_heads(b, half):
                pe.wait_ge(pv_read, 2 * b + half + 1)
                if half:
                    pe.wait_ge(heads_read, 2 * b + 1)
                else:
                    at_least(pe, out_read, b)
                for q in range(4):
                    i = pe.transpose(c.psum[TAIL][:, q * P:(q + 1) * P], pv[:, half, q * P:(q + 1) * P], c.ident[:, :])
                i.then_inc(heads_turned, 1)

            def turn_o(b):
                pe.wait_ge(heads_read, 2 * b + 2)
                for t in range(2):
                    i = pe.transpose(c.psum[TAIL][:, t * P:(t + 1) * P], o[:, t, :], c.ident[:, :])
                i.then_inc(o_turned, 1)

            def project_out(b):
                pe.wait_ge(oT_read, b + 1)
                for t in range(2):
                    dst = c.psum[TAIL][:, t * P:(t + 1) * P]
                    i = pe.matmul(dst, oT[:, t * P:(t + 1) * P], wo[:, :], start=True, stop=not out_bias)
                    if out_bias:
                        i = pe.matmul(dst, c.ones[0:1, :], bo[:, :], start=False, stop=True)
                i.then_inc(out_ready, 1)

            def step(j, u, last=False):
                b = 2 * j + u
                first = isinstance(b, int) and b == 0
                ends = last and u == 1
                for h in range(H):
                    scores(b, u, h)
                    if h < LAG:
                        max_scores(b, u, H - LAG + h)
                    elif not ends:
                        if h % 8 == LAG:
                            pe.wait_ge(stack_in[1 - u][h // 8], 16 * n_stack * (j + 1 + u))
                        max_scores(b + 1, 1 - u, h - LAG)
                    if h > 0:
                        weigh(b, u, h - 1)
                    elif not first:
                        weigh(b - 1, 1 - u, H - 1)
                    if h == 1 and not last:
                        project_qk(j + 1, u, wq, wk, qk_ready)
                    if h == 2 and not first:
                        turn_heads(b - 1, 1)
                    if h == 3 and rope and not last:
                        pe.wait_ge(qk_read, b + 3)
                        project_qk(j + 1, u, wsq, wsk, sw_ready)
                    if h == 4 and not first:
                        turn_o(b - 1)
                    if h == 6:
                        if not last:
                            pe.wait_ge(sw_read if rope else qk_read, b + 3)
                        turn_max(b, 1)
                    if h == 7 and not first:
                        project_out(b - 1)
                    if h == 10:
                        turn_heads(b, 0)
                    if h == 14 and not ends:
                        pe.wait_ge(mT_read, 2 * b + 2)
                        turn_max(b + 1, 0)

            for u in range(2):
                at_least(pe, qk_read, u)
                if rope:
                    at_least(pe, sw_read, u)
                project_qk(0, u, wq, wk, qk_ready)
                if rope:
                    pe.wait_ge(qk_read, u + 1)
                    project_qk(0, u, wsq, wsk, sw_ready)
            pe.wait_ge(qk_read, 2)
            if rope:
                pe.wait_ge(sw_read, 2)
            for h in range(H - LAG):
                if h % 8 == 0:
                    pe.wait_ge(stack_in[0][h // 8], 16 * n_stack)
                max_scores(0, 0, h)
            turn_max(0, 0)
            step(0, 0)
            step(0, 1)
            with pe.Fori(1, B // 2 - 1) as j:
                step(j, 0)
                step(j, 1)
            step(B // 2 - 1, 0, True)
            step(B // 2 - 1, 1, True)
            weigh(B - 1, 1, H - 1)
            turn_heads(B - 1, 1)
            turn_o(B - 1)
            project_out(B - 1)

        @block.scalar
        def _(act):
            for g in range(CHUNKS):
                act.wait_ge(v_ready, g + 1)
                act.activation(values[:, 4 * g:4 * g + 4, :], c.psum[4 + g][:, :].rearrange("p (t d) -> p t d", t=4),
                               ACT.Copy).then_inc(v_copied, 1)
            norm.scalar(act, c.xn, 1)
            norm.copy_scalar(act, (0, 1, 2, 3))

            def take_qk(b, dst, ready, read, bias):
                act.wait_ge(ready, b + 1)
                at_least(act, split_done, b)
                if bias:
                    act.wait_ge(weights_in, 16 * n_weights)
                    act.activation(dst[:, 0, :], c.psum[AUX][:, 0:S], ACT.Identity, bias=bqk[:, 0:1])
                    act.activation(dst[:, 1, :], c.psum[AUX][:, S:2 * S], ACT.Identity,
                                   bias=bqk[:, 1:2]).then_inc(read, 1)
                else:
                    act.activation(dst[:, :, :], c.psum[AUX][:, :], ACT.Copy).then_inc(read, 1)

            def take_max(b, u, half):
                act.wait_ge(mT_ready, 2 * b + half + 1)
                act.activation(c.qs[EXTRA:P, u, 4 * half:4 * half + 4, :],
                               auxb[0:MROWS, 0:S].unsqueeze(1).to_broadcast([MROWS, 4, S]), ACT.Copy).then_inc(mT_read, 1)

            def take_pv(b, half):
                act.wait_ge(pv_ready, H * b + 8 * (half + 1))
                at_least(act, heads_turned, 2 * (b - 1) + half + 1)
                act.activation(pv[:, half, :], c.psum[PVB[half]][:, :], ACT.Copy).then_inc(pv_read, 1)

            def step(j, u, last=False):
                b = 2 * j + u
                first = isinstance(b, int) and b == 0
                ends = last and u == 1
                for h in range(H):
                    act.wait_ge(score_ready, H * b + h + 1)
                    at_least(act, pv_ready, H * b + h - 3)
                    act.activation(probs[:, h % 4, 0:n_exp], c.psum[SCB[h % 2]][:, 0:n_exp], ACT.Exp,
                                   scale=SCALE).then_inc(exp_done, 1)
                    if h == 1 and not first:
                        take_pv(b - 1, 1)
                    if h == 5 and not first:
                        act.wait_ge(o_turned, b)
                        act.activation(oT[:, :], c.psum[TAIL][:, 0:S], ACT.Copy).then_inc(oT_read, 1)
                    if h == 2 and not last:
                        take_qk(b + 2, qk, qk_ready, qk_read, biased)
                    if h == 6:
                        take_max(b, u, 1)
                    if h == 9:
                        take_pv(b, 0)
                    if h == 4 and rope and not last:
                        take_qk(b + 2, qks, sw_ready, sw_read, False)
                    if h == 14 and not ends:
                        take_max(b + 1, 1 - u, 0)

            for u in range(2):
                take_qk(u, qk, qk_ready, qk_read, biased)
                if rope:
                    take_qk(u, qks, sw_ready, sw_read, False)
            take_max(0, 0, 0)
            step(0, 0)
            step(0, 1)
            with act.Fori(1, B // 2 - 1) as j:
                step(j, 0)
                step(j, 1)
            step(B // 2 - 1, 0, True)
            step(B // 2 - 1, 1, True)
            take_pv(B - 1, 1)
            act.wait_ge(o_turned, B)
            act.activation(oT[:, :], c.psum[TAIL][:, 0:S], ACT.Copy).then_inc(oT_read, 1)

        @block.vector
        def _(dve):
            chain = Chain(dve, dve_own)
            if key_mask:
                dve.wait_ge(keymask_in, 16)
                dve.tensor_scalar(kmb[:, :], km[:, :], 0.0, NEG, ALU.is_equal, ALU.mult).then_inc(keymask_made, 1)
            norm.vector(dve, chain, c.x, c.xn, LN_EPS)
            norm.copy_vector(dve, (0, 1, 2, 3))
            if biased:
                dve.wait_ge(weights_in, 16 * n_weights)

            def take_v(b, u):
                at_least(dve, v_copied, CHUNKS if isinstance(b, int) and b == 0 else 0)
                at_least(dve, pv_ready, H * (b - 1))
                dst = c.vaug[:, u, :, :, 0:HD]
                src = values[:, bass.ds(2 * b, 2), :].rearrange("p t (h d) -> p t h d", h=H)
                if biased:
                    i = dve.tensor_tensor(dst, src, bv[:, :].rearrange("p (h d) -> p h d", h=H).unsqueeze(1)
                                          .to_broadcast([P, 2, H, HD]), ALU.add)
                else:
                    i = dve.tensor_copy(dst, src)
                i.then_inc(v_taken, 1)

            def head_max(b, h):
                dve.wait_ge(max_ready, H * b + h + 1)
                if h % 8 == 0:
                    at_least(dve, nsplit_done, 2 * b + h // 8 - 1)
                dve.tensor_reduce(nmax[:, h // 8, :, h % 8], c.psum[MAXB[h % 2]][:, :].rearrange(
                    "p (t k) -> p t k", t=2), AXX, ALU.max, negate=True).then_inc(max_read, 1)

            def take_heads(b, half):
                dve.wait_ge(heads_turned, 2 * b + half + 1)
                t4 = c.psum[TAIL][:, :].rearrange("p (g t h w) -> p g t h w", g=2, t=2, h=4)
                for t in range(2):
                    i = dve.reciprocal(recip[:, t, :, :], t4[:, :, t, :, HD])
                i.then_inc(recip_done, 1)
                dve.wait_ge(recip_done, 2 * b + half + 1)
                at_least(dve, o_turned, b)
                for t in range(2):
                    i = dve.tensor_tensor(
                        o[:, t, 64 * half:64 * half + 64].rearrange("p (g h d) -> p g h d", g=2, h=4),
                        t4[:, :, t, :, 0:HD], recip[:, t, :, :].unsqueeze(3).to_broadcast([P, 2, 4, HD]), ALU.mult)
                i.then_inc(heads_read, 1)

            def add_out(b):
                dve.wait_ge(out_ready, b + 1)
                xs = c.x[:, bass.ds(2 * b, 2), :]
                dve.tensor_tensor(xs, xs, c.psum[TAIL][:, 0:S].rearrange("p (t d) -> p t d", t=2),
                                  ALU.add).then_inc(out_read, 1)

            def make_maskq(b, u):
                dve.wait_ge(maskq_in, 16 * (b + 1))
                at_least(dve, max_ready, H * (b - 1))
                dve.tensor_scalar(maskq[:, u, :, :], rawq[:, :, :], 0.0, MASKED, ALU.is_equal,
                                  ALU.mult).then_inc(maskq_made, 1)

            def make_maskk(b, u):
                dve.wait_ge(maskk_in, 16 * (b + 1))
                at_least(dve, score_ready, H * (b - 1))
                dve.tensor_scalar(maskk[:, u, :, :], rawk[:, :, :], 0.0, MASKED, ALU.is_equal,
                                  ALU.mult).then_inc(maskk_made, 1)

            def step(j, u, last=False):
                b = 2 * j + u
                first = isinstance(b, int) and b == 0
                ends = last and u == 1
                for h in range(H):
                    if h < LAG:
                        head_max(b, H - LAG + h)
                    elif not ends:
                        head_max(b + 1, h - LAG)
                    if h == 2 and not first:
                        take_heads(b - 1, 1)
                    if h == 6 and full_mask and not last:
                        make_maskq(b + 2, u)
                    if h == 8 and not first:
                        add_out(b - 1)
                    if h == 10 and not ends:
                        take_v(b + 1, 1 - u)
                    if h == 11:
                        take_heads(b, 0)
                    if h == 12 and full_mask and not ends:
                        make_maskk(b + 1, 1 - u)

            if full_mask:
                make_maskq(0, 0)
                make_maskk(0, 0)
                make_maskq(1, 1)
            if causal:
                dve.wait_ge(norm.copied, CHUNKS)
                for bank in MAXB:
                    i = dve.memset(c.psum[bank][:, P:S], NEG)
                i.then_inc(unused_made, 1)
            take_v(0, 0)
            for h in range(H - LAG):
                head_max(0, h)
            step(0, 0)
            step(0, 1)
            with dve.Fori(1, B // 2 - 1) as j:
                step(j, 0)
                step(j, 1)
            step(B // 2 - 1, 0, True)
            step(B // 2 - 1, 1, True)
            take_heads(B - 1, 1)
            add_out(B - 1)

        @block.gpsimd
        def _(pool):
            chain = Chain(pool, pool_own, passed=pool_passed)
            chain(pool.memset(nparts[:, :, :, :], 0.0))
            chain(pool.memset(nparts[:, :, :, 0:1], 1.0))
            if causal:
                for table, sign in ((maskq, 1), (maskk, -1)):
                    chain(pool.memset(table[:, :], 0.0))
                    chain(pool.affine_select(out=table[:, :], in_=table[:, :], compare_op=ALU.is_ge, fill=NEG, base=0,
                                             pattern=[[-sign, P]], channel_multiplier=sign))
            if rope:
                pool.wait_ge(weights_in, 16 * n_weights)
            setup = chain.n
            per_step = 8 + (7 if rope else 4)

            def split(src, spare, dsts, last_sem):
                for n, dst in enumerate(dsts):
                    i = pool.tensor_scalar(dst, src, 1.0, 1.0, ALU.mult, ALU.mult)
                    if n == PARTS - 1:
                        i.then_inc(last_sem, 1)
                    else:
                        chain(i)
                        chain(pool.tensor_tensor(spare, src, dst, ALU.subtract))
                        src = spare

            def split_max(b, half):
                pool.wait_ge(max_read, H * b + 8 * (half + 1))
                at_least(pool, mT_ready, 2 * b + half - 1)
                apart(pool, b, pool_passed)
                split(nmax[:, half, :, :], nrest[:, :, :],
                      [nparts[:, half, :, 1 + 8 * n:9 + 8 * n] for n in range(PARTS)], nsplit_done)

            def split_qk(b):
                pool.wait_ge(qk_read, b + 1)
                at_least(pool, split_out, 96 * b)
                apart(pool, b, pool_passed)
                if rope:
                    pool.wait_ge(sw_read, b + 1)
                    both = [P, 2, S]
                    chain(pool.tensor_tensor(qk[:, :, :], qk[:, :, :], cos[:, :].unsqueeze(1).to_broadcast(both), ALU.mult))
                    chain(pool.tensor_tensor(qks[:, :, :], qks[:, :, :], sin[:, :].unsqueeze(1).to_broadcast(both), ALU.mult))
                    chain(pool.tensor_tensor(qk[:, :, :], qk[:, :, :], qks[:, :, :], ALU.add))
                split(qk[:, :, :], rest[:, :, :], [parts[:, n, :, :] for n in range(PARTS)], split_done)

            def step(j, u, last=False):
                b = 2 * j + u
                split_max(b, 1)
                if not last:
                    split_qk(b + 2)
                if not (last and u == 1):
                    split_max(b + 1, 0)

            split_qk(0)
            split_qk(1)
            split_max(0, 0)
            before = chain.n
            step(0, 0)
            step(0, 1)
            assert chain.n == before + 2 * per_step, (chain.n, before, per_step)
            with pool.Fori(1, B // 2 - 1) as j:
                chain.rebase(before + 2 * per_step * j)
                step(j, 0)
                step(j, 1)
            chain.rebase(before + 2 * per_step * (B // 2 - 1))
            step(B // 2 - 1, 0, True)
            step(B // 2 - 1, 1, True)


def top_experts(dve, chain, cur, n, k, sel, tmp, flag, best, lower):
    every = [P, TILES, n]

    def all_of(a):
        return a.unsqueeze(2).to_broadcast(every)

    for i in range(k):
        top = best[:, i, :]
        chain(dve.tensor_reduce(top, cur, AXX, ALU.max))
        chain(dve.tensor_tensor(tmp, cur, all_of(top), ALU.is_equal))
        chain(dve.tensor_tensor(tmp, tmp, lower, ALU.mult))
        chain(dve.tensor_reduce(flag, tmp, AXX, ALU.max))
        chain(dve.tensor_tensor(tmp, tmp, all_of(flag), ALU.is_equal))
        if i == 0:
            chain(dve.tensor_copy(sel, tmp))
        else:
            chain(dve.tensor_tensor(sel, sel, tmp, ALU.add))
        if i < k - 1:
            chain(dve.scalar_tensor_tensor(cur, tmp, NEG, cur, ALU.mult, ALU.add))


def experts(chip, tag, kind):
    nc, c, dram = chip.nc, chip, chip.dram
    shared = kind == "capacity"
    E = {"capacity": 32, "nearest": 8, "top": 16}[kind]
    HB = {"capacity": 1, "nearest": 2, "top": 4}[kind]
    UP = {"capacity": 2, "nearest": 4, "top": 4}[kind]
    gated = kind != "top"
    UNITS = HB * CHUNKS
    K = {"capacity": 4, "nearest": 1, "top": 4}[kind]
    GROUPS = 8
    CAP = int(1.25 * N * 4 / 32)
    ACTF = ACT.Silu if gated else ACT.Gelu
    SLOTS = 4
    AFTER = 1
    BEHIND = 3
    with ExitStack() as ctx:
        def sb(name, shape, dt=F32):
            return ctx.enter_context(nc.sbuf_tensor(f"{tag}_{name}", shape, dt))

        sem = Semaphores(nc, ctx, tag)
        norm = Norm(chip, ctx, tag + "n", sem)
        router = sb("router", [P, E])
        up = sb("up", [P, 2, UP, P])
        down = sb("down", [P, 2, HB, P])
        ups = sb("ups", [P, 2, 2, UP, P], F32R)
        downs = sb("downs", [P, 2, 2, HB, P], F32R)
        xs2 = sb("xs2", [P, 2, N], F32R)
        hiddens = sb("hiddens", [P, SLOTS, 2, CHUNK], F32R)
        gate = sb("gate", [P, 2, N])
        act_out = sb("act_out", [P, SLOTS, CHUNK])
        weighed = sb("weighed", [P, SLOTS, CHUNK]) if gated else None
        hidden = sb("hidden", [P, SLOTS, CHUNK])
        sharedw = sb("sharedw", [P, 3, P]) if shared else None
        shareds = sb("shareds", [P, 2, 3, P], F32R) if shared else None
        logits, work, tmp, sel, W = (sb(n, [P, TILES, E]) for n in ("logits", "work", "tmp", "sel", "W"))
        best = sb("best", [P, 4, TILES])
        flag = sb("flag", [P, TILES])
        gT = sb("gT", [E, N])
        outT = sb("outT", [P, N])
        g_dram = nc.dram_tensor(f"{tag}_gates", (E, N), F32, kind="Internal").ap()
        xr = c.xn
        if shared:
            grp, gwork, gtmp, gsel = (sb(n, [P, TILES, GROUPS]) for n in ("grp", "gwork", "gtmp", "gsel"))
            selb = sb("selb", [P, TILES, E], BF16)
            upper = sb("upper", [P, P], BF16)
            onesb = sb("onesb", [P, P], BF16)
        if kind == "nearest":
            xr = sb("xr", [P, TILES, D])
            scale = sb("scale", [P, D])
            csq, cm2 = sb("csq", [P, E]), sb("cm2", [P, E])
            nx = sb("nx", [P, TILES])
        if kind == "top":
            csq, cm2 = sb("csq", [P, E]), sb("cm2", [P, E])
            rw = sb("rw", [P, E])
            rb = sb("rb", [1, E])
            b1 = sb("b1", [P, 2, HB])
            b2 = sb("b2", [E, D])
            nx = sb("nx", [P, TILES])

        small_in = sem("small_in")
        w_in = [sem("w_in0"), sem("w_in1")]
        g_in = [sem("g_in0"), sem("g_in1")]
        scaled = sem("scaled")
        router_made, logits_ready, shifted, exped = (sem(n) for n in ("router_made", "logits_ready", "shifted", "exped"))
        sel_ready, counted, gates_ready, gates_turned, gates_copied, gates_out = (
            sem(n) for n in ("sel_ready", "counted", "gates_ready", "gates_turned", "gates_copied", "gates_out"))
        up_ready, act_done, weighed_done, hidden_done, down_done = (
            sem(n) for n in ("up_ready", "act_done", "weighed_done", "hidden_done", "down_done"))
        x_high, x_low, h_high, h_low = (sem(n) for n in ("x_high", "x_low", "h_high", "h_low"))
        up_split, down_split, shared_split = (sem(n) for n in ("up_split", "down_split", "shared_split"))
        acc_ready, acc_copied, out_turned = sem("acc_ready"), sem("acc_copied"), sem("out_turned")
        sp_passed = sem("sp_passed")
        dve_own, pool_own, act_own, pe_own = sem("dve_own"), sem("pool_own"), sem("act_own"), sem("pe_own")

        OFF = CHUNKS if shared else 0
        ACC = (0, 1, 2, 3)
        A_BANKS = (4, 5) if gated else (4, 5, 6, 7)
        NA = len(A_BANKS)
        LOGITS = 4
        n_small = {"capacity": 4, "nearest": 2, "top": 4}[kind]
        n_w = {"capacity": 3, "nearest": 2, "top": 3}[kind]

        def take_low(eng, n, k):
            eng.wait_ge(h_high, n + 1)
            eng.tensor_tensor(hiddens[:, k % SLOTS, 1, :], hidden[:, k % SLOTS, :],
                              hiddens[:, k % SLOTS, 0, :].bitcast(F32), ALU.subtract).then_inc(h_low, 1)

        block = sem.open_block()

        @block.sync
        def _(sp):
            sp.dma_start(router[:, :], dram[f"{tag}_router"]).then_inc(small_in, 16)
            if shared:
                for n, name in enumerate(("sw1", "sw3", "sw2")):
                    sp.dma_start(sharedw[:, n, :], dram[f"{tag}_{name}"]).then_inc(small_in, 16)
            if kind == "nearest":
                sp.dma_start(scale[:, :], dram[f"{tag}_scale"].rearrange("(a n) -> a n", a=1)
                             .to_broadcast([P, D])).then_inc(small_in, 16)
            if kind == "top":
                sp.dma_start(rw[:, :], dram[f"{tag}_rw"]).then_inc(small_in, 16)
                sp.dma_start(rb[:, :], dram[f"{tag}_rb"].rearrange("(a n) -> a n", a=1)).then_inc(small_in, 16)
                sp.dma_start(b2[:, :], dram[f"{tag}_b2"]).then_inc(small_in, 16)

            def load(j, u):
                e = 2 * j + u
                at_least(sp, down_split, 2 * (e - 1))
                if kind == "top":
                    apart(sp, e, sp_passed)
                    at_least(sp, act_done, UNITS * (e - 1))
                apart(sp, e, sp_passed)
                one = bass.ds(e, 1)
                if kind == "capacity":
                    for n, name in enumerate(("w1", "w3")):
                        sp.dma_start(up[:, u, n, :], dram[f"{tag}_{name}"][one, :, :].rearrange("e d h -> d (e h)"))\
                          .then_inc(w_in[u], 16)
                    sp.dma_start(down[:, u, 0, :], dram[f"{tag}_w2"][one, :, :].rearrange("e h d -> h (e d)"))\
                      .then_inc(w_in[u], 16)
                else:
                    sp.dma_start(up[:, u, :, :], dram[f"{tag}_up"][one, :, :].rearrange("e d (b h) -> d (e b) h", b=UP))\
                      .then_inc(w_in[u], 16)
                    sp.dma_start(down[:, u, :, :], dram[f"{tag}_down"][one, :, :].rearrange("e (b h) d -> h (e b) d", b=HB))\
                      .then_inc(w_in[u], 16)
                if kind == "top":
                    sp.dma_start(b1[:, u, :], dram[f"{tag}_b1"][one, :, :].rearrange("e p b -> p (e b)"))\
                      .then_inc(w_in[u], 16)

            def load_gate(j, u):
                e = 2 * j + u
                at_least(sp, weighed_done if gated else hidden_done, OFF + UNITS * (e - 1))
                apart(sp, e, sp_passed)
                sp.dma_start(gate[:, u, :], g_dram[bass.ds(e, 1), :].to_broadcast([P, N])).then_inc(g_in[u], 16)

            load(0, 0)
            load(0, 1)
            sp.wait_ge(gates_copied, CHUNKS)
            sp.dma_start(g_dram, gT[:, :]).then_inc(gates_out, 16)
            sp.wait_ge(gates_out, 16)
            load_gate(0, 0)
            load_gate(0, 1)
            with sp.Fori(1, E // 2) as j:
                for u in range(2):
                    load(j, u)
                    load_gate(j, u)

        @block.tensor
        def _(pe):
            pe.wait_ge(*((scaled, 1) if kind == "nearest" else (norm.normed, 1)))
            norm.tensor(pe, xr, (0, 1, 2, 3))
            pe.wait_ge(norm.copied, CHUNKS)
            pe.wait_ge(small_in, 16 * n_small)
            if kind != "capacity":
                pe.wait_ge(router_made, 2)
            for t in range(TILES):
                dst = c.psum[LOGITS][:, t * E:(t + 1) * E]
                lhs = c.xnT[:, t * P:(t + 1) * P]
                if kind == "capacity":
                    i = pe.matmul(dst, lhs, router[:, :], start=True, stop=True)
                else:
                    pe.matmul(dst, lhs, cm2[:, :], start=True, stop=False)
                    if kind == "top":
                        pe.matmul(dst, lhs, rw[:, :], start=False, stop=False)
                        pe.matmul(dst, c.ones[0:1, :], rb[:, :], start=False, stop=False)
                    i = pe.matmul(dst, c.ones[:, :], csq[:, :], start=False, stop=True)
            i.then_inc(logits_ready, 1)
            if shared:
                pe.wait_ge(sel_ready, 1)
                pe.wait_ge(pool_own, 3)
                bank = c.psum[LOGITS + 1]
                pe.matmul(bank[:, :], upper[:, :], selb[:, :, :], start=True, stop=False)
                for t in range(TILES - 1):
                    rest = TILES - 1 - t
                    pe.matmul(bank[:, (t + 1) * E:], onesb[:, :],
                              selb[:, t:t + 1, :].to_broadcast([P, rest, E]), start=False, stop=False)
                i = pe.matmul(bank[:, :], c.zrow[:, 0:P], c.zrow[:, :], start=False, stop=True)
                i.then_inc(counted, 1)
            pe.wait_ge(gates_ready, 1)
            for g in range(CHUNKS):
                for t in range(4):
                    i = pe.transpose(c.psum[g][0:E, t * P:(t + 1) * P], W[:, 4 * g + t, :], c.ident[:, :])
                i.then_inc(gates_turned, 1)
            pe.wait_ge(gates_copied, CHUNKS)
            for g in range(CHUNKS):
                if kind == "top":
                    pe.matmul(c.psum[ACC[g]][:, :], b2[:, :], gT[:, g * CHUNK:(g + 1) * CHUNK], start=True, stop=False)
                else:
                    pe.matmul(c.psum[ACC[g]][:, :], c.zrow[:, 0:P], c.zrow[:, :], start=True, stop=False)

            def product(out, w, x, **flags):
                pe.matmul(out, w(0), x(0), start=flags["start"], stop=False)
                pe.matmul(out, w(0), x(1), start=False, stop=False)
                return pe.matmul(out, w(1), x(0), start=False, stop=flags["stop"])

            def project_up(n, k, ws):
                cs = slice(k % CHUNKS * CHUNK, (k % CHUNKS + 1) * CHUNK)
                at_least(pe, act_done, n - NA + 1)
                i = product(c.psum[A_BANKS[k % NA]][:, :], ws[0], lambda part: xs2[:, part, cs], start=True, stop=True)
                if gated:
                    at_least(pe, hidden_done, n - 1)
                    i = product(c.psum[6 + k % 2][:, :], ws[1], lambda part: xs2[:, part, cs], start=True, stop=True)
                i.then_inc(up_ready, 1)

            def project_down(n, k, w):
                pe.wait_ge(h_low, n + 1)
                product(c.psum[ACC[k % CHUNKS]][:, :], w, lambda part: hiddens[:, k % SLOTS, part, :], start=False,
                        stop=False).then_inc(down_done, 1)

            def up_weights(u, k):
                i = k // CHUNKS

                def block(n):
                    return lambda part: ups[:, u, part, n, :]
                if kind == "capacity":
                    return block(0), block(1)
                if kind == "nearest":
                    return block(2 + i), block(i)
                return (block(i),)

            def down_weights(u, k):
                return lambda part: downs[:, u, part, k // CHUNKS, :]

            def shared_weights(n):
                return lambda part: shareds[:, part, n, :]

            def expert(j, u, first=False):
                e = 2 * j + u
                n0 = OFF + UNITS * e
                pe.wait_ge(up_split, 2 * (e + 1))
                for k in range(UNITS):
                    project_up(n0 + k, k, up_weights(u, k))
                    if k >= BEHIND:
                        if k == BEHIND:
                            pe.wait_ge(down_split, 2 * (e + 1))
                        project_down(n0 + k - BEHIND, k - BEHIND, down_weights(u, k - BEHIND))
                    elif not first:
                        project_down(n0 + k - BEHIND, UNITS + k - BEHIND, down_weights(1 - u, UNITS + k - BEHIND))
                    elif shared:
                        project_down(n0 + k - BEHIND, CHUNKS + k - BEHIND, shared_weights(2))

            pe.wait_ge(x_low, CHUNKS)
            if shared:
                pe.wait_ge(shared_split, 2)
                for k in range(CHUNKS):
                    project_up(k, k, (shared_weights(0), shared_weights(1)))
                    if k >= BEHIND:
                        project_down(k - BEHIND, k - BEHIND, shared_weights(2))
            expert(0, 0, True)
            expert(0, 1)
            with pe.Fori(1, E // 2) as j:
                expert(j, 0)
                expert(j, 1)
            for k in range(UNITS - BEHIND, UNITS):
                project_down(OFF + UNITS * (E - 1) + k, k, down_weights(1, k))
            for g in range(CHUNKS):
                pe.matmul(c.psum[ACC[g]][:, :], c.zrow[:, 0:P], c.zrow[:, :], start=False,
                          stop=True).then_inc(acc_ready, 1)
            for g in range(CHUNKS):
                pe.wait_ge(acc_copied, g + 1)
                for t in range(4):
                    i = pe.transpose(c.psum[4 + g][:, t * P:(t + 1) * P],
                                     outT[:, (4 * g + t) * P:(4 * g + t + 1) * P], c.ident[:, :])
                i.then_inc(out_turned, 1)

        @block.scalar
        def _(act):
            chain = Chain(act, act_own)
            norm.scalar(act, c.xn, 1)
            if kind == "nearest":
                norm.scalar(act, c.xn, 2)
            if kind != "capacity":
                act.wait_ge(small_in, 16 * n_small)
                sign = 1.0 if kind == "nearest" else -1.0
                act.mul(cm2[:, :], router[:, :], -2.0 * sign).then_inc(router_made, 1)
                chain(act.activation(csq[:, :], router[:, :], ACT.Square))
                act.mul(csq[:, :], csq[:, :], sign).then_inc(router_made, 1)
            norm.copy_scalar(act, (0, 1, 2, 3))
            if kind != "nearest":
                act.wait_ge(shifted, 1)
                act.activation(work[:, :, :], work[:, :, :], ACT.Exp).then_inc(exped, 1)
            for g in range(CHUNKS):
                act.wait_ge(gates_turned, g + 1)
                act.activation(gT[:, g * CHUNK:(g + 1) * CHUNK], c.psum[g][0:E, :], ACT.Copy).then_inc(gates_copied, 1)

            act.wait_ge(norm.copied, CHUNKS)
            for g in range(CHUNKS):
                act.activation(xs2[:, 0, g * CHUNK:(g + 1) * CHUNK], c.xnT[:, g * CHUNK:(g + 1) * CHUNK],
                               ACT.Copy).then_inc(x_high, 1)

            def take_high(n, k):
                act.wait_ge(hidden_done, n + 1)
                at_least(act, down_done, n - SLOTS + 1)
                act.activation(hiddens[:, k % SLOTS, 0, :], hidden[:, k % SLOTS, :], ACT.Copy).then_inc(h_high, 1)

            def unit(n, k, bias=0.0):
                act.wait_ge(up_ready, n + 1)
                at_least(act, weighed_done if gated else hidden_done, n - SLOTS + 1)
                act.activation(act_out[:, k % SLOTS, :], c.psum[A_BANKS[k % NA]][:, :], ACTF,
                               bias=bias).then_inc(act_done, 1)

            for k in range(OFF):
                unit(k, k)
                if k >= AFTER:
                    take_high(k - AFTER, k - AFTER)

            def expert(j, u, first=False):
                n0 = OFF + UNITS * (2 * j + u)
                if kind == "top":
                    act.wait_ge(w_in[u], 16 * n_w * (j + 1))
                for k in range(UNITS):
                    bias = 0.0
                    if kind == "top":
                        bias = b1[:, u, k // CHUNKS:k // CHUNKS + 1]
                    unit(n0 + k, k, bias)
                    if not first or shared or k >= AFTER:
                        take_high(n0 + k - AFTER, (k - AFTER) % SLOTS)

            expert(0, 0, True)
            expert(0, 1)
            with act.Fori(1, E // 2) as j:
                expert(j, 0)
                expert(j, 1)
            for k in range(UNITS - AFTER, UNITS):
                take_high(OFF + UNITS * (E - 1) + k, k)
            for g in range(0, CHUNKS):
                act.wait_ge(acc_ready, g + 1)
                act.activation(outT[:, g * CHUNK:(g + 1) * CHUNK], c.psum[ACC[g]][:, :], ACT.Copy).then_inc(acc_copied, 1)

        @block.vector
        def _(dve):
            chain = Chain(dve, dve_own)
            norm.vector(dve, chain, c.x, c.xn, LN_EPS)
            if kind == "nearest":
                norm.vector(dve, chain, c.xn, xr, 1e-6, centre=False)
                dve.wait_ge(small_in, 16 * n_small)
                dve.tensor_tensor(xr[:, :, :], xr[:, :, :], scale[:, :].unsqueeze(1).to_broadcast([P, TILES, D]),
                                  ALU.mult).then_inc(scaled, 1)
                dve.wait_ge(scaled, 1)
            norm.copy_vector(dve, (0, 1, 2, 3))

            def split_weights(j, u, src, dst, done):
                dve.wait_ge(w_in[u], 16 * n_w * (j + 1))
                dve.tensor_copy(dst[:, u, 0, :, :], src[:, u, :, :]).then_inc(done, 1)
                dve.wait_ge(done, 2 * (2 * j + u) + 1)
                dve.tensor_tensor(dst[:, u, 1, :, :], src[:, u, :, :], dst[:, u, 0, :, :].bitcast(F32),
                                  ALU.subtract).then_inc(done, 1)

            if shared:
                dve.wait_ge(small_in, 16 * n_small)
                dve.tensor_copy(shareds[:, 0, :, :], sharedw[:, :, :]).then_inc(shared_split, 1)
                dve.wait_ge(shared_split, 1)
                dve.tensor_tensor(shareds[:, 1, :, :], sharedw[:, :, :], shareds[:, 0, :, :].bitcast(F32),
                                  ALU.subtract).then_inc(shared_split, 1)

            every = [P, TILES, E]

            def all_of(a):
                return a.unsqueeze(2).to_broadcast(every)

            lower = c.rev[:, 0:E].unsqueeze(1).to_broadcast(every)
            lg = c.psum[LOGITS][:, 0:TILES * E].rearrange("p (t e) -> p t e", t=TILES)
            if kind != "capacity":
                chain(dve.tensor_tensor(norm.sq[:, :, :], xr[:, :, :], xr[:, :, :], ALU.mult))
                chain(dve.tensor_reduce(nx[:, :], norm.sq[:, :, :], AXX, ALU.add))
            dve.wait_ge(logits_ready, 1)
            if kind == "capacity":
                chain(dve.tensor_reduce(flag[:, :], lg, AXX, ALU.max))
                dve.tensor_tensor(work[:, :, :], lg, all_of(flag[:, :]), ALU.subtract).then_inc(shifted, 1)
                dve.wait_ge(exped, 1)
                chain(dve.tensor_reduce(flag[:, :], work[:, :, :], AXX, ALU.add))
                chain(dve.reciprocal(flag[:, :], flag[:, :]))
                chain(dve.tensor_tensor(logits[:, :, :], work[:, :, :], all_of(flag[:, :]), ALU.mult))
                chain(dve.tensor_reduce(gwork[:, :, :], logits[:, :, :].rearrange("p t (g i) -> p (t g) i", g=GROUPS),
                                        AXX, ALU.max))
                top_experts(dve, chain, gwork[:, :, :], GROUPS, 4, gsel[:, :, :], gtmp[:, :, :], flag[:, :], best,
                            c.rev[:, 0:GROUPS].unsqueeze(1).to_broadcast([P, TILES, GROUPS]))
                by_group = [P, TILES * GROUPS, E // GROUPS]
                keep = gsel[:, :, :].rearrange("p t g -> p (t g)").unsqueeze(2).to_broadcast(by_group)
                less = gtmp[:, :, :].rearrange("p t g -> p (t g)").unsqueeze(2).to_broadcast(by_group)
                cur = work[:, :, :].rearrange("p t (g i) -> p (t g) i", g=GROUPS)
                chain(dve.tensor_scalar(gtmp[:, :, :], gsel[:, :, :], -1.0, None, ALU.add))
                chain(dve.tensor_tensor(cur, logits[:, :, :].rearrange("p t (g i) -> p (t g) i", g=GROUPS), keep, ALU.mult))
                chain(dve.tensor_tensor(cur, cur, less, ALU.add))
                top_experts(dve, chain, work[:, :, :], E, K, sel[:, :, :], tmp[:, :, :], flag[:, :], best, lower)
                dve.tensor_copy(selb[:, :, :], sel[:, :, :]).then_inc(sel_ready, 1)
                chain(dve.tensor_tensor(W[:, :, :], logits[:, :, :], sel[:, :, :], ALU.mult))
                chain(dve.tensor_reduce(flag[:, :], W[:, :, :], AXX, ALU.add))
                chain(dve.tensor_scalar(flag[:, :], flag[:, :], 1e-9, None, ALU.add))
                chain(dve.reciprocal(flag[:, :], flag[:, :]))
                chain(dve.tensor_tensor(W[:, :, :], W[:, :, :], all_of(flag[:, :]), ALU.mult))
                dve.wait_ge(counted, 1)
                chain(dve.tensor_scalar(tmp[:, :, :], c.psum[LOGITS + 1][:, :].rearrange("p (t e) -> p t e", t=TILES),
                                        float(CAP), None, ALU.is_lt))
                dve.tensor_tensor(W[:, :, :], W[:, :, :], tmp[:, :, :], ALU.mult).then_inc(gates_ready, 1)
            elif kind == "nearest":
                chain(dve.tensor_tensor(work[:, :, :], lg, all_of(nx[:, :]), ALU.add))
                chain(dve.tensor_scalar(work[:, :, :], work[:, :, :], -1.0, None, ALU.mult))
                top_experts(dve, chain, work[:, :, :], E, K, W[:, :, :], tmp[:, :, :], flag[:, :], best, lower)
                dve.tensor_copy(W[:, :, :], W[:, :, :]).then_inc(gates_ready, 1)
            else:
                chain(dve.tensor_tensor(logits[:, :, :], lg, all_of(nx[:, :]), ALU.subtract))
                chain(dve.tensor_copy(work[:, :, :], logits[:, :, :]))
                top_experts(dve, chain, work[:, :, :], E, K, sel[:, :, :], tmp[:, :, :], flag[:, :], best, lower)
                dve.tensor_tensor(work[:, :, :], logits[:, :, :], all_of(best[:, 0, :]), ALU.subtract)\
                   .then_inc(shifted, 1)
                dve.wait_ge(exped, 1)
                chain(dve.tensor_tensor(W[:, :, :], work[:, :, :], sel[:, :, :], ALU.mult))
                chain(dve.tensor_reduce(flag[:, :], W[:, :, :], AXX, ALU.add))
                chain(dve.reciprocal(flag[:, :], flag[:, :]))
                dve.tensor_tensor(W[:, :, :], W[:, :, :], all_of(flag[:, :]), ALU.mult).then_inc(gates_ready, 1)
            if kind == "nearest":
                chain(dve.tensor_tensor(c.x[:, :, :], c.x[:, :, :], c.xn[:, :, :], ALU.add))

            split_weights(0, 0, up, ups, up_split)
            split_weights(0, 0, down, downs, down_split)

            def unit(n, k, u):
                dve.wait_ge(weighed_done if gated else act_done, n + 1)
                at_least(dve, h_low, n - SLOTS + 1)
                cs = slice(k % CHUNKS * CHUNK, (k % CHUNKS + 1) * CHUNK)
                if gated:
                    i = dve.tensor_tensor(hidden[:, k % SLOTS, :], weighed[:, k % SLOTS, :], c.psum[6 + k % 2][:, :], ALU.mult)
                else:
                    i = dve.tensor_tensor(hidden[:, k % SLOTS, :], act_out[:, k % SLOTS, :], gate[:, u, cs], ALU.mult)
                i.then_inc(hidden_done, 1)

            def low(n, k):
                if gated:
                    take_low(dve, n, k)

            for k in range(OFF):
                unit(k, k, 0)
                if k >= AFTER:
                    low(k - AFTER, k - AFTER)

            def expert(j, u, first=False, last=False):
                e = 2 * j + u
                n0 = OFF + UNITS * e
                if not gated:
                    dve.wait_ge(g_in[u], 16 * (j + 1))
                for k in range(UNITS):
                    unit(n0 + k, k, u)
                    if not first or shared or k >= AFTER:
                        low(n0 + k - AFTER, (k - AFTER) % SLOTS)
                    if k == 1 and not last:
                        split_weights(j + u, 1 - u, up, ups, up_split)
                    if k == 3 and not last:
                        at_least(dve, down_done, OFF + UNITS * e)
                        split_weights(j + u, 1 - u, down, downs, down_split)

            expert(0, 0, True)
            expert(0, 1)
            with dve.Fori(1, E // 2 - 1) as j:
                expert(j, 0)
                expert(j, 1)
            expert(E // 2 - 1, 0)
            expert(E // 2 - 1, 1, last=True)
            for k in range(UNITS - AFTER, UNITS):
                low(OFF + UNITS * (E - 1) + k, k)
            for g in range(CHUNKS):
                dve.wait_ge(out_turned, g + 1)
                xs = c.x[:, 4 * g:4 * g + 4, :]
                dve.tensor_tensor(xs, xs, c.psum[4 + g][:, :].rearrange("p (t d) -> p t d", t=4), ALU.add)

        @block.gpsimd
        def _(pool):
            chain = Chain(pool, pool_own)
            if shared:
                chain(pool.memset(onesb[:, :], 1.0))
                chain(pool.memset(upper[:, :], 1.0))
                chain(pool.affine_select(out=upper[:, :], in_=upper[:, :], compare_op=ALU.is_gt, fill=0.0, base=0,
                                         pattern=[[1, P]], channel_multiplier=-1))
            for g in range(CHUNKS):
                cs = slice(g * CHUNK, (g + 1) * CHUNK)
                pool.wait_ge(x_high, g + 1)
                pool.tensor_tensor(xs2[:, 1, cs], c.xnT[:, cs], xs2[:, 0, cs].bitcast(F32), ALU.subtract).then_inc(x_low, 1)
            if not gated:
                def expert(j, u):
                    for k in range(UNITS):
                        take_low(pool, UNITS * (2 * j + u) + k, k)

                expert(0, 0)
                expert(0, 1)
                with pool.Fori(1, E // 2) as j:
                    expert(j, 0)
                    expert(j, 1)
            if gated:
                def unit(n, k, gates):
                    pool.wait_ge(act_done, n + 1)
                    at_least(pool, hidden_done, n - SLOTS + 1)
                    if gates is None:
                        i = pool.tensor_scalar(weighed[:, k % SLOTS, :], act_out[:, k % SLOTS, :], 1.0, 1.0,
                                               ALU.mult, ALU.mult)
                    else:
                        i = pool.tensor_tensor(weighed[:, k % SLOTS, :], act_out[:, k % SLOTS, :], gates, ALU.mult)
                    i.then_inc(weighed_done, 1)

                for k in range(OFF):
                    unit(k, k, None)

                def expert(j, u):
                    pool.wait_ge(g_in[u], 16 * (j + 1))
                    for k in range(UNITS):
                        cs = slice(k % CHUNKS * CHUNK, (k % CHUNKS + 1) * CHUNK)
                        unit(OFF + UNITS * (2 * j + u) + k, k, gate[:, u, cs])

                expert(0, 0)
                expert(0, 1)
                with pool.Fori(1, E // 2) as j:
                    expert(j, 0)
                    expert(j, 1)


def ternary(chip, tag):
    nc, c, dram = chip.nc, chip, chip.dram
    EPS, QB, LN2_EPS = 1e-5, 128.0, 1e-3
    ROUND = 1.5 * 2.0 ** 23
    with ExitStack() as ctx:
        def sb(name, shape, dt=F32):
            return ctx.enter_context(nc.sbuf_tensor(f"{tag}_{name}", shape, dt))

        sem = Semaphores(nc, ctx, tag)
        norm = Norm(chip, ctx, tag + "n", sem)
        w, wq, wabs = sb("w", [P, D]), sb("wq", [P, D]), sb("wabs", [P, 1])
        gamma, beta = sb("gamma", [P, D]), sb("beta", [P, D])
        st = sb("st", [P, 8])
        loaded, made, summed, peak, peak_all, clipped, out_ready = (
            sem(n) for n in ("loaded", "made", "summed", "peak", "peak_all", "clipped", "out_ready"))
        dve_own = sem("dve_own")
        block = sem.open_block()

        @block.sync
        def _(sp):
            sp.dma_start(w[:, :], dram[f"{tag}_w"]).then_inc(loaded, 16)
            for name, tile in (("gamma", gamma), ("beta", beta)):
                sp.dma_start(tile[:, :], dram[f"{tag}_{name}"].rearrange("(a n) -> a n", a=1)
                             .to_broadcast([P, D])).then_inc(loaded, 16)

        @block.gpsimd
        def _(pool):
            pool.wait_ge(peak, 1)
            pool.partition_all_reduce(st[:, 4:5], st[:, 3:4], P, RMAX).then_inc(peak_all, 1)

        @block.scalar
        def _(act):
            norm.scalar(act, c.xn, 1)
            norm.scalar(act, c.xn, 2)
            norm.copy_scalar(act, (0, 1, 2, 3))

        @block.tensor
        def _(pe):
            pe.wait_ge(made, 1)
            pe.matmul(c.psum[4][:, 0:1], c.ones[:, :], wabs[:, :], start=True, stop=True).then_inc(summed, 1)
            pe.wait_ge(clipped, 1)
            norm.tensor(pe, c.xn, (0, 1, 2, 3))
            pe.wait_ge(norm.copied, CHUNKS)
            for g in range(CHUNKS):
                for t in range(4):
                    n = 4 * g + t
                    i = pe.matmul(c.psum[4 + g][:, t * P:(t + 1) * P], c.xnT[:, n * P:(n + 1) * P], wq[:, :],
                                  start=True, stop=True)
                i.then_inc(out_ready, 1)

        @block.vector
        def _(dve):
            chain = Chain(dve, dve_own)
            dve.wait_ge(loaded, 48)
            dve.tensor_reduce(wabs[:, :], w[:, :], AXX, ALU.add, apply_absolute_value=True).then_inc(made, 1)
            norm.vector(dve, chain, c.x, c.xn, LN_EPS)
            norm.vector(dve, chain, c.xn, c.xn, LN2_EPS)
            every = [P, TILES, D]
            xn = c.xn[:, :, :]
            chain(dve.tensor_tensor(xn, xn, gamma[:, :].unsqueeze(1).to_broadcast(every), ALU.mult))
            chain(dve.tensor_tensor(xn, xn, beta[:, :].unsqueeze(1).to_broadcast(every), ALU.add))
            dve.tensor_reduce(st[:, 3:4], c.xn[:, :, :].rearrange("p t d -> p (t d)"), AXX, ALU.max,
                              apply_absolute_value=True).then_inc(peak, 1)
            dve.wait_ge(summed, 1)
            chain(dve.tensor_scalar(st[:, 0:1], c.psum[4][:, 0:1], 1.0 / (D * D), None, ALU.mult))
            chain(dve.tensor_scalar(st[:, 1:2], st[:, 0:1], EPS, None, ALU.add))
            chain(dve.reciprocal(st[:, 1:2], st[:, 1:2]))
            chain(dve.tensor_scalar(wq[:, :], w[:, :], st[:, 1:2], None, ALU.mult))
            chain(dve.tensor_scalar(wq[:, :], wq[:, :], 2.0, -2.0, ALU.min, ALU.max))
            chain(dve.tensor_scalar(wq[:, :], wq[:, :], ROUND, None, ALU.add))
            chain(dve.tensor_scalar(wq[:, :], wq[:, :], -ROUND, None, ALU.add))
            chain(dve.tensor_scalar(wq[:, :], wq[:, :], 1.0, -1.0, ALU.min, ALU.max))
            dve.wait_ge(peak_all, 1)
            chain(dve.reciprocal(st[:, 5:6], st[:, 4:5]))
            chain(dve.tensor_tensor(st[:, 6:7], st[:, 4:5], st[:, 0:1], ALU.mult))
            chain(dve.tensor_scalar(st[:, 6:7], st[:, 6:7], 1.0 / QB, None, ALU.mult))
            chain(dve.tensor_scalar(xn, xn, QB, st[:, 5:6], ALU.mult, ALU.mult))
            dve.tensor_scalar(xn, xn, QB - EPS, EPS - QB, ALU.min, ALU.max).then_inc(clipped, 1)
            norm.copy_vector(dve, (0, 1, 2, 3))
            for g in range(CHUNKS):
                dve.wait_ge(out_ready, g + 1)
                xs = c.x[:, 4 * g:4 * g + 4, :]
                dve.scalar_tensor_tensor(xs, c.psum[4 + g][:, :].rearrange("p (t d) -> p t d", t=4), st[:, 6:7],
                                         xs, ALU.mult, ALU.add)


def store_x(chip, out):
    nc, c = chip.nc, chip
    with ExitStack() as ctx:
        sem = Semaphores(nc, ctx, "end")
        stored = sem("stored")
        block = sem.open_block()

        @block.sync
        def _(sp):
            sp.dma_start(out.rearrange("(t p) d -> p t d", p=P), c.x[:, :, :]).then_inc(stored, 16)
            sp.wait_ge(stored, 16)


def build(nc, dram, out, upto=8, first=0):
    with ExitStack() as ctx:
        chip = Chip(nc, ctx, dram)
        start_up(chip)
        sublayers = [
            lambda: attention(chip, "a0"),
            lambda: experts(chip, "f0", "capacity"),
            lambda: attention(chip, "a1", biased=True, full_mask="mask"),
            lambda: experts(chip, "f1", "nearest"),
            lambda: attention(chip, "a2", rope=True, causal=True, key_mask="keep2"),
            lambda: ternary(chip, "f2"),
            lambda: attention(chip, "a3", key_mask="keep3", out_bias=False),
            lambda: experts(chip, "f3", "top"),
        ]
        for sublayer in sublayers[first:upto]:
            sublayer()
        store_x(chip, out)


def rotary():
    theta = (1.0 / np.float32(10000.0) ** (np.arange(0, HD, 2, dtype=np.float32) / np.float32(HD))).astype(np.float32)
    angle = np.arange(S, dtype=np.float32)[None, :] * np.repeat(theta, 2)[:, None]
    sign = np.where(np.arange(HD) % 2 == 0, -1.0, 1.0).astype(np.float32)[:, None]
    cos, sin = np.cos(angle), np.sin(angle) * sign
    return np.tile(cos, (H, 1)).astype(np.float32), np.tile(sin, (H, 1)).astype(np.float32)


def arrange(v):
    swap = np.arange(D) ^ 1
    cos, sin = rotary()
    a = {"x": v["x"].reshape(N, D), "ctxT": v["ctx_1024"].reshape(N, D).T,
         "mask": v["mask_BxSxS2_if1"], "mask_T": v["mask_BxSxS2_if1"].transpose(0, 2, 1),
         "keep2": v["mask_BxS2_if1"], "keep3": v["mask_BxS2_ik0"]}
    for n in range(3):
        for w in "qkvo":
            a[f"a{n}_w{w}"] = v[f"L{n}_xattn_W{w}"].T
        a[f"a{n}_bo"] = v[f"L{n}_xattn_bo"]
    for w in "qkv":
        a[f"a1_b{w}"] = v[f"L1_xattn_b{w}"]
    a["a2_wsq"], a["a2_wsk"] = v["L2_xattn_Wq"][swap].T, v["L2_xattn_Wk"][swap].T
    a["a2_cos"], a["a2_sin"] = cos, sin
    a["a3_wq"], a["a3_wo"] = v["L3_xattn_Wq"].T, v["L3_xattn_Wo"].T
    a["a3_wk"], a["a3_wv"] = v["L3_xattn_Wkv"][:D].T, v["L3_xattn_Wkv"][D:].T
    a["f0_router"] = v["L0_ffn_wg"].T
    for w in ("w1", "w2", "w3", "sw1", "sw2", "sw3"):
        a[f"f0_{w}"] = v[f"L0_ffn_{w}"]
    a["f1_router"], a["f1_scale"] = v["L1_ffn_centroids"].T, v["L1_ffn_scale"]
    a["f1_up"], a["f1_down"] = v["L1_ffn_up_w"], v["L1_ffn_down_w"]
    a["f2_w"], a["f2_gamma"], a["f2_beta"] = v["L2_ffn_weight"], v["L2_ffn_ln_gamma"], v["L2_ffn_ln_beta"]
    a["f3_router"], a["f3_rw"], a["f3_rb"] = v["L3_ffn_keys"].T, v["L3_ffn_rw"].T, v["L3_ffn_rb"]
    a["f3_up"], a["f3_down"] = v["L3_ffn_w1"].transpose(0, 2, 1), v["L3_ffn_w2"].transpose(0, 2, 1)
    a["f3_b1"] = v["L3_ffn_b1"].reshape(16, 4, P).transpose(0, 2, 1)
    a["f3_b2"] = v["L3_ffn_b2"]
    return {k: np.ascontiguousarray(x) for k, x in a.items()}


UPTO = 8


def kernel(**inputs):
    import numpy as _np
    import concourse.bacc as _bacc
    from concourse import mybir as _mybir
    from concourse.bass_utils import run_bass_kernel_spmd as _run

    nc = _bacc.Bacc("TRN2", target_bir_lowering=False, num_devices=1)
    arrays, dram = {}, {}
    for name, a in arrange({k: _np.asarray(x) for k, x in inputs.items()}).items():
        arrays[f"in_{name}"] = a
        dram[name] = nc.dram_tensor(f"in_{name}", a.shape, _mybir.dt.from_np(a.dtype), kind="ExternalInput").ap()
    out = nc.dram_tensor("out_x", (N, D), _mybir.dt.float32, kind="ExternalOutput").ap()
    build(nc, dram, out, UPTO)
    r = _run(nc, [arrays], core_ids=[0])
    return r.results[0]["out_x"].reshape(B, S, D)
```

```python
from contextlib import ExitStack

import numpy as np

import concourse.bass as bass
from concourse import mybir

F32 = mybir.dt.float32
BF16 = mybir.dt.bfloat16
F32R = mybir.dt.float32r
I32 = mybir.dt.int32
ALU = mybir.AluOpType
ACT = mybir.ActivationFunctionType
AXX = mybir.AxisListType.X
RMAX = bass.bass_isa.ReduceOp.max

B, S, D, H = 8, 256, 128, 16
HD = D // H
N = B * S
P = 128
TILES = N // P
CHUNK = 512
CHUNKS = N // CHUNK
PAIRS = H // 2
PARTS = 3
BLOCKS = 6
STACK = BLOCKS * HD
EXTRA = 2 * STACK
MROWS = P - EXTRA
VW = 32
LN_EPS, RMS_EPS, LN2_EPS = 1e-5, 1e-6, 1e-3
NEG = -1e30
MASKED = -1e9
MARK = -3e38
LAG = 4

Q_BLOCKS = [(0, 3, 0, 0), (3, 2, 1, 0), (5, 1, 2, 0)]
K_BLOCKS = [(0, 3, 0, 1), (3, 2, 0, 1), (5, 1, 0, 0)]


def at_least(eng, sem, n):
    if not isinstance(n, int) or n > 0:
        eng.wait_ge(sem, n)


def apart(eng, n, passed):
    if not isinstance(n, int):
        eng.sem_inc(passed, 1)


class Chain:

    def __init__(self, eng, sem, base=0, passed=None):
        self.eng, self.sem, self.base, self.n, self.passed = eng, sem, base, 0, passed

    def __call__(self, ins):
        ins.then_inc(self.sem, 1)
        self.n += 1
        self.eng.wait_ge(self.sem, self.base + self.n)
        apart(self.eng, self.base, self.passed)

    def rebase(self, base):
        self.base, self.n = base, 0


class Semaphores:

    def __init__(self, nc, ctx, tag):
        self.nc, self.ctx, self.tag, self.numbers = nc, ctx, tag, []

    def __call__(self, name):
        s = self.ctx.enter_context(self.nc.semaphore(f"{self.tag}_{name}"))
        self.numbers.append(s.num)
        return s

    def open_block(self):
        self.ctx.callback(self.clear)
        return self.ctx.enter_context(self.nc.Block())

    def clear(self):
        numbers, start = sorted(self.numbers), 0
        for n in range(1, len(numbers) + 1):
            if n == len(numbers) or numbers[n] != numbers[n - 1] + 1:
                self.nc.gpsimd.sem_clear(range(numbers[start], numbers[n - 1] + 1))
                start = n
        self.nc.all_engine_barrier()


class Chip:

    def __init__(self, nc, ctx, dram):
        self.nc, self.dram = nc, dram

        def sb(name, shape, dt=F32):
            return ctx.enter_context(nc.sbuf_tensor(name, shape, dt))

        self.x = sb("x", [P, TILES, D])
        self.xn = sb("xn", [P, TILES, D])
        self.xnT = sb("xnT", [P, N])
        self.ctxT = sb("ctxT", [P, N])
        self.ident = sb("ident", [P, P])
        self.identb = sb("identb", [P, P], BF16)
        self.ones = sb("ones", [P, P])
        eps = sb("eps", [P, 3])
        self.eps = {value: eps[:, n:n + 1] for n, value in enumerate((LN_EPS, RMS_EPS, LN2_EPS))}
        self.zrow = sb("zrow", [1, CHUNK], BF16)
        self.rev = sb("rev", [P, 32])
        self.own_rows = sb("own_rows", [P, PAIRS], BF16)
        self.qs = sb("qs", [P, 2, PAIRS, S], BF16)
        self.ks = sb("ks", [P, 2, H, S], BF16)
        self.vaug = sb("vaug", [P, 2, 2, H, VW])
        self.psum = [ctx.enter_context(nc.psum_tensor(f"bank{i}", [P, CHUNK], F32)) for i in range(8)]


def start_up(chip):
    nc, c = chip.nc, chip
    with ExitStack() as ctx:
        sem = Semaphores(nc, ctx, "start")
        loaded, filled, cleared = sem("x_loaded"), sem("filled"), sem("cleared")
        ROWS_MADE = 1 + PARTS
        block = sem.open_block()

        @block.sync
        def _(sp):
            sp.dma_start(c.x[:, :, :], c.dram["x"].rearrange("(t p) d -> p t d", p=P)).then_inc(loaded, 16)
            sp.dma_start(c.ctxT[:, :], c.dram["ctxT"]).then_inc(loaded, 16)
            sp.wait_ge(loaded, 32)

        @block.vector
        def _(dve):
            dve.memset(c.vaug[:, :, :, :, :], 0.0).then_inc(cleared, 1)
            dve.memset(c.ks[0:EXTRA, 0, :, :].bitcast(F32), 0.0)
            dve.memset(c.qs[EXTRA:P, :, :, :], 1.0)
            dve.wait_ge(cleared, 1)
            dve.memset(c.vaug[:, :, :, :, HD:HD + 1], 1.0)

        @block.scalar
        def _(act):
            act.wait_ge(filled, ROWS_MADE)
            for u in range(2):
                for half in range(2):
                    act.activation(c.ks[EXTRA:P, u, 8 * half:8 * half + 8, :],
                                   c.own_rows[EXTRA:P, :].unsqueeze(2).to_broadcast([MROWS, PAIRS, S]), ACT.Copy)

        @block.gpsimd
        def _(pool):
            done = Chain(pool, filled)
            done(pool.memset(c.own_rows[:, :], 0.0))
            for part in range(PARTS):
                done(pool.affine_select(out=c.own_rows[:, :], in_=c.own_rows[:, :], compare_op=ALU.not_equal,
                                        fill=1.0, base=-(EXTRA + 1 + 8 * part), pattern=[[-1, PAIRS]],
                                        channel_multiplier=1))
            assert done.n == ROWS_MADE
            pool.memset(c.ks[0:EXTRA, 1, :, :].bitcast(F32), 0.0)
            done(pool.memset(c.ones[:, :], 1.0))
            done(pool.memset(c.zrow[:, :], 0.0))
            for value, column in c.eps.items():
                done(pool.memset(column, value))
            done(pool.iota(c.rev[:, :], [[-1, 32]], base=32, channel_multiplier=0,
                           allow_small_or_imprecise_dtypes=True))
            for m in (c.ident, c.identb):
                done(pool.memset(m[:, :], 0.0))
                done(pool.affine_select(out=m[:, :], in_=m[:, :], compare_op=ALU.not_equal, fill=1.0,
                                        base=0, pattern=[[-1, P]], channel_multiplier=1))


class Norm:

    def __init__(self, chip, ctx, tag, sem):
        nc, self.c = chip.nc, chip
        self.measured, self.spread = sem("norm_measured"), sem("norm_spread")
        self.rooted, self.normed = sem("norm_rooted"), sem("norm_normed")
        self.turned, self.copied = sem("norm_turned"), sem("norm_copied")
        self.parts = ctx.enter_context(nc.sbuf_tensor(f"{tag}_parts", [P, TILES, 6], F32))
        self.st = ctx.enter_context(nc.sbuf_tensor(f"{tag}_st", [P, TILES, 2], F32))
        self.rstd = ctx.enter_context(nc.sbuf_tensor(f"{tag}_rstd", [P, TILES], F32))
        self.inverted = sem("norm_inverted")
        self.measures = self.roots = self.inverses = 0

    def take_stats(self, dve, g, src):
        self.measures += 1
        for t in range(4 * g, 4 * g + 4):
            i = dve.bn_stats(self.parts[:, t, :], src[:, t, :])
        i.then_inc(self.measured, 1)
        dve.wait_ge(self.measured, self.measures)
        for t in range(4 * g, 4 * g + 4):
            i = dve.bn_aggr(self.st[:, t, :], self.parts[:, t, :])
        i.then_inc(self.spread, 1)

    def take_root(self, act, g, eps):
        self.roots += 1
        act.wait_ge(self.spread, self.roots)
        every = slice(4 * g, 4 * g + 4)
        act.activation(self.rstd[:, every], self.st[:, every, 1], ACT.Sqrt, bias=self.c.eps[eps]).then_inc(self.rooted, 1)

    def take_square_root(self, act, chain, g, src, spare, eps):
        act.wait_ge(self.normed, g + 1)
        for t in range(4 * g, 4 * g + 4):
            i = act.activation(spare[:, t, :], src[:, t, :], ACT.Square, accum_out=self.st[:, t, 1:2])
        chain(i)
        every = slice(4 * g, 4 * g + 4)
        act.activation(self.rstd[:, every], self.st[:, every, 1], ACT.Sqrt, scale=1.0 / D,
                       bias=self.c.eps[eps]).then_inc(self.rooted, 1)

    def take_inverse(self, dve, g):
        self.inverses += 1
        dve.wait_ge(self.rooted, self.inverses)
        every = slice(4 * g, 4 * g + 4)
        dve.reciprocal(self.rstd[:, every], self.rstd[:, every]).then_inc(self.inverted, 1)
        dve.wait_ge(self.inverted, self.inverses)

    def normalise(self, dve, g, src, dst):
        self.take_inverse(dve, g)
        for t in range(4 * g, 4 * g + 4):
            i = dve.tensor_scalar(dst[:, t, :], src[:, t, :], self.st[:, t, 0:1], self.rstd[:, t:t + 1],
                                  ALU.subtract, ALU.mult)
        i.then_inc(self.normed, 1)

    def vector(self, dve, src, dst):
        self.take_stats(dve, 0, src)
        for g in range(CHUNKS):
            if g + 1 < CHUNKS:
                self.take_stats(dve, g + 1, src)
            self.normalise(dve, g, src, dst)

    def tensor(self, pe, src, g, bank, ready):
        pe.wait_ge(ready, g + 1)
        for t in range(4):
            i = pe.transpose(self.c.psum[bank][:, t * P:(t + 1) * P], src[:, 4 * g + t, :], self.c.ident[:, :])
        i.then_inc(self.turned, 1)

    def scalar(self, act, g, bank):
        act.wait_ge(self.turned, g + 1)
        act.activation(self.c.xnT[:, g * CHUNK:(g + 1) * CHUNK], self.c.psum[bank][:, :],
                       ACT.Copy).then_inc(self.copied, 1)


def attention(chip, tag, biased=False, rope=False, full_mask=None, causal=False, key_mask=None,
              out_bias=True):
    nc, c, dram = chip.nc, chip, chip.dram
    SCALE = float(HD) ** -0.5
    masked = causal or full_mask is not None
    with ExitStack() as ctx:
        def sb(name, shape, dt=F32):
            return ctx.enter_context(nc.sbuf_tensor(f"{tag}_{name}", shape, dt))

        sem = Semaphores(nc, ctx, tag)
        norm = Norm(chip, ctx, tag + "n", sem)
        wq, wk, wv, wo = (sb(n, [P, P]) for n in ("wq", "wk", "wv", "wo"))
        wsq, wsk = (sb(n, [P, P]) for n in ("wsq", "wsk")) if rope else (None, None)
        cos, sin = (sb(n, [P, S]) for n in ("cos", "sin")) if rope else (None, None)
        bqk = sb("bqk", [P, 2]) if biased else None
        bv = sb("bv", [P, D]) if biased else None
        bo = sb("bo", [P, D]) if out_bias else None
        values = sb("values", [P, TILES, D])
        qk = sb("qk", [P, 2, S])
        qks = sb("qks", [P, 2, S]) if rope else None
        rest = sb("rest", [P, 2, S])
        parts = sb("parts", [P, PARTS, 2, S], BF16)
        nmax = sb("nmax", [P, 2, 2, PAIRS])
        nrest = sb("nrest", [P, 2, PAIRS])
        nparts = sb("nparts", [P, 2, 2, MROWS], BF16)
        probs = sb("probs", [P, 4, 2 * S])
        pv = sb("pv", [P, 2, CHUNK])
        recip = sb("recip", [P, 2, 2, 4])
        o = sb("o", [P, 2, D])
        oT = sb("oT", [P, S])
        mask_shape = [P, P] if causal else [P, 2, 2, S]
        maskq = sb("maskq", mask_shape, BF16) if masked else None
        maskk = sb("maskk", mask_shape, BF16) if masked else None
        masked_scores = sb("masked_scores", [P, 2, 2, S], BF16) if full_mask else None
        rawq = sb("rawq", [P, 2, S], I32) if full_mask else None
        rawk = sb("rawk", [P, 2, S], I32) if full_mask else None
        km = sb("km", [B, S], I32) if key_mask else None
        kmb = sb("kmb", [B, S], BF16) if key_mask else None

        def scratch(name, shape, dt):
            return nc.dram_tensor(f"{tag}_{name}", shape, dt, kind="Internal").ap()

        q_dram, k_dram = (scratch(n, (2, P, BLOCKS, S), BF16) for n in ("q_dram", "k_dram"))
        m_dram = scratch("m_dram", (B, S), BF16) if key_mask else None

        qk_weights_in, weights_in = sem("qk_weights_in"), sem("weights_in")
        k0_ready, k0_read, k0_split = sem("k0_ready"), sem("k0_read"), sem("k0_split")
        stack_in = [[sem(f"stack_in{u}{half}") for half in range(2)] for u in range(2)]
        unused_made, bias_added = sem("unused_made"), sem("bias_added")
        split_out = sem("split_out")
        maskq_in, maskk_in, maskq_made, maskk_made = (sem(n) for n in ("mq_in", "mk_in", "mq_made", "mk_made"))
        keymask_in, keymask_made, keymask_out = (sem(n) for n in ("km_in", "km_made", "km_out"))
        qk_ready, qk_read, sw_ready, sw_read = (sem(n) for n in ("qk_ready", "qk_read", "sw_ready", "sw_read"))
        v_ready, v_copied, v_taken = sem("v_ready"), sem("v_copied"), sem("v_taken")
        split_done = sem("split_done")
        max_ready, max_read = sem("max_ready"), sem("max_read")
        nsplit_done = sem("nsplit_done")
        mT_ready, mT_read = sem("mT_ready"), sem("mT_read")
        score_ready, exp_done = sem("score_ready"), sem("exp_done")
        pv_ready, pv_read = sem("pv_ready"), sem("pv_read")
        heads_turned, recip_done, heads_read = sem("heads_turned"), sem("recip_done"), sem("heads_read")
        o_turned, oT_read = sem("o_turned"), sem("oT_read")
        out_ready, out_read = sem("out_ready"), sem("out_read")
        dve_own, pool_own = sem("dve_own"), sem("pool_own")
        sp_passed, pool_passed, dve_passed = sem("sp_passed"), sem("pool_passed"), sem("dve_passed")

        CAUSAL_BLOCKS = ((0, 0), (0, 1), (1, 1))
        n_exp = (len(CAUSAL_BLOCKS) if causal else 4) * P
        MAXB, SCB, PVB, AUX, TAIL = (0, 1), (2, 3), (4, 5), 6, 7
        V_BANKS = (4, 5, 2, 3)
        K0_BANK, SW0_BANK = TAIL, 5
        auxb = c.psum[AUX][:, :].bitcast(BF16)
        qk_weights = [("wk", wk), ("wq", wq)]
        if rope:
            qk_weights += [("wsk", wsk), ("cos", cos), ("sin", sin), ("wsq", wsq)]
        n_qk_weights = len(qk_weights) + 2 * biased
        n_stack = 3 + (1 if key_mask else 0)
        rows = EXTRA + (1 if key_mask else 0)

        n_weights = 2 + biased + out_bias
        BOTH, Q_ONLY, K_ONLY = slice(0, 2), slice(0, 1), slice(1, 2)

        block = sem.open_block()

        @block.sync
        def _(sp):
            def load_weight(name, tile, done):
                sp.dma_start(tile[:, :], dram[f"{tag}_{name}"]).then_inc(done, 16)

            if key_mask:
                sp.dma_start(km[:, :], dram[key_mask]).then_inc(keymask_in, 16)
            for name, tile in qk_weights:
                load_weight(name, tile, qk_weights_in)
            if biased:
                for n, name in enumerate(("bk", "bq")):
                    sp.dma_start(bqk[:, 1 - n:2 - n], dram[f"{tag}_{name}"].rearrange("(p a) -> p a", a=1)).then_inc(qk_weights_in, 16)
            load_weight("wv", wv, weights_in)
            load_weight("wo", wo, weights_in)
            for name, tile in (("bv", bv), ("bo", bo)):
                if tile is not None:
                    sp.dma_start(tile[:, :], dram[f"{tag}_{name}"].rearrange("(a n) -> a n", a=1)
                                 .to_broadcast([P, D])).then_inc(weights_in, 16)
            if key_mask:
                sp.wait_ge(keymask_made, 1)
                sp.dma_start(m_dram, kmb[:, :]).then_inc(keymask_out, 16)
                sp.wait_ge(keymask_out, 16)

            def load_maskq(b):
                at_least(sp, maskq_made, b)
                apart(sp, b, sp_passed)
                sp.dma_start(rawq[:, :, :], dram[full_mask][bass.ds(b, 1), :, :]
                             .rearrange("a (t p) k -> p (a t) k", p=P)).then_inc(maskq_in, 16)

            def load_maskk(b):
                at_least(sp, maskk_made, b)
                apart(sp, b, sp_passed)
                sp.dma_start(rawk[:, :, :], dram[full_mask + "_T"][bass.ds(b, 1), :, :]
                             .rearrange("a (t p) q -> p (a t) q", p=P)).then_inc(maskk_in, 16)

            def write_parts(j, u):
                b = 2 * j + u
                if not (isinstance(j, int) and j == 0):
                    for half in range(2):
                        sp.wait_ge(stack_in[u][half], 16 * n_stack * j)
                        apart(sp, j, sp_passed)
                first = isinstance(b, int) and b == 0
                if first:
                    sp.wait_ge(k0_split, 1)
                else:
                    sp.wait_ge(split_done, b + 1)
                for n, where, blocks in ((1, k_dram, K_BLOCKS), (0, q_dram, Q_BLOCKS)):
                    if first and n == 0:
                        sp.wait_ge(split_done, 1)
                    for first, count, part, step in blocks:
                        if step:
                            src = parts[:, part:part + count, n, :]
                        else:
                            src = parts[:, part:part + 1, n, :].to_broadcast([P, count, S])
                        sp.dma_start(where[u, :, first:first + count, :], src).then_inc(split_out, 16)
                sp.wait_ge(split_out, 96 * (b + 1))
                apart(sp, b, sp_passed)

            def load_stacks(j, u):
                b = 2 * j + u
                for half in range(2):
                    at_least(sp, score_ready, H * (b - 2) + 8 * (half + 1))
                    apart(sp, b, sp_passed)
                    pairs = slice(4 * half, 4 * half + 4)
                    src = q_dram[u].rearrange("(g h d) c t -> (h d c) g t", g=PAIRS, h=2)
                    sp.dma_start(c.qs[0:EXTRA, u, pairs, :], src[:, pairs, :]).then_inc(stack_in[u][half], 16)
                    for par in range(2):
                        src = k_dram[u].rearrange("(g h d) c t -> h (d c) g t", g=PAIRS, h=2)[par]
                        sp.dma_start(c.ks[STACK * par:STACK * (par + 1), u, 8 * half + par:8 * half + 8:2, :],
                                     src[:, pairs, :]).then_inc(stack_in[u][half], 16)
                    if key_mask:
                        sp.dma_start(c.ks[EXTRA:EXTRA + 1, u, 8 * half:8 * half + 8, :],
                                     m_dram[bass.ds(b, 1), :].unsqueeze(1).to_broadcast([1, PAIRS, S]))\
                          .then_inc(stack_in[u][half], 16)

            def step(j, u, last=False):
                b = 2 * j + u
                if full_mask and not last:
                    load_maskq(b + 2)
                if full_mask and not (last and u == 1):
                    load_maskk(b + 1)
                if not last:
                    write_parts(j + 1, u)
                    load_stacks(j + 1, u)

            if full_mask:
                load_maskq(0)
                load_maskk(0)
                load_maskq(1)
            for u in range(2):
                write_parts(0, u)
                load_stacks(0, u)
            step(0, 0)
            step(0, 1)
            with sp.Fori(1, B // 2 - 1) as j:
                step(j, 0)
                step(j, 1)
            step(B // 2 - 1, 0, True)
            step(B // 2 - 1, 1, True)

        @block.tensor
        def _(pe):
            pe.wait_ge(qk_weights_in, 16 * n_qk_weights)
            for w, bank in ((wk, K0_BANK), (wsk, SW0_BANK)):
                if w is not None:
                    pe.matmul(c.psum[bank][:, S:2 * S], w[:, :], c.ctxT[:, 0:S], start=True, stop=True).then_inc(k0_ready, 1)
            norm.tensor(pe, c.xn, 0, 0, norm.normed)
            pe.wait_ge(norm.copied, 1)

            def project_qk(j, u, a, b_, ready):
                tokens = bass.ds((2 * j + u) * S, S)
                i = pe.matmul(c.psum[AUX][:, 0:S], a[:, :], c.xnT[:, tokens], start=True, stop=True)
                if isinstance(j, int) and j == u == 0:
                    i.then_inc(ready, 1)
                    return
                pe.matmul(c.psum[AUX][:, S:2 * S], b_[:, :], c.ctxT[:, tokens], start=True, stop=True).then_inc(ready, 1)

            def max_scores(b, u, h):
                bank = c.psum[MAXB[h % 2]]
                q, k = c.qs[0:rows, u, h // 2, :], c.ks[0:rows, u, h, :]
                at_least(pe, max_read, H * b + h - 1)
                if causal:
                    if h < 2:
                        pe.wait_ge(unused_made, 1)
                    for qt, kt in ((1, 0), (0, 0), (1, 1)):
                        dst = bank[:, qt * S + kt * P:qt * S + (kt + 1) * P]
                        if qt == kt:
                            pe.matmul(dst, c.identb[:, :], maskq[:, :], start=True, stop=False)
                        i = pe.matmul(dst, q[:, qt * P:(qt + 1) * P], k[:, kt * P:(kt + 1) * P], start=qt != kt,
                                      stop=True)
                else:
                    for t in range(2):
                        i = pe.matmul(bank[:, t * S:(t + 1) * S], q[:, t * P:(t + 1) * P], k, start=True, stop=True)
                i.then_inc(max_ready, 1)

            def turn_max(b, half):
                pe.wait_ge(nsplit_done, 2 * b + half + 1)
                for t in range(2):
                    i = pe.transpose(auxb[0:MROWS, t * P:(t + 1) * P], nparts[:, half, t, :], c.identb[:, :])
                i.then_inc(mT_ready, 1)

            def scores(b, u, h):
                bank = c.psum[SCB[h % 2]]
                at_least(pe, exp_done, H * b + h - 1)
                if h % 4 == 0:
                    pe.wait_ge(mT_read, 4 * b + h // 4 + 1)
                q, k = c.qs[:, u, h // 2, :], c.ks[:, u, h, :]
                if causal:
                    for n, (kt, qt) in enumerate(CAUSAL_BLOCKS):
                        dst = bank[:, n * P:(n + 1) * P]
                        if qt == kt:
                            pe.matmul(dst, c.identb[:, :], maskk[:, :], start=True, stop=False)
                        i = pe.matmul(dst, k[:, kt * P:(kt + 1) * P], q[:, qt * P:(qt + 1) * P], start=qt != kt,
                                      stop=True)
                else:
                    if full_mask:
                        pe.wait_ge(maskk_made, b + 1)
                    for t in range(2):
                        dst = bank[:, t * S:(t + 1) * S]
                        if full_mask:
                            pe.matmul(dst, c.identb[:, :], maskk[:, u, t, :], start=True, stop=False)
                        i = pe.matmul(dst, k[:, t * P:(t + 1) * P], q, start=not full_mask, stop=True)
                i.then_inc(score_ready, 1)

            def weigh(b, u, h):
                if h % 8 == 0:
                    at_least(pe, pv_read, 2 * b + h // 8 - 1)
                if h == 0:
                    pe.wait_ge(v_taken, b + 1)
                pe.wait_ge(exp_done, H * b + h + 1)
                j = h % 4
                out = c.psum[PVB[h // 8]][32 * j:32 * j + 32, (h // 4 % 2) * S:(h // 4 % 2 + 1) * S]
                if causal:
                    for n, (kt, qt) in enumerate(CAUSAL_BLOCKS):
                        i = pe.matmul(out[:, qt * P:(qt + 1) * P], c.vaug[:, u, kt, h, :],
                                      probs[:, h % 4, n * P:(n + 1) * P], start=(kt == 0), stop=(kt == qt))
                else:
                    for t in range(2):
                        i = pe.matmul(out, c.vaug[:, u, t, h, :], probs[:, h % 4, t * S:(t + 1) * S], start=(t == 0),
                                      stop=(t == 1))
                i.then_inc(pv_ready, 1)

            def turn_heads(b, half):
                pe.wait_ge(pv_read, 2 * b + half + 1)
                if half:
                    pe.wait_ge(heads_read, 2 * b + 1)
                else:
                    at_least(pe, out_read, b)
                for q in range(4):
                    i = pe.transpose(c.psum[TAIL][:, q * P:(q + 1) * P], pv[:, half, q * P:(q + 1) * P], c.ident[:, :])
                i.then_inc(heads_turned, 1)

            def turn_o(b):
                pe.wait_ge(heads_read, 2 * b + 2)
                for t in range(2):
                    i = pe.transpose(c.psum[TAIL][:, t * P:(t + 1) * P], o[:, t, :], c.ident[:, :])
                i.then_inc(o_turned, 1)

            def project_out(b):
                pe.wait_ge(oT_read, b + 1)
                for t in range(2):
                    dst = c.psum[TAIL][:, t * P:(t + 1) * P]
                    i = pe.matmul(dst, oT[:, t * P:(t + 1) * P], wo[:, :], start=True, stop=True)
                i.then_inc(out_ready, 1)

            def step(j, u, last=False):
                b = 2 * j + u
                first = isinstance(b, int) and b == 0
                ends = last and u == 1
                for h in range(H):
                    scores(b, u, h)
                    if h < LAG:
                        max_scores(b, u, H - LAG + h)
                    elif not ends:
                        if h % 8 == LAG:
                            pe.wait_ge(stack_in[1 - u][h // 8], 16 * n_stack * (j + 1 + u))
                        max_scores(b + 1, 1 - u, h - LAG)
                    if h > 0:
                        weigh(b, u, h - 1)
                    elif not first:
                        weigh(b - 1, 1 - u, H - 1)
                    if h == 1 and not last:
                        pe.wait_ge(mT_read, 4 * b + 2)
                        project_qk(j + 1, u, wq, wk, qk_ready)
                    if h == 2 and not first:
                        turn_heads(b - 1, 1)
                    if h == 3 and rope and not last:
                        pe.wait_ge(qk_read, b + 3)
                        project_qk(j + 1, u, wsq, wsk, sw_ready)
                    if h == 4 and not first:
                        turn_o(b - 1)
                    if h == 6:
                        if last:
                            pe.wait_ge(mT_read, 4 * b + 2)
                        else:
                            pe.wait_ge(sw_read if rope else qk_read, b + 3)
                        turn_max(b, 1)
                    if h == 7 and not first:
                        project_out(b - 1)
                    if h == 10:
                        turn_heads(b, 0)
                    if h == 14 and not ends:
                        pe.wait_ge(mT_read, 4 * b + 4)
                        turn_max(b + 1, 0)

            def project_v(g):
                for t in range(4):
                    token = (4 * g + t) * P
                    i = pe.matmul(c.psum[V_BANKS[g]][:, t * D:(t + 1) * D], c.ctxT[:, token:token + P], wv[:, :],
                                  start=True, stop=True)
                i.then_inc(v_ready, 1)

            project_qk(0, 0, wq, wk, qk_ready)
            if rope:
                pe.wait_ge(qk_read, 1)
                project_qk(0, 0, wsq, wsk, sw_ready)
            pe.wait_ge(weights_in, 16 * n_weights)
            project_v(0)
            norm.tensor(pe, c.xn, 1, 1, norm.normed)
            norm.tensor(pe, c.xn, 2, 2, norm.normed)
            if rope:
                pe.wait_ge(k0_read, 2)
            project_v(1)
            norm.tensor(pe, c.xn, 3, 3, norm.normed)
            pe.wait_ge(qk_read, 1)
            if rope:
                pe.wait_ge(sw_read, 1)
            project_qk(0, 1, wq, wk, qk_ready)
            pe.wait_ge(norm.copied, CHUNKS)
            project_v(2)
            project_v(3)
            pe.wait_ge(qk_read, 2)
            if rope:
                project_qk(0, 1, wsq, wsk, sw_ready)
                pe.wait_ge(sw_read, 2)
            for h in range(H - LAG):
                if h % 8 == 0:
                    pe.wait_ge(stack_in[0][h // 8], 16 * n_stack)
                max_scores(0, 0, h)
                if h == 9:
                    turn_max(0, 0)
            step(0, 0)
            step(0, 1)
            with pe.Fori(1, B // 2 - 1) as j:
                step(j, 0)
                step(j, 1)
            step(B // 2 - 1, 0, True)
            step(B // 2 - 1, 1, True)
            weigh(B - 1, 1, H - 1)
            turn_heads(B - 1, 1)
            turn_o(B - 1)
            project_out(B - 1)

        @block.scalar
        def _(act):
            norm.take_root(act, 0, LN_EPS)
            norm.take_root(act, 1, LN_EPS)

            def take(dst, bank, halves, read, bias):
                if bias:
                    for n in range(halves.start, halves.stop):
                        i = act.activation(dst[:, n, :], c.psum[bank][:, n * S:(n + 1) * S], ACT.Identity,
                                           bias=bqk[:, n:n + 1])
                else:
                    i = act.activation(dst[:, halves, :], c.psum[bank][:, halves.start * S:halves.stop * S]
                                       .rearrange("p (n t) -> p n t", t=S), ACT.Copy)
                i.then_inc(read, 1)

            if biased:
                act.wait_ge(qk_weights_in, 16 * n_qk_weights)
            act.wait_ge(k0_ready, 1)
            take(qk, K0_BANK, K_ONLY, k0_read, biased)
            if rope:
                act.wait_ge(k0_ready, 2)
                take(qks, SW0_BANK, K_ONLY, k0_read, False)
            norm.scalar(act, 0, 0)
            norm.take_root(act, 2, LN_EPS)

            def take_qk(b, dst, ready, read, bias):
                act.wait_ge(ready, b + 1)
                at_least(act, split_done, b)
                take(dst, AUX, Q_ONLY if isinstance(b, int) and b == 0 else BOTH, read, bias)

            def take_max(b, u, half, part):
                if part == 0:
                    act.wait_ge(mT_ready, 2 * b + half + 1)
                pair = 4 * half + 2 * part
                act.activation(c.qs[EXTRA:P, u, pair:pair + 2, :],
                               auxb[0:MROWS, 0:S].unsqueeze(1).to_broadcast([MROWS, 2, S]), ACT.Copy).then_inc(mT_read, 1)

            def take_pv(b, half):
                act.wait_ge(pv_ready, H * b + 8 * (half + 1))
                at_least(act, heads_turned, 2 * (b - 1) + half + 1)
                act.activation(pv[:, half, :], c.psum[PVB[half]][:, :], ACT.Copy).then_inc(pv_read, 1)

            def step(j, u, last=False):
                b = 2 * j + u
                first = isinstance(b, int) and b == 0
                ends = last and u == 1
                for h in range(H):
                    act.wait_ge(score_ready, H * b + h + 1)
                    at_least(act, pv_ready, H * b + h - 3)
                    act.activation(probs[:, h % 4, 0:n_exp], c.psum[SCB[h % 2]][:, 0:n_exp], ACT.Exp,
                                   scale=SCALE).then_inc(exp_done, 1)
                    if h == 1 and not first:
                        take_pv(b - 1, 1)
                    if h == 5 and not first:
                        act.wait_ge(o_turned, b)
                        act.activation(oT[:, :], c.psum[TAIL][:, 0:S], ACT.Copy).then_inc(oT_read, 1)
                    if h == 2 and not last and not rope:
                        take_qk(b + 2, qk, qk_ready, qk_read, biased)
                    if h in (6, 7):
                        take_max(b, u, 1, h - 6)
                    if h == 9:
                        take_pv(b, 0)
                    if h >= 14 and not ends:
                        take_max(b + 1, 1 - u, 0, h - 14)

            def take_values(g):
                act.wait_ge(v_ready, g + 1)
                act.activation(values[:, 4 * g:4 * g + 4, :], c.psum[V_BANKS[g]][:, :]
                               .rearrange("p (t d) -> p t d", t=4), ACT.Copy).then_inc(v_copied, 1)

            take_qk(0, qk, qk_ready, qk_read, biased)
            if rope:
                take_qk(0, qks, sw_ready, sw_read, False)
            norm.take_root(act, 3, LN_EPS)
            take_values(0)
            norm.scalar(act, 1, 1)
            norm.scalar(act, 2, 2)
            take_values(1)
            norm.scalar(act, 3, 3)
            take_values(2)
            take_values(3)
            take_qk(1, qk, qk_ready, qk_read, biased)
            if rope:
                take_qk(1, qks, sw_ready, sw_read, False)
            act.activation(recip[:, 0, 0, 0:1], c.ones[:, 0:1], ACT.Exp).then_inc(v_copied, 1)
            take_max(0, 0, 0, 0)
            take_max(0, 0, 0, 1)
            step(0, 0)
            step(0, 1)
            with act.Fori(1, B // 2 - 1) as j:
                step(j, 0)
                step(j, 1)
            step(B // 2 - 1, 0, True)
            step(B // 2 - 1, 1, True)
            take_pv(B - 1, 1)
            act.wait_ge(o_turned, B)
            act.activation(oT[:, :], c.psum[TAIL][:, 0:S], ACT.Copy).then_inc(oT_read, 1)

        @block.vector
        def _(dve):
            chain = Chain(dve, dve_own)
            norm.vector(dve, c.x, c.xn)
            if biased:
                dve.wait_ge(weights_in, 16 * n_weights)
            if rope:
                dve.wait_ge(qk_weights_in, 16 * n_qk_weights)

            def take_v(b, u):
                if isinstance(b, int) and b == 0:
                    dve.wait_ge(v_copied, CHUNKS + 1)
                at_least(dve, pv_ready, H * (b - 1))
                dst = c.vaug[:, u, :, :, 0:HD]
                src = values[:, bass.ds(2 * b, 2), :].rearrange("p t (h d) -> p t h d", h=H)
                if biased:
                    i = dve.tensor_tensor(dst, src, bv[:, :].rearrange("p (h d) -> p h d", h=H).unsqueeze(1)
                                          .to_broadcast([P, 2, H, HD]), ALU.add)
                else:
                    i = dve.tensor_copy(dst, src)
                i.then_inc(v_taken, 1)

            def head_max(b, u, h):
                dve.wait_ge(max_ready, H * b + h + 1)
                if h % 8 == 0:
                    at_least(dve, nsplit_done, 2 * b + h // 8 - 1)
                if full_mask:
                    apart(dve, b, dve_passed)
                    for t in range(2):
                        i = dve.tensor_tensor_reduce(out=masked_scores[:, h % 2, t, :], in0=c.psum[MAXB[h % 2]][:, t * S:(t + 1) * S],
                                                     in1=maskq[:, u, t, :], scale=1.0, scalar=NEG, op0=ALU.add,
                                                     op1=ALU.max, accum_out=nmax[:, h // 8, t, h % 8:h % 8 + 1])
                    i.then_inc(max_read, 1)
                    return
                dve.tensor_reduce(nmax[:, h // 8, :, h % 8], c.psum[MAXB[h % 2]][:, :].rearrange(
                    "p (t k) -> p t k", t=2), AXX, ALU.max, negate=True).then_inc(max_read, 1)

            def take_heads(b, half):
                dve.wait_ge(heads_turned, 2 * b + half + 1)
                t4 = c.psum[TAIL][:, :].rearrange("p (g t h w) -> p g t h w", g=2, t=2, h=4)
                for t in range(2):
                    i = dve.reciprocal(recip[:, t, :, :], t4[:, :, t, :, HD])
                i.then_inc(recip_done, 1)
                dve.wait_ge(recip_done, 2 * b + half + 1)
                at_least(dve, o_turned, b)
                for t in range(2):
                    i = dve.tensor_tensor(
                        o[:, t, 64 * half:64 * half + 64].rearrange("p (g h d) -> p g h d", g=2, h=4),
                        t4[:, :, t, :, 0:HD], recip[:, t, :, :].unsqueeze(3).to_broadcast([P, 2, 4, HD]), ALU.mult)
                i.then_inc(heads_read, 1)

            def add_out(b):
                dve.wait_ge(out_ready, b + 1)
                if out_bias and isinstance(b, int) and b == 0:
                    dve.wait_ge(bias_added, 1)
                xs = c.x[:, bass.ds(2 * b, 2), :]
                dve.tensor_tensor(xs, xs, c.psum[TAIL][:, 0:S].rearrange("p (t d) -> p t d", t=2),
                                  ALU.add).then_inc(out_read, 1)

            def make_maskq(b, u):
                dve.wait_ge(maskq_in, 16 * (b + 1))
                dve.tensor_scalar(maskq[:, u, :, :], rawq[:, :, :], 0.0, MASKED, ALU.is_equal,
                                  ALU.mult).then_inc(maskq_made, 1)

            def make_maskk(b, u):
                dve.wait_ge(maskk_in, 16 * (b + 1))
                at_least(dve, score_ready, H * (b - 1))
                dve.tensor_scalar(maskk[:, u, :, :], rawk[:, :, :], 0.0, MASKED, ALU.is_equal,
                                  ALU.mult).then_inc(maskk_made, 1)

            def rotate(b, dst, table, ready, read):
                dve.wait_ge(ready, b + 1)
                at_least(dve, split_done, b)
                dve.tensor_tensor(dst[:, :, :], c.psum[AUX][:, :].rearrange("p (n t) -> p n t", t=S),
                                  table[:, :].unsqueeze(1).to_broadcast([P, 2, S]), ALU.mult).then_inc(read, 1)

            def step(j, u, last=False):
                b = 2 * j + u
                first = isinstance(b, int) and b == 0
                ends = last and u == 1
                for h in range(H):
                    if rope and not last:
                        if h == 2:
                            rotate(b + 2, qk, cos, qk_ready, qk_read)
                        if h == 4:
                            rotate(b + 2, qks, sin, sw_ready, sw_read)
                    if h < LAG:
                        head_max(b, u, H - LAG + h)
                    elif not ends:
                        head_max(b + 1, 1 - u, h - LAG)
                    if h == 2 and not first:
                        take_heads(b - 1, 1)
                    if h == 6 and full_mask and not last:
                        make_maskq(b + 2, u)
                    if h == 8 and not first:
                        add_out(b - 1)
                    if h == 10 and not ends:
                        take_v(b + 1, 1 - u)
                    if h == 11:
                        take_heads(b, 0)
                    if h == 12 and full_mask and not ends:
                        make_maskk(b + 1, 1 - u)

            if full_mask:
                make_maskq(0, 0)
                make_maskk(0, 0)
                make_maskq(1, 1)
            if causal:
                dve.wait_ge(norm.copied, CHUNKS)
                for bank in MAXB:
                    i = dve.memset(c.psum[bank][:, P:S], NEG)
                i.then_inc(unused_made, 1)
            for h in range(H - LAG):
                head_max(0, 0, h)
                if h == 8:
                    take_v(0, 0)
            step(0, 0)
            step(0, 1)
            with dve.Fori(1, B // 2 - 1) as j:
                step(j, 0)
                step(j, 1)
            step(B // 2 - 1, 0, True)
            step(B // 2 - 1, 1, True)
            take_heads(B - 1, 1)
            add_out(B - 1)

        @block.gpsimd
        def _(pool):
            chain = Chain(pool, pool_own, passed=pool_passed)
            if key_mask:
                pool.wait_ge(keymask_in, 16)
                pool.tensor_scalar(kmb[:, :], km[:, :], 0.0, NEG, ALU.is_equal, ALU.mult).then_inc(keymask_made, 1)
            chain(pool.memset(nparts[:, :, :, :], 0.0))
            chain(pool.memset(nparts[:, :, :, 0:1], 1.0))
            if causal:
                for table, sign in ((maskq, 1), (maskk, -1)):
                    chain(pool.memset(table[:, :], 0.0))
                    chain(pool.affine_select(out=table[:, :], in_=table[:, :], compare_op=ALU.is_ge, fill=NEG, base=0,
                                             pattern=[[-sign, P]], channel_multiplier=sign))
            if rope:
                pool.wait_ge(qk_weights_in, 16 * n_qk_weights)
            per_step = 8 + (2 if full_mask else 0) + (5 if rope else 4)

            def split(src, spare, dsts, last_sem):
                for n, dst in enumerate(dsts):
                    i = pool.tensor_scalar(dst, src, 1.0, 1.0, ALU.mult, ALU.mult)
                    if n == PARTS - 1:
                        i.then_inc(last_sem, 1)
                    else:
                        chain(i)
                        chain(pool.tensor_tensor(spare, src, dst, ALU.subtract))
                        src = spare

            def split_max(b, half):
                pool.wait_ge(max_read, H * b + 8 * (half + 1))
                at_least(pool, mT_ready, 2 * b + half - 1)
                apart(pool, b, pool_passed)
                if full_mask:
                    chain(pool.tensor_scalar(nmax[:, half, :, :], nmax[:, half, :, :], -1.0, 1.0, ALU.mult, ALU.mult))
                split(nmax[:, half, :, :], nrest[:, :, :],
                      [nparts[:, half, :, 1 + 8 * n:9 + 8 * n] for n in range(PARTS)], nsplit_done)

            def turn_and_split(halves, done, rotated=False):
                a, swapped = (qk[:, halves, :], qks[:, halves, :]) if rope else (None, None)
                if rope and rotated:
                    chain(pool.tensor_tensor(a, a, swapped, ALU.add))
                elif rope:
                    n = halves.stop - halves.start
                    over = [P, n, S]
                    chain(pool.tensor_tensor(a, a, cos[:, :].unsqueeze(1).to_broadcast(over), ALU.mult))
                    chain(pool.tensor_tensor(swapped, swapped, sin[:, :].unsqueeze(1).to_broadcast(over), ALU.mult))
                    chain(pool.tensor_tensor(a, a, swapped, ALU.add))
                split(qk[:, halves, :], rest[:, halves, :], [parts[:, n, halves, :] for n in range(PARTS)], done)

            def split_qk(b):
                pool.wait_ge(qk_read, b + 1)
                at_least(pool, split_out, 96 * b)
                apart(pool, b, pool_passed)
                if rope:
                    pool.wait_ge(sw_read, b + 1)
                turn_and_split(Q_ONLY if isinstance(b, int) and b == 0 else BOTH, split_done,
                               rotated=not (isinstance(b, int) and b < 2))

            def step(j, u, last=False):
                b = 2 * j + u
                split_max(b, 1)
                if not last:
                    split_qk(b + 2)
                if not (last and u == 1):
                    split_max(b + 1, 0)

            pool.wait_ge(k0_read, 2 if rope else 1)
            turn_and_split(K_ONLY, k0_split)
            split_qk(0)
            if out_bias:
                pool.wait_ge(norm.normed, CHUNKS)
                pool.wait_ge(weights_in, 16 * n_weights)
                pool.tensor_tensor(c.x[:, :, :], c.x[:, :, :], bo[:, :].unsqueeze(1).to_broadcast([P, TILES, D]),
                                   ALU.add).then_inc(bias_added, 1)
            split_qk(1)
            split_max(0, 0)
            before = chain.n
            step(0, 0)
            step(0, 1)
            assert chain.n == before + 2 * per_step, (chain.n, before, per_step)
            with pool.Fori(1, B // 2 - 1) as j:
                chain.rebase(before + 2 * per_step * j)
                step(j, 0)
                step(j, 1)
            chain.rebase(before + 2 * per_step * (B // 2 - 1))
            step(B // 2 - 1, 0, True)
            step(B // 2 - 1, 1, True)


def first_best(dve, chain, cur, n, sel, tmp, flag, best, lower):
    every = [P, TILES, n]
    chain(dve.tensor_reduce(best, cur, AXX, ALU.max))
    chain(dve.tensor_tensor(tmp, cur, best.unsqueeze(2).to_broadcast(every), ALU.is_equal))
    chain(dve.tensor_tensor(tmp, tmp, lower, ALU.mult))
    chain(dve.tensor_reduce(flag, tmp, AXX, ALU.max))
    chain(dve.tensor_tensor(sel, tmp, flag.unsqueeze(2).to_broadcast(every), ALU.is_equal))


def best_four(dve, chain, cur, n, sel, eight, left, spare):
    for t in range(TILES):
        i = dve.max(eight[:, t, :], cur[:, t, 0:n])
    chain(i)
    chain(dve.tensor_copy(eight[:, :, 4:8], spare))
    for t in range(TILES):
        i = dve.match_replace(left[:, t, 0:n + 4], eight[:, t, :], cur[:, t, 0:n + 4], MARK)
    chain(i)
    chain(dve.tensor_scalar(sel, left[:, :, 0:n], MARK, None, ALU.is_equal))


def experts(chip, tag, kind):
    nc, c, dram = chip.nc, chip, chip.dram
    shared = kind == "capacity"
    E = {"capacity": 32, "nearest": 8, "top": 16}[kind]
    HB = {"capacity": 1, "nearest": 2, "top": 4}[kind]
    UP = {"capacity": 2, "nearest": 4, "top": 4}[kind]
    gated = kind != "top"
    UNITS = HB * CHUNKS
    K = {"capacity": 4, "nearest": 1, "top": 4}[kind]
    GROUPS = 8
    CAP = int(1.25 * N * 4 / 32)
    ACTF = ACT.Silu if gated else ACT.Gelu
    SLOTS = 4
    AFTER = 1
    BEHIND = 3 if shared else 4
    with ExitStack() as ctx:
        def sb(name, shape, dt=F32):
            return ctx.enter_context(nc.sbuf_tensor(f"{tag}_{name}", shape, dt))

        sem = Semaphores(nc, ctx, tag)
        norm = Norm(chip, ctx, tag + "n", sem)
        router = sb("router", [P, E])
        up = sb("up", [P, 2, UP, P])
        down = sb("down", [P, 2, HB, P])
        ups = sb("ups", [P, 2, 2, UP, P], F32R)
        downs = sb("downs", [P, 2, 2, HB, P], F32R)
        xs2 = sb("xs2", [P, 2, N], F32R)
        hiddens = sb("hiddens", [P, SLOTS, 2, CHUNK], F32R)
        gate = sb("gate", [P, 2, N])
        act_out = sb("act_out", [P, SLOTS, CHUNK])
        weighed = sb("weighed", [P, SLOTS, CHUNK]) if gated else None
        hidden = sb("hidden", [P, SLOTS, CHUNK])
        sharedw = sb("sharedw", [P, 3, P]) if shared else None
        shareds = sb("shareds", [P, 2, 3, P], F32R) if shared else None
        logits, tmp, sel, W = (sb(n, [P, TILES, E]) for n in ("logits", "tmp", "sel", "W"))
        ranked, left = sb("ranked", [P, TILES, E + 4]), sb("left", [P, TILES, E + 4])
        work = ranked[:, :, 0:E]
        eight = sb("eight", [P, TILES, 8])
        best = sb("best", [P, TILES])
        warm = sb("warm", [P, 1])
        spare = sb("spare", [P, 4])
        flag = sb("flag", [P, TILES])
        gT_all = sb("gT", [P if kind == "top" else E, N])
        gT = gT_all[0:E, :]
        outT = sb("outT", [P, N])
        g_dram = nc.dram_tensor(f"{tag}_gates", (E, N), F32, kind="Internal").ap()
        xr = c.xn
        if shared:
            gtmp, gsel = (sb(n, [P, TILES, GROUPS]) for n in ("gtmp", "gsel"))
            granked = sb("granked", [P, TILES, GROUPS + 4])
            selb = sb("selb", [P, TILES, E], BF16)
            upper = sb("upper", [P, P], BF16)
            onesb = sb("onesb", [P, P], BF16)
        if kind == "nearest":
            xr = sb("xr", [P, TILES, D])
            scale = sb("scale", [P, D])
            csq, cm2 = sb("csq", [P, E]), sb("cm2", [P, E])
            nx = sb("nx", [P, TILES])
            ebias = sb("ebias", [E, 1])
        if kind == "top":
            csq, cm2 = sb("csq", [P, E]), sb("cm2", [P, E])
            rw = sb("rw", [P, E])
            rb = sb("rb", [E, 1])
            b1 = sb("b1", [P, 2, HB])
            b2 = sb("b2", [P, D])
            nx = sb("nx", [P, TILES])
            ebias = sb("ebias", [E, 1])

        small_in = sem("small_in")
        w_in = [sem("w_in0"), sem("w_in1")]
        g_in = [sem("g_in0"), sem("g_in1")]
        g_first = [sem(f"g_first{g}") for g in range(CHUNKS)]
        scaled, csum_ready, csum_taken = sem("scaled"), sem("csum_ready"), sem("csum_taken")
        padded = sem("padded")
        scored, scores_copied = sem("scored"), sem("scores_copied")
        router_made, logits_ready, shifted, exped = (sem(n) for n in ("router_made", "logits_ready", "shifted", "exped"))
        sel_ready, counted, gates_ready, gates_turned, gates_copied, gates_out = (
            sem(n) for n in ("sel_ready", "counted", "gates_ready", "gates_turned", "gates_copied", "gates_out"))
        up_ready, act_done, weighed_done, hidden_done, down_done = (
            sem(n) for n in ("up_ready", "act_done", "weighed_done", "hidden_done", "down_done"))
        x_high, x_low, h_high = (sem(n) for n in ("x_high", "x_low", "h_high"))
        h_low, h_low_pool = sem("h_low"), sem("h_low_pool")
        up_split, down_split, shared_split = (sem(n) for n in ("up_split", "down_split", "shared_split"))
        acc_ready, acc_copied, out_turned = sem("acc_ready"), sem("acc_copied"), sem("out_turned")
        sp_passed = sem("sp_passed")
        dve_own, pool_own, act_own = sem("dve_own"), sem("pool_own"), sem("act_own")

        OFF = CHUNKS if shared else 0
        ACC = (0, 1, 2, 3)
        A_BANKS = (4, 5) if gated else (4, 5, 6, 7)
        NA = len(A_BANKS)
        LOGITS = 4
        n_small = {"capacity": 4, "nearest": 2, "top": 4}[kind]
        n_w = {"capacity": 3, "nearest": 2, "top": 3}[kind]

        def wait_gates(eng, j, u, k):
            if isinstance(j, int) and j == u == 0:
                if k < CHUNKS:
                    eng.wait_ge(g_first[k], 16)
            elif k == 0:
                eng.wait_ge(g_in[u], 16 * (j + u))

        def pools(k):
            return not gated and k % 4 < 3

        def low_done(e, k):
            e, k = (e - 1, k + UNITS) if k < 0 else (e, k)
            if gated:
                return h_low, OFF + UNITS * e + k + 1
            if pools(k):
                return h_low_pool, UNITS * 3 // 4 * e + k - k // 4 + 1
            return h_low, UNITS // 4 * e + k // 4 + 1

        def take_low(eng, n, k, done):
            eng.wait_ge(h_high, n + 1)
            eng.tensor_tensor(hiddens[:, k % SLOTS, 1, :], hidden[:, k % SLOTS, :],
                              hiddens[:, k % SLOTS, 0, :].bitcast(F32), ALU.subtract).then_inc(done, 1)

        block = sem.open_block()

        @block.sync
        def _(sp):
            sp.dma_start(router[:, :], dram[f"{tag}_router"]).then_inc(small_in, 16)
            if shared:
                for n, name in enumerate(("sw1", "sw3", "sw2")):
                    sp.dma_start(sharedw[:, n, :], dram[f"{tag}_{name}"]).then_inc(small_in, 16)
            if kind == "nearest":
                sp.dma_start(scale[:, :], dram[f"{tag}_scale"].rearrange("(a n) -> a n", a=1)
                             .to_broadcast([P, D])).then_inc(small_in, 16)
            if kind == "top":
                sp.dma_start(rw[:, :], dram[f"{tag}_rw"]).then_inc(small_in, 16)
                sp.dma_start(rb[:, :], dram[f"{tag}_rb"].rearrange("(n a) -> n a", a=1)).then_inc(small_in, 16)
                sp.wait_ge(padded, 2)
                sp.dma_start(b2[0:E, :], dram[f"{tag}_b2"]).then_inc(small_in, 16)

            def load(j, u):
                e = 2 * j + u
                at_least(sp, down_split, 2 * (e - 1))
                if kind == "top":
                    apart(sp, e, sp_passed)
                    at_least(sp, act_done, UNITS * (e - 1))
                apart(sp, e, sp_passed)
                one = bass.ds(e, 1)
                if kind == "capacity":
                    for n, name in enumerate(("w1", "w3")):
                        sp.dma_start(up[:, u, n, :], dram[f"{tag}_{name}"][one, :, :].rearrange("e d h -> d (e h)"))\
                          .then_inc(w_in[u], 16)
                    sp.dma_start(down[:, u, 0, :], dram[f"{tag}_w2"][one, :, :].rearrange("e h d -> h (e d)"))\
                      .then_inc(w_in[u], 16)
                else:
                    sp.dma_start(up[:, u, :, :], dram[f"{tag}_up"][one, :, :].rearrange("e d (b h) -> d (e b) h", b=UP))\
                      .then_inc(w_in[u], 16)
                    sp.dma_start(down[:, u, :, :], dram[f"{tag}_down"][one, :, :].rearrange("e (b h) d -> h (e b) d", b=HB))\
                      .then_inc(w_in[u], 16)
                if kind == "top":
                    sp.dma_start(b1[:, u, :], dram[f"{tag}_b1"][one, :, :].rearrange("e p b -> p (e b)"))\
                      .then_inc(w_in[u], 16)

            def load_gate(j, u):
                e = 2 * j + u
                at_least(sp, weighed_done if gated else hidden_done, OFF + UNITS * (e - 1))
                apart(sp, e, sp_passed)
                if isinstance(e, int) and e == 0:
                    for g in range(CHUNKS):
                        cs = slice(g * CHUNK, (g + 1) * CHUNK)
                        sp.dma_start(gate[:, 0, cs], g_dram[0:1, cs].to_broadcast([P, CHUNK])).then_inc(g_first[g], 16)
                    return
                sp.dma_start(gate[:, u, :], g_dram[bass.ds(e, 1), :].to_broadcast([P, N])).then_inc(g_in[u], 16)

            load(0, 0)
            load(0, 1)
            sp.wait_ge(gates_copied, CHUNKS)
            sp.dma_start(g_dram, gT[:, :]).then_inc(gates_out, 16)
            sp.wait_ge(gates_out, 16)
            load_gate(0, 0)
            load_gate(0, 1)
            with sp.Fori(1, E // 2) as j:
                for u in range(2):
                    load(j, u)
                    load_gate(j, u)

        @block.tensor
        def _(pe):
            def logits_of(g):
                pe.wait_ge(norm.copied, g + 1)
                if g == 0:
                    pe.wait_ge(small_in, 16 * n_small)
                    if kind != "capacity":
                        pe.wait_ge(router_made, 2)
                        pe.matmul(c.psum[7][0:E, 0:1], csq[:, :], c.ones[:, 0:1], start=True, stop=True).then_inc(csum_ready, 1)
                terms = (router,) if kind == "capacity" else (cm2,) if kind == "nearest" else (cm2, rw)
                for n, term in enumerate(terms):
                    i = pe.matmul(c.psum[g][0:E, :], term[:, :], c.xnT[:, g * CHUNK:(g + 1) * CHUNK], start=(n == 0),
                                  stop=(n == len(terms) - 1))
                i.then_inc(scored, 1)

            for g in range(CHUNKS):
                norm.tensor(pe, xr, g, g, scaled if kind == "nearest" else norm.normed)
                if g:
                    logits_of(g - 1)
            logits_of(CHUNKS - 1)
            for t in range(TILES):
                if t % 4 == 0:
                    pe.wait_ge(scores_copied, t // 4 + 1)
                i = pe.transpose(c.psum[LOGITS][:, t * E:(t + 1) * E], gT[:, t * P:(t + 1) * P], c.ident[0:E, 0:E])
            i.then_inc(logits_ready, 1)
            if shared:
                pe.wait_ge(sel_ready, 1)
                pe.wait_ge(pool_own, 3)
                bank = c.psum[LOGITS + 1]
                pe.matmul(bank[:, :], upper[:, :], selb[:, :, :], start=True, stop=False)
                for t in range(TILES - 1):
                    rest = TILES - 1 - t
                    pe.matmul(bank[:, (t + 1) * E:], onesb[:, :],
                              selb[:, t:t + 1, :].to_broadcast([P, rest, E]), start=False, stop=False)
                i = pe.matmul(bank[:, :], c.zrow[:, 0:P], c.zrow[:, :], start=False, stop=True)
                i.then_inc(counted, 1)
            pe.wait_ge(gates_ready, 1)
            for g in range(CHUNKS):
                for t in range(4):
                    i = pe.transpose(c.psum[g][0:E, t * P:(t + 1) * P], W[:, 4 * g + t, :], c.ident[:, :])
                i.then_inc(gates_turned, 1)
            pe.wait_ge(gates_copied, CHUNKS)
            for g in range(CHUNKS):
                if kind == "top":
                    pe.matmul(c.psum[ACC[g]][:, :], b2[:, :], gT_all[:, g * CHUNK:(g + 1) * CHUNK], start=True, stop=False)
                else:
                    pe.matmul(c.psum[ACC[g]][:, :], c.zrow[:, 0:P], c.zrow[:, :], start=True, stop=False)

            def product(out, w, x, **flags):
                pe.matmul(out, w(0), x(0), start=flags["start"], stop=False)
                pe.matmul(out, w(0), x(1), start=False, stop=False)
                return pe.matmul(out, w(1), x(0), start=False, stop=flags["stop"])

            def project_up(n, k, ws):
                cs = slice(k % CHUNKS * CHUNK, (k % CHUNKS + 1) * CHUNK)
                at_least(pe, act_done, n - NA + 1)
                i = product(c.psum[A_BANKS[k % NA]][:, :], ws[0], lambda part: xs2[:, part, cs], start=True, stop=True)
                if gated:
                    at_least(pe, hidden_done, n - 1)
                    i = product(c.psum[6 + k % 2][:, :], ws[1], lambda part: xs2[:, part, cs], start=True, stop=True)
                i.then_inc(up_ready, 1)

            def project_down(done, k, w):
                pe.wait_ge(*done)
                product(c.psum[ACC[k % CHUNKS]][:, :], w, lambda part: hiddens[:, k % SLOTS, part, :], start=False,
                        stop=False).then_inc(down_done, 1)

            def up_weights(u, k):
                i = k // CHUNKS

                def block(n):
                    return lambda part: ups[:, u, part, n, :]
                if kind == "capacity":
                    return block(0), block(1)
                if kind == "nearest":
                    return block(2 + i), block(i)
                return (block(i),)

            def down_weights(u, k):
                return lambda part: downs[:, u, part, k // CHUNKS, :]

            def shared_weights(n):
                return lambda part: shareds[:, part, n, :]

            def expert(j, u, first=False):
                e = 2 * j + u
                n0 = OFF + UNITS * e
                pe.wait_ge(up_split, 2 * (e + 1))
                for k in range(UNITS):
                    project_up(n0 + k, k, up_weights(u, k))
                    if k >= BEHIND:
                        if k == BEHIND:
                            pe.wait_ge(down_split, 2 * (e + 1))
                        project_down(low_done(e, k - BEHIND), k - BEHIND, down_weights(u, k - BEHIND))
                    elif not first:
                        project_down(low_done(e, k - BEHIND), UNITS + k - BEHIND, down_weights(1 - u, UNITS + k - BEHIND))
                    elif shared:
                        project_down((h_low, CHUNKS + k - BEHIND + 1), CHUNKS + k - BEHIND, shared_weights(2))

            pe.wait_ge(x_low, CHUNKS)
            if shared:
                pe.wait_ge(shared_split, 2)
                for k in range(CHUNKS):
                    project_up(k, k, (shared_weights(0), shared_weights(1)))
                    if k >= BEHIND:
                        project_down((h_low, k - BEHIND + 1), k - BEHIND, shared_weights(2))
            expert(0, 0, True)
            expert(0, 1)
            with pe.Fori(1, E // 2) as j:
                expert(j, 0)
                expert(j, 1)
            for k in range(UNITS - BEHIND, UNITS):
                project_down(low_done(E - 1, k), k, down_weights(1, k))
            for g in range(CHUNKS):
                pe.matmul(c.psum[ACC[g]][:, :], c.zrow[:, 0:P], c.zrow[:, :], start=False,
                          stop=True).then_inc(acc_ready, 1)
            for g in range(CHUNKS):
                pe.wait_ge(acc_copied, g + 1)
                for t in range(4):
                    i = pe.transpose(c.psum[4 + g][:, t * P:(t + 1) * P],
                                     outT[:, (4 * g + t) * P:(4 * g + t + 1) * P], c.ident[:, :])
                i.then_inc(out_turned, 1)

        @block.scalar
        def _(act):
            chain = Chain(act, act_own)
            if kind != "capacity":
                act.wait_ge(small_in, 16 * n_small)
                sign = 1.0 if kind == "nearest" else -1.0
                act.mul(cm2[:, :], router[:, :], -2.0 * sign).then_inc(router_made, 1)
                chain(act.activation(csq[:, :], router[:, :], ACT.Square))
                act.mul(csq[:, :], csq[:, :], sign).then_inc(router_made, 1)
            norm.take_root(act, 0, LN_EPS)
            for g in range(CHUNKS):
                if kind == "nearest":
                    norm.take_square_root(act, chain, g, c.xn, act_out[:, :, :].rearrange("p s (t d) -> p (s t) d", d=D),
                                          RMS_EPS)
                if g + 1 < CHUNKS:
                    norm.take_root(act, g + 1, LN_EPS)
                norm.scalar(act, g, g)
                act.wait_ge(norm.copied, g + 1)
                act.activation(xs2[:, 0, g * CHUNK:(g + 1) * CHUNK], c.xnT[:, g * CHUNK:(g + 1) * CHUNK],
                               ACT.Copy).then_inc(x_high, 1)
            if kind != "capacity":
                act.wait_ge(csum_ready, 1)
                if kind == "top":
                    act.activation(ebias[:, :], c.psum[7][0:E, 0:1], ACT.Identity, bias=rb[:, :]).then_inc(csum_taken, 1)
                else:
                    act.activation(ebias[:, :], c.psum[7][0:E, 0:1], ACT.Copy).then_inc(csum_taken, 1)
                act.wait_ge(csum_taken, 1)
            if kind == "top":
                act.wait_ge(padded, 2)
            for g in range(CHUNKS):
                act.wait_ge(scored, g + 1)
                dst, src = gT[:, g * CHUNK:(g + 1) * CHUNK], c.psum[g][0:E, :]
                if kind == "capacity":
                    i = act.activation(dst, src, ACT.Copy)
                else:
                    i = act.activation(dst, src, ACT.Identity, bias=ebias[:, :])
                i.then_inc(scores_copied, 1)
            if kind != "nearest":
                act.wait_ge(shifted, 1)
                act.activation(work, work, ACT.Exp).then_inc(exped, 1)
            act.activation(warm[:, :], c.ones[:, 0:1], ACTF)
            for g in range(CHUNKS):
                act.wait_ge(gates_turned, g + 1)
                act.activation(gT[:, g * CHUNK:(g + 1) * CHUNK], c.psum[g][0:E, :], ACT.Copy).then_inc(gates_copied, 1)

            def take_high(n, k):
                act.wait_ge(hidden_done, n + 1)
                at_least(act, down_done, n - SLOTS + 1)
                act.activation(hiddens[:, k % SLOTS, 0, :], hidden[:, k % SLOTS, :], ACT.Copy).then_inc(h_high, 1)

            def unit(n, k, bias=0.0):
                act.wait_ge(up_ready, n + 1)
                at_least(act, weighed_done if gated else hidden_done, n - SLOTS + 1)
                act.activation(act_out[:, k % SLOTS, :], c.psum[A_BANKS[k % NA]][:, :], ACTF,
                               bias=bias).then_inc(act_done, 1)

            for k in range(OFF):
                unit(k, k)
                if k >= AFTER:
                    take_high(k - AFTER, k - AFTER)

            def expert(j, u, first=False):
                n0 = OFF + UNITS * (2 * j + u)
                if kind == "top":
                    act.wait_ge(w_in[u], 16 * n_w * (j + 1))
                for k in range(UNITS):
                    bias = 0.0
                    if kind == "top":
                        bias = b1[:, u, k // CHUNKS:k // CHUNKS + 1]
                    unit(n0 + k, k, bias)
                    if not first or shared or k >= AFTER:
                        take_high(n0 + k - AFTER, (k - AFTER) % SLOTS)

            expert(0, 0, True)
            expert(0, 1)
            with act.Fori(1, E // 2) as j:
                expert(j, 0)
                expert(j, 1)
            for k in range(UNITS - AFTER, UNITS):
                take_high(OFF + UNITS * (E - 1) + k, k)
            for g in range(0, CHUNKS):
                act.wait_ge(acc_ready, g + 1)
                act.activation(outT[:, g * CHUNK:(g + 1) * CHUNK], c.psum[ACC[g]][:, :], ACT.Copy).then_inc(acc_copied, 1)

        @block.vector
        def _(dve):
            chain = Chain(dve, dve_own)
            if kind == "nearest":
                dve.wait_ge(small_in, 16 * n_small)
                norm.take_stats(dve, 0, c.x)
                for g in range(CHUNKS):
                    norm.normalise(dve, g, c.x, c.xn)
                    if g + 1 < CHUNKS:
                        norm.take_stats(dve, g + 1, c.x)
                    norm.take_inverse(dve, g)
                    for t in range(4 * g, 4 * g + 4):
                        i = dve.scalar_tensor_tensor(xr[:, t, :], c.xn[:, t, :], norm.rstd[:, t:t + 1], scale[:, :],
                                                     ALU.mult, ALU.mult)
                    i.then_inc(scaled, 1)
            else:
                norm.vector(dve, c.x, c.xn)

            def split_weights(j, u, src, dst, done):
                dve.wait_ge(w_in[u], 16 * n_w * (j + 1))
                dve.tensor_copy(dst[:, u, 0, :, :], src[:, u, :, :]).then_inc(done, 1)
                dve.wait_ge(done, 2 * (2 * j + u) + 1)
                dve.tensor_tensor(dst[:, u, 1, :, :], src[:, u, :, :], dst[:, u, 0, :, :].bitcast(F32),
                                  ALU.subtract).then_inc(done, 1)

            if shared:
                dve.wait_ge(small_in, 16 * n_small)
                dve.tensor_copy(shareds[:, 0, :, :], sharedw[:, :, :]).then_inc(shared_split, 1)
                dve.wait_ge(shared_split, 1)
                dve.tensor_tensor(shareds[:, 1, :, :], sharedw[:, :, :], shareds[:, 0, :, :].bitcast(F32),
                                  ALU.subtract).then_inc(shared_split, 1)

            every = [P, TILES, E]

            def all_of(a):
                return a.unsqueeze(2).to_broadcast(every)

            if K > 1:
                for n in range(4):
                    chain(dve.memset(spare[:, n:n + 1], (n + 2) * NEG))
                spares = spare[:, :].unsqueeze(1).to_broadcast([P, TILES, 4])
                chain(dve.tensor_copy(ranked[:, :, E:E + 4], spares))
                if shared:
                    chain(dve.tensor_copy(granked[:, :, GROUPS:GROUPS + 4], spares))
            lower = c.rev[:, 0:E].unsqueeze(1).to_broadcast(every)
            lg = c.psum[LOGITS][:, 0:TILES * E].rearrange("p (t e) -> p t e", t=TILES)
            if kind != "capacity":
                dve.wait_ge(scaled if kind == "nearest" else norm.normed, CHUNKS)
                squares = act_out[:, :, :].rearrange("p s (t d) -> p (s t) d", d=D)
                chain(dve.tensor_tensor(squares, xr[:, :, :], xr[:, :, :], ALU.mult))
                chain(dve.tensor_reduce(nx[:, :], squares, AXX, ALU.add))
            dve.wait_ge(logits_ready, 1)
            if kind == "capacity":
                chain(dve.tensor_reduce(flag[:, :], lg, AXX, ALU.max))
                dve.tensor_tensor(work, lg, all_of(flag[:, :]), ALU.subtract).then_inc(shifted, 1)
                dve.wait_ge(exped, 1)
                chain(dve.tensor_reduce(flag[:, :], work, AXX, ALU.add))
                chain(dve.reciprocal(flag[:, :], flag[:, :]))
                chain(dve.tensor_tensor(logits[:, :, :], work, all_of(flag[:, :]), ALU.mult))
                chain(dve.tensor_reduce(granked[:, :, 0:GROUPS], logits[:, :, :].rearrange("p t (g i) -> p t g i", g=GROUPS),
                                        AXX, ALU.max))
                best_four(dve, chain, granked, GROUPS, gsel[:, :, :], eight, left, spares)
                by_group = [P, TILES, GROUPS, E // GROUPS]
                keep = gsel[:, :, :].unsqueeze(3).to_broadcast(by_group)
                less = gtmp[:, :, :].unsqueeze(3).to_broadcast(by_group)
                cur = work.rearrange("p t (g i) -> p t g i", g=GROUPS)
                chain(dve.tensor_scalar(gtmp[:, :, :], gsel[:, :, :], -1.0, None, ALU.add))
                chain(dve.tensor_tensor(cur, logits[:, :, :].rearrange("p t (g i) -> p t g i", g=GROUPS), keep, ALU.mult))
                chain(dve.tensor_tensor(cur, cur, less, ALU.add))
                best_four(dve, chain, ranked, E, sel[:, :, :], eight, left, spares)
                dve.tensor_copy(selb[:, :, :], sel[:, :, :]).then_inc(sel_ready, 1)
                chain(dve.tensor_tensor(W[:, :, :], logits[:, :, :], sel[:, :, :], ALU.mult))
                chain(dve.tensor_reduce(flag[:, :], W[:, :, :], AXX, ALU.add))
                chain(dve.tensor_scalar(flag[:, :], flag[:, :], 1e-9, None, ALU.add))
                chain(dve.reciprocal(flag[:, :], flag[:, :]))
                chain(dve.tensor_tensor(W[:, :, :], W[:, :, :], all_of(flag[:, :]), ALU.mult))
                dve.wait_ge(counted, 1)
                chain(dve.tensor_scalar(tmp[:, :, :], c.psum[LOGITS + 1][:, :].rearrange("p (t e) -> p t e", t=TILES),
                                        float(CAP), None, ALU.is_lt))
                dve.tensor_tensor(W[:, :, :], W[:, :, :], tmp[:, :, :], ALU.mult).then_inc(gates_ready, 1)
            elif kind == "nearest":
                chain(dve.tensor_tensor(work, lg, all_of(nx[:, :]), ALU.add))
                chain(dve.tensor_scalar(work, work, -1.0, None, ALU.mult))
                first_best(dve, chain, work, E, W[:, :, :], tmp[:, :, :], flag[:, :], best[:, :], lower)
                dve.tensor_copy(W[:, :, :], W[:, :, :]).then_inc(gates_ready, 1)
            else:
                chain(dve.tensor_tensor(logits[:, :, :], lg, all_of(nx[:, :]), ALU.subtract))
                chain(dve.tensor_copy(work, logits[:, :, :]))
                best_four(dve, chain, ranked, E, sel[:, :, :], eight, left, spares)
                dve.tensor_tensor(work, logits[:, :, :], all_of(eight[:, :, 0]), ALU.subtract)\
                   .then_inc(shifted, 1)
                dve.wait_ge(exped, 1)
                chain(dve.tensor_tensor(W[:, :, :], work, sel[:, :, :], ALU.mult))
                chain(dve.tensor_reduce(flag[:, :], W[:, :, :], AXX, ALU.add))
                chain(dve.reciprocal(flag[:, :], flag[:, :]))
                dve.tensor_tensor(W[:, :, :], W[:, :, :], all_of(flag[:, :]), ALU.mult).then_inc(gates_ready, 1)
            if kind == "nearest":
                chain(dve.tensor_tensor(c.x[:, :, :], c.x[:, :, :], c.xn[:, :, :], ALU.add))

            split_weights(0, 0, up, ups, up_split)
            split_weights(0, 0, down, downs, down_split)

            def unit(n, k, u, low_before):
                dve.wait_ge(weighed_done if gated else act_done, n + 1)
                if low_before:
                    at_least(dve, *low_before)
                cs = slice(k % CHUNKS * CHUNK, (k % CHUNKS + 1) * CHUNK)
                if gated:
                    i = dve.tensor_tensor(hidden[:, k % SLOTS, :], weighed[:, k % SLOTS, :], c.psum[6 + k % 2][:, :], ALU.mult)
                else:
                    i = dve.tensor_tensor(hidden[:, k % SLOTS, :], act_out[:, k % SLOTS, :], gate[:, u, cs], ALU.mult)
                i.then_inc(hidden_done, 1)

            def low(n, k):
                if not pools(k):
                    take_low(dve, n, k, h_low)

            for k in range(OFF):
                unit(k, k, 0, None)
                if k >= AFTER:
                    low(k - AFTER, k - AFTER)

            def expert(j, u, first=False, last=False):
                e = 2 * j + u
                n0 = OFF + UNITS * e
                for k in range(UNITS):
                    if not gated:
                        wait_gates(dve, j, u, k)
                    before = low_done(e, k - SLOTS) if k >= SLOTS or not first else (h_low, k + 1) if shared else None
                    unit(n0 + k, k, u, before)
                    if not first or shared or k >= AFTER:
                        low(n0 + k - AFTER, (k - AFTER) % SLOTS)
                    if k == 1 and not last:
                        split_weights(j + u, 1 - u, up, ups, up_split)
                    if k == (3 if shared else 5) and not last:
                        at_least(dve, down_done, OFF + UNITS * e)
                        split_weights(j + u, 1 - u, down, downs, down_split)

            expert(0, 0, True)
            expert(0, 1)
            with dve.Fori(1, E // 2 - 1) as j:
                expert(j, 0)
                expert(j, 1)
            expert(E // 2 - 1, 0)
            expert(E // 2 - 1, 1, last=True)
            for k in range(UNITS - AFTER, UNITS):
                low(OFF + UNITS * (E - 1) + k, k)
            for g in range(CHUNKS):
                dve.wait_ge(out_turned, g + 1)
                xs = c.x[:, 4 * g:4 * g + 4, :]
                dve.tensor_tensor(xs, xs, c.psum[4 + g][:, :].rearrange("p (t d) -> p t d", t=4), ALU.add)

        @block.gpsimd
        def _(pool):
            chain = Chain(pool, pool_own)
            if kind == "top":
                pool.memset(b2[:, :], 0.0).then_inc(padded, 1)
                pool.memset(gT_all[:, :], 0.0).then_inc(padded, 1)
            if shared:
                chain(pool.memset(onesb[:, :], 1.0))
                chain(pool.memset(upper[:, :], 1.0))
                chain(pool.affine_select(out=upper[:, :], in_=upper[:, :], compare_op=ALU.is_gt, fill=0.0, base=0,
                                         pattern=[[1, P]], channel_multiplier=-1))
            for g in range(CHUNKS):
                cs = slice(g * CHUNK, (g + 1) * CHUNK)
                pool.wait_ge(x_high, g + 1)
                pool.tensor_tensor(xs2[:, 1, cs], c.xnT[:, cs], xs2[:, 0, cs].bitcast(F32), ALU.subtract).then_inc(x_low, 1)
            if not gated:
                def expert(j, u):
                    for k in range(UNITS):
                        if pools(k):
                            take_low(pool, UNITS * (2 * j + u) + k, k, h_low_pool)

                expert(0, 0)
                expert(0, 1)
                with pool.Fori(1, E // 2) as j:
                    expert(j, 0)
                    expert(j, 1)
            if gated:
                def unit(n, k, gates):
                    pool.wait_ge(act_done, n + 1)
                    at_least(pool, hidden_done, n - SLOTS + 1)
                    if gates is None:
                        i = pool.tensor_scalar(weighed[:, k % SLOTS, :], act_out[:, k % SLOTS, :], 1.0, 1.0,
                                               ALU.mult, ALU.mult)
                    else:
                        i = pool.tensor_tensor(weighed[:, k % SLOTS, :], act_out[:, k % SLOTS, :], gates, ALU.mult)
                    i.then_inc(weighed_done, 1)

                for k in range(OFF):
                    unit(k, k, None)

                def expert(j, u):
                    for k in range(UNITS):
                        wait_gates(pool, j, u, k)
                        cs = slice(k % CHUNKS * CHUNK, (k % CHUNKS + 1) * CHUNK)
                        unit(OFF + UNITS * (2 * j + u) + k, k, gate[:, u, cs])

                expert(0, 0)
                expert(0, 1)
                with pool.Fori(1, E // 2) as j:
                    expert(j, 0)
                    expert(j, 1)


def ternary(chip, tag):
    nc, c, dram = chip.nc, chip, chip.dram
    EPS, QB = 1e-5, 128.0
    ROUND = 1.5 * 2.0 ** 23
    with ExitStack() as ctx:
        def sb(name, shape, dt=F32):
            return ctx.enter_context(nc.sbuf_tensor(f"{tag}_{name}", shape, dt))

        sem = Semaphores(nc, ctx, tag)
        norm = Norm(chip, ctx, tag + "n", sem)
        w, wq, wabs = sb("w", [P, D]), sb("wq", [P, D]), sb("wabs", [P, 1])
        gamma, beta = sb("gamma", [P, D]), sb("beta", [P, D])
        st, peaks = sb("st", [P, 8]), sb("peaks", [P, CHUNKS])
        loaded, made, summed, peak, peak_all, clipped, out_ready = (
            sem(n) for n in ("loaded", "made", "summed", "peak", "peak_all", "clipped", "out_ready"))
        dve_own, twice_normed, scaled = sem("dve_own"), sem("twice_normed"), sem("scaled")
        block = sem.open_block()

        @block.sync
        def _(sp):
            sp.dma_start(w[:, :], dram[f"{tag}_w"]).then_inc(loaded, 16)
            for name, tile in (("gamma", gamma), ("beta", beta)):
                sp.dma_start(tile[:, :], dram[f"{tag}_{name}"].rearrange("(a n) -> a n", a=1)
                             .to_broadcast([P, D])).then_inc(loaded, 16)

        @block.gpsimd
        def _(pool):
            pool.wait_ge(loaded, 48)
            for g in range(CHUNKS):
                pool.wait_ge(twice_normed, g + 1)
                xn = c.xn[:, 4 * g:4 * g + 4, :]
                for n, (tile, op) in enumerate(((gamma, ALU.mult), (beta, ALU.add))):
                    pool.tensor_tensor(xn, xn, tile[:, :].unsqueeze(1).to_broadcast([P, 4, D]), op).then_inc(scaled, 1)
                    pool.wait_ge(scaled, 2 * g + n + 1)
            pool.wait_ge(peak, 1)
            pool.partition_all_reduce(st[:, 4:5], st[:, 3:4], P, RMAX).then_inc(peak_all, 1)

        @block.scalar
        def _(act):
            for g in range(CHUNKS):
                norm.take_root(act, g, LN_EPS)
                norm.take_root(act, g, LN2_EPS)
            for g in range(CHUNKS):
                norm.scalar(act, g, g)

        @block.tensor
        def _(pe):
            pe.wait_ge(made, 1)
            pe.matmul(c.psum[4][:, 0:1], c.ones[:, :], wabs[:, :], start=True, stop=True).then_inc(summed, 1)
            for g in range(CHUNKS):
                norm.tensor(pe, c.xn, g, g, clipped)
            for g in range(CHUNKS):
                pe.wait_ge(norm.copied, g + 1)
                for t in range(4):
                    n = 4 * g + t
                    i = pe.matmul(c.psum[4 + g][:, t * P:(t + 1) * P], c.xnT[:, n * P:(n + 1) * P], wq[:, :],
                                  start=True, stop=True)
                i.then_inc(out_ready, 1)

        @block.vector
        def _(dve):
            chain = Chain(dve, dve_own)
            dve.wait_ge(loaded, 48)
            dve.tensor_reduce(wabs[:, :], w[:, :], AXX, ALU.add, apply_absolute_value=True).then_inc(made, 1)
            norm.take_stats(dve, 0, c.x)
            for g in range(CHUNKS):
                norm.normalise(dve, g, c.x, c.xn)
                dve.wait_ge(norm.normed, g + 1)
                norm.take_stats(dve, g, c.xn)
                if g + 1 < CHUNKS:
                    norm.take_stats(dve, g + 1, c.x)
                norm.take_inverse(dve, g)
                for t in range(4 * g, 4 * g + 4):
                    i = dve.tensor_scalar(c.xn[:, t, :], c.xn[:, t, :], norm.st[:, t, 0:1], norm.rstd[:, t:t + 1],
                                          ALU.subtract, ALU.mult)
                i.then_inc(twice_normed, 1)
            for g in range(CHUNKS):
                dve.wait_ge(scaled, 2 * (g + 1))
                i = dve.tensor_reduce(peaks[:, g:g + 1], c.xn[:, 4 * g:4 * g + 4, :].rearrange("p t d -> p (t d)"),
                                      AXX, ALU.max, apply_absolute_value=True)
            chain(i)
            dve.tensor_reduce(st[:, 3:4], peaks[:, :], AXX, ALU.max).then_inc(peak, 1)
            dve.wait_ge(summed, 1)
            chain(dve.tensor_scalar(st[:, 0:1], c.psum[4][:, 0:1], 1.0 / (D * D), None, ALU.mult))
            chain(dve.tensor_scalar(st[:, 1:2], st[:, 0:1], EPS, None, ALU.add))
            chain(dve.reciprocal(st[:, 1:2], st[:, 1:2]))
            chain(dve.tensor_scalar(wq[:, :], w[:, :], st[:, 1:2], None, ALU.mult))
            chain(dve.tensor_scalar(wq[:, :], wq[:, :], 2.0, -2.0, ALU.min, ALU.max))
            chain(dve.tensor_scalar(wq[:, :], wq[:, :], ROUND, None, ALU.add))
            chain(dve.tensor_scalar(wq[:, :], wq[:, :], -ROUND, None, ALU.add))
            chain(dve.tensor_scalar(wq[:, :], wq[:, :], 1.0, -1.0, ALU.min, ALU.max))
            dve.wait_ge(peak_all, 1)
            chain(dve.reciprocal(st[:, 5:6], st[:, 4:5]))
            chain(dve.tensor_tensor(st[:, 6:7], st[:, 4:5], st[:, 0:1], ALU.mult))
            chain(dve.tensor_scalar(st[:, 6:7], st[:, 6:7], 1.0 / QB, None, ALU.mult))
            for g in range(CHUNKS):
                xn = c.xn[:, 4 * g:4 * g + 4, :]
                chain(dve.tensor_scalar(xn, xn, QB, st[:, 5:6], ALU.mult, ALU.mult))
                dve.tensor_scalar(xn, xn, QB - EPS, EPS - QB, ALU.min, ALU.max).then_inc(clipped, 1)
            for g in range(CHUNKS):
                dve.wait_ge(out_ready, g + 1)
                xs = c.x[:, 4 * g:4 * g + 4, :]
                dve.scalar_tensor_tensor(xs, c.psum[4 + g][:, :].rearrange("p (t d) -> p t d", t=4), st[:, 6:7],
                                         xs, ALU.mult, ALU.add)


def store_x(chip, out):
    nc, c = chip.nc, chip
    with ExitStack() as ctx:
        sem = Semaphores(nc, ctx, "end")
        stored = sem("stored")
        block = sem.open_block()

        @block.sync
        def _(sp):
            sp.dma_start(out.rearrange("(t p) d -> p t d", p=P), c.x[:, :, :]).then_inc(stored, 16)
            sp.wait_ge(stored, 16)


def build(nc, dram, out, upto=8, first=0):
    with ExitStack() as ctx:
        chip = Chip(nc, ctx, dram)
        start_up(chip)
        sublayers = [
            lambda: attention(chip, "a0"),
            lambda: experts(chip, "f0", "capacity"),
            lambda: attention(chip, "a1", biased=True, full_mask="mask"),
            lambda: experts(chip, "f1", "nearest"),
            lambda: attention(chip, "a2", rope=True, causal=True, key_mask="keep2"),
            lambda: ternary(chip, "f2"),
            lambda: attention(chip, "a3", key_mask="keep3", out_bias=False),
            lambda: experts(chip, "f3", "top"),
        ]
        for sublayer in sublayers[first:upto]:
            sublayer()
        store_x(chip, out)


def rotary():
    theta = (1.0 / np.float32(10000.0) ** (np.arange(0, HD, 2, dtype=np.float32) / np.float32(HD))).astype(np.float32)
    angle = np.arange(S, dtype=np.float32)[None, :] * np.repeat(theta, 2)[:, None]
    sign = np.where(np.arange(HD) % 2 == 0, -1.0, 1.0).astype(np.float32)[:, None]
    cos, sin = np.cos(angle), np.sin(angle) * sign
    return np.tile(cos, (H, 1)).astype(np.float32), np.tile(sin, (H, 1)).astype(np.float32)


def arrange(v):
    swap = np.arange(D) ^ 1
    cos, sin = rotary()
    a = {"x": v["x"].reshape(N, D), "ctxT": v["ctx_1024"].reshape(N, D).T,
         "mask": v["mask_BxSxS2_if1"], "mask_T": v["mask_BxSxS2_if1"].transpose(0, 2, 1),
         "keep2": v["mask_BxS2_if1"], "keep3": v["mask_BxS2_ik0"]}
    for n in range(3):
        for w in "qkvo":
            a[f"a{n}_w{w}"] = v[f"L{n}_xattn_W{w}"].T
        a[f"a{n}_bo"] = v[f"L{n}_xattn_bo"]
    for w in "qkv":
        a[f"a1_b{w}"] = v[f"L1_xattn_b{w}"]
    a["a2_wsq"], a["a2_wsk"] = v["L2_xattn_Wq"][swap].T, v["L2_xattn_Wk"][swap].T
    a["a2_cos"], a["a2_sin"] = cos, sin
    a["a3_wq"], a["a3_wo"] = v["L3_xattn_Wq"].T, v["L3_xattn_Wo"].T
    a["a3_wk"], a["a3_wv"] = v["L3_xattn_Wkv"][:D].T, v["L3_xattn_Wkv"][D:].T
    a["f0_router"] = v["L0_ffn_wg"].T
    for w in ("w1", "w2", "w3", "sw1", "sw2", "sw3"):
        a[f"f0_{w}"] = v[f"L0_ffn_{w}"]
    a["f1_router"], a["f1_scale"] = v["L1_ffn_centroids"].T, v["L1_ffn_scale"]
    a["f1_up"], a["f1_down"] = v["L1_ffn_up_w"], v["L1_ffn_down_w"]
    a["f2_w"], a["f2_gamma"], a["f2_beta"] = v["L2_ffn_weight"], v["L2_ffn_ln_gamma"], v["L2_ffn_ln_beta"]
    a["f3_router"], a["f3_rw"], a["f3_rb"] = v["L3_ffn_keys"].T, v["L3_ffn_rw"].T, v["L3_ffn_rb"]
    a["f3_up"], a["f3_down"] = v["L3_ffn_w1"].transpose(0, 2, 1), v["L3_ffn_w2"].transpose(0, 2, 1)
    a["f3_b1"] = v["L3_ffn_b1"].reshape(16, 4, P).transpose(0, 2, 1)
    a["f3_b2"] = v["L3_ffn_b2"]
    return {k: np.ascontiguousarray(x) for k, x in a.items()}


UPTO = 8


def kernel(**inputs):
    import numpy as _np
    import concourse.bacc as _bacc
    from concourse import mybir as _mybir
    from concourse.bass_utils import run_bass_kernel_spmd as _run

    nc = _bacc.Bacc("TRN2", target_bir_lowering=False, num_devices=1)
    arrays, dram = {}, {}
    for name, a in arrange({k: _np.asarray(x) for k, x in inputs.items()}).items():
        arrays[f"in_{name}"] = a
        dram[name] = nc.dram_tensor(f"in_{name}", a.shape, _mybir.dt.from_np(a.dtype), kind="ExternalInput").ap()
    out = nc.dram_tensor("out_x", (N, D), _mybir.dt.float32, kind="ExternalOutput").ap()
    build(nc, dram, out, UPTO)
    r = _run(nc, [arrays], core_ids=[0])
    return r.results[0]["out_x"].reshape(B, S, D)
```
